# Optimizing a Trainium2 kernel written in Bass

```python
import numpy as np
import jax
import jax.numpy as jnp

def _softmax(x, axis=-1):
    return jax.nn.softmax(x, axis=axis)

def _gelu(x):
    return jax.nn.gelu(x, approximate=True)

def _silu(x):
    return jax.nn.silu(x)

def _sigmoid(x):
    return jax.nn.sigmoid(x)

def _layernorm(x, axis=-1, eps=1e-05):
    m = jnp.mean(x, axis=axis, keepdims=True)
    v = jnp.var(x, axis=axis, keepdims=True)
    return (x - m) / jnp.sqrt(v + eps)

def _scatter_add(tgt, idx, src, axis=0):
    return tgt.at[idx].add(src)

def _segment_sum(src, seg, n):
    return jax.ops.segment_sum(src, seg, n)
kernel_name = 'mk_gnn_resnorm_d4_gnn_r16_f18d6c'

def setup_inputs(seed: int=0):
    np.random.seed(seed)
    _w = jnp.asarray

    def _rec_inputs():
        import jax
        import jax.numpy as jnp
        _gk = jax.random.key(seed)
        x = -0.0003713 + 1 * jax.random.normal(jax.random.fold_in(_gk, 1), (6250, 128), jnp.float32)
        _s = jax.random.randint(jax.random.fold_in(_gk, 2), (50000,), 0, 6250, jnp.int32)
        _d = jax.random.randint(jax.random.fold_in(_gk, 3), (50000,), 0, 6250, jnp.int32)
        _loop = jnp.arange(6250, dtype=jnp.int32)
        src = jnp.concatenate([_s, _d, _loop])
        dst = jnp.concatenate([_d, _s, _loop])
        _o = jnp.argsort(dst, stable=True)
        src = src[_o]
        dst = dst[_o]
        edge_type_2 = jax.random.randint(jax.random.fold_in(_gk, 13), (106250,), 0, 2, jnp.int32)
        edge_type_64 = jax.random.randint(jax.random.fold_in(_gk, 14), (106250,), 0, 64, jnp.int32)
        edge_weight = jax.random.uniform(jax.random.fold_in(_gk, 15), (106250,), jnp.float32, 0.0, 1)
        return (x, src, dst, edge_type_2, edge_type_64, edge_weight)
    x, src, dst, edge_type_2, edge_type_64, edge_weight = _rec_inputs()

    def _L0_gnn_setup():
        import jax, jax.numpy as jnp
        import numpy as np
        N_NODES = 6250
        N_EDGES = 200000
        IN_DIM = 128
        OUT_DIM = 128
        key = jax.random.key(seed)
        k1, k2, k3, k4 = jax.random.split(key, 4)
        inp = jax.random.normal(k1, (N_NODES, IN_DIM), dtype=jnp.float32)
        edge_row = jax.random.randint(k2, (N_EDGES,), 0, N_NODES, dtype=jnp.int32)
        edge_col = jax.random.randint(k3, (N_EDGES,), 0, N_NODES, dtype=jnp.int32)
        edge_val = jax.random.uniform(k4, (N_EDGES,), dtype=jnp.float32)
        kernel = jnp.ones((IN_DIM, OUT_DIM), dtype=jnp.float32)
        bias = jnp.ones((OUT_DIM,), dtype=jnp.float32)
        return {'inp': inp, 'edge_row': edge_row, 'edge_col': edge_col, 'edge_val': edge_val, 'kernel': kernel, 'bias': bias}
    _L0_gnn_all = _L0_gnn_setup()
    _L0_gnn_in = {k: v for k, v in _L0_gnn_all.items() if k in ('kernel', 'bias')}
    del _L0_gnn_all

    def _L1_gnn_setup():
        import jax, jax.numpy as jnp
        import numpy as np
        N = 6250
        E = 100000
        D = 128
        R = 64
        B = 8
        key = jax.random.key(seed)
        k1, k2, k3, k4, k5, k6 = jax.random.split(key, 6)
        x = jax.random.normal(k1, (N, D), dtype=jnp.float32)
        bases = jax.random.normal(k2, (B, D, D), dtype=jnp.float32) * (2.0 / (D + D)) ** 0.5
        rw = jax.random.uniform(k3, (R, B), dtype=jnp.float32)
        relation_base_weights = rw / jnp.sum(rw, axis=1, keepdims=True)
        source = jax.random.randint(k4, (E,), 0, N)
        target = jax.random.randint(k5, (E,), 0, N)
        edge_type = jax.random.randint(k6, (E,), 0, R)
        return {'x': x, 'bases': bases, 'relation_base_weights': relation_base_weights, 'source': source, 'target': target, 'edge_type': edge_type}
    _L1_gnn_all = _L1_gnn_setup()
    _L1_gnn_in = {k: v for k, v in _L1_gnn_all.items() if k in ('bases', 'relation_base_weights')}
    del _L1_gnn_all

    def _L2_gnn_setup():
        import jax, jax.numpy as jnp
        import numpy as np
        IN_DIM = 128
        OUT_DIM = 128
        N_NODES = 625
        N_EDGES = 40000
        key = jax.random.key(seed)
        ks = jax.random.split(key, 9)
        X = jax.random.normal(ks[0], (N_NODES, IN_DIM), dtype=jnp.float32)
        edge_index = jax.random.randint(ks[1], (2, N_EDGES), 0, N_NODES, dtype=jnp.int64)
        edge_types = jax.random.randint(ks[2], (N_EDGES,), 0, 2, dtype=jnp.int64)
        s = 1.0 / np.sqrt(IN_DIM)
        W_data = jax.random.uniform(ks[3], (OUT_DIM, IN_DIM), minval=-s, maxval=s, dtype=jnp.float32)
        b_data = jax.random.uniform(ks[4], (OUT_DIM,), minval=-s, maxval=s, dtype=jnp.float32)
        W_control = jax.random.uniform(ks[5], (OUT_DIM, IN_DIM), minval=-s, maxval=s, dtype=jnp.float32)
        b_control = jax.random.uniform(ks[6], (OUT_DIM,), minval=-s, maxval=s, dtype=jnp.float32)
        W_self = jax.random.uniform(ks[7], (OUT_DIM, IN_DIM), minval=-s, maxval=s, dtype=jnp.float32)
        b_self = jax.random.uniform(ks[8], (OUT_DIM,), minval=-s, maxval=s, dtype=jnp.float32)
        return {'X': X, 'edge_index': edge_index, 'edge_types': edge_types, 'W_data': W_data, 'b_data': b_data, 'W_control': W_control, 'b_control': b_control, 'W_self': W_self, 'b_self': b_self}
    _L2_gnn_all = _L2_gnn_setup()
    _L2_gnn_in = {k: v for k, v in _L2_gnn_all.items() if k in ('W_data', 'b_data', 'W_control', 'b_control', 'W_self', 'b_self')}
    del _L2_gnn_all

    def _L3_gnn_setup():
        import jax, jax.numpy as jnp
        import numpy as np
        N_NODES = 6250
        N_EDGES = 50000
        D_IN = 128
        D_HID = 128

        def _gcn_conv(x, W, b, src, dst, norm, num_nodes):
            h = x @ W.T
            msg = h[src] * norm[:, None]
            out = jax.ops.segment_sum(msg, dst, num_segments=num_nodes)
            return out + b
        key = jax.random.key(seed)
        ks = jax.random.split(key, 5)
        x = jax.random.normal(ks[0], (N_NODES, D_IN), dtype=jnp.float32)
        edge_index = jax.random.randint(ks[1], (2, N_EDGES), 0, N_NODES, dtype=jnp.int64)
        W1 = jax.random.normal(ks[2], (D_HID, D_IN), dtype=jnp.float32) * 0.05
        b1 = jnp.zeros((D_HID,), dtype=jnp.float32)
        W2 = jax.random.normal(ks[3], (D_HID, D_HID), dtype=jnp.float32) * 0.05
        b2 = jnp.zeros((D_HID,), dtype=jnp.float32)
        return {'x': x, 'edge_index': edge_index, 'W1': W1, 'b1': b1, 'W2': W2, 'b2': b2}
    _L3_gnn_all = _L3_gnn_setup()
    _L3_gnn_in = {k: v for k, v in _L3_gnn_all.items() if k in ('W1', 'b1', 'W2', 'b2')}
    del _L3_gnn_all
    return {'x': x, 'src': src, 'dst': dst, 'edge_type_2': edge_type_2, 'edge_type_64': edge_type_64, 'edge_weight': edge_weight, 'L0_gnn_kernel': _L0_gnn_in['kernel'], 'L0_gnn_bias': _L0_gnn_in['bias'], 'L1_gnn_bases': _L1_gnn_in['bases'], 'L1_gnn_relation_base_weights': _L1_gnn_in['relation_base_weights'], 'L2_gnn_W_data': _L2_gnn_in['W_data'], 'L2_gnn_b_data': _L2_gnn_in['b_data'], 'L2_gnn_W_control': _L2_gnn_in['W_control'], 'L2_gnn_b_control': _L2_gnn_in['b_control'], 'L2_gnn_W_self': _L2_gnn_in['W_self'], 'L2_gnn_b_self': _L2_gnn_in['b_self'], 'L3_gnn_W1': _L3_gnn_in['W1'], 'L3_gnn_b1': _L3_gnn_in['b1'], 'L3_gnn_W2': _L3_gnn_in['W2'], 'L3_gnn_b2': _L3_gnn_in['b2']}

def reference(x, src, dst, edge_type_2, edge_type_64, edge_weight, L0_gnn_kernel, L0_gnn_bias, L1_gnn_bases, L1_gnn_relation_base_weights, L2_gnn_W_data, L2_gnn_b_data, L2_gnn_W_control, L2_gnn_b_control, L2_gnn_W_self, L2_gnn_b_self, L3_gnn_W1, L3_gnn_b1, L3_gnn_W2, L3_gnn_b2):
    import jax
    import jax.numpy as jnp

    def _L0_gnn_ref(inp, edge_row, edge_col, edge_val, kernel, bias):
        import jax, jax.numpy as jnp
        import numpy as np
        N_NODES = 6250
        N_EDGES = 200000
        IN_DIM = 128
        OUT_DIM = 128
        support = jnp.matmul(inp, kernel)
        messages = edge_val[:, None] * support[edge_col]
        output = jax.ops.segment_sum(messages, edge_row, num_segments=N_NODES)
        return output + bias

    def _L1_gnn_ref(x, bases, relation_base_weights, source, target, edge_type):
        import jax, jax.numpy as jnp
        import numpy as np
        N = 6250
        E = 100000
        D = 128
        R = 64
        B = 8
        xs = x[source]
        alpha = relation_base_weights[edge_type]
        num_bases = bases.shape[0]
        m = alpha[:, 0:1] * (xs @ bases[0])
        for b in range(1, num_bases):
            m = m + alpha[:, b:b + 1] * (xs @ bases[b])
        return jax.ops.segment_sum(m, target, num_segments=x.shape[0])

    def _L2_gnn_ref(X, edge_index, edge_types, W_data, b_data, W_control, b_control, W_self, b_self):
        import jax, jax.numpy as jnp
        import numpy as np
        IN_DIM = 128
        OUT_DIM = 128
        N_NODES = 625
        N_EDGES = 40000
        src, dst = (edge_index[0], edge_index[1])
        Xs = X[src]
        m_data = Xs @ W_data.T + b_data
        m_ctrl = Xs @ W_control.T + b_control
        msg = jnp.where((edge_types == 0)[:, None], m_data, m_ctrl)
        agg = jax.ops.segment_sum(msg, dst, num_segments=X.shape[0])
        out = agg + (X @ W_self.T + b_self)
        return jax.nn.relu(out)

    def _L3_gnn_ref(x, edge_index, W1, b1, W2, b2):
        import jax, jax.numpy as jnp
        import numpy as np
        N_NODES = 6250
        N_EDGES = 50000
        D_IN = 128
        D_HID = 128

        def _gcn_conv(x, W, b, src, dst, norm, num_nodes):
            h = x @ W.T
            msg = h[src] * norm[:, None]
            out = jax.ops.segment_sum(msg, dst, num_segments=num_nodes)
            return out + b
        n = x.shape[0]
        loops = jnp.arange(n, dtype=edge_index.dtype)
        src = jnp.concatenate([edge_index[0], loops])
        dst = jnp.concatenate([edge_index[1], loops])
        deg = jax.ops.segment_sum(jnp.ones_like(dst, dtype=x.dtype), dst, num_segments=n)
        dis = jnp.where(deg > 0, jax.lax.rsqrt(jnp.maximum(deg, 1e-12)), 0.0)
        norm = dis[src] * dis[dst]
        h = jax.nn.relu(_gcn_conv(x, W1, b1, src, dst, norm, n))
        return _gcn_conv(h, W2, b2, src, dst, norm, n)
    edge_index = jnp.stack([src, dst])
    x = _layernorm(x + _L0_gnn_ref(x, src, dst, edge_weight, L0_gnn_kernel, L0_gnn_bias), axis=-1)
    x = _layernorm(x + _L1_gnn_ref(x, L1_gnn_bases, L1_gnn_relation_base_weights, src, dst, edge_type_64), axis=-1)
    x = _layernorm(x + _L2_gnn_ref(x, edge_index, edge_type_2, L2_gnn_W_data, L2_gnn_b_data, L2_gnn_W_control, L2_gnn_b_control, L2_gnn_W_self, L2_gnn_b_self), axis=-1)
    x = _layernorm(x + _L3_gnn_ref(x, edge_index, L3_gnn_W1, L3_gnn_b1, L3_gnn_W2, L3_gnn_b2), axis=-1)
    return x

_drawn_inputs = setup_inputs


def setup_inputs(seed=0):
    import zlib

    import numpy as np

    out = dict(_drawn_inputs(seed))
    spreads = {'L0_gnn_kernel': (1.0, 0.2),
     'L0_gnn_bias': (1.0, 0.2),
     'L3_gnn_b1': (0.0, 0.1),
     'L3_gnn_b2': (0.0, 0.1)}
    factors = {'L2_gnn_b_self': 3.117}
    for name, (base, spread) in spreads.items():
        noise = np.random.default_rng([zlib.crc32(name.encode()), seed]).standard_normal(out[name].shape)
        drawn = base * np.exp(spread * noise) if base else spread * noise
        out[name] = jnp.asarray(drawn.astype(out[name].dtype))
    for name, factor in factors.items():
        out[name] = (out[name] * factor).astype(out[name].dtype)
    return out
```

```python
import numpy as np

import concourse.bass as bass
from concourse import mybir

FP = mybir.dt.float32
I32 = mybir.dt.int32
ALU = mybir.AluOpType
ACT = mybir.ActivationFunctionType

P = 128
N = 6250
E = 106250
NB = 8
R = 64
GT = 4
RING = 4
BODY = GT * RING
T = -(-E // (P * BODY)) * BODY
TX = T + BODY
NG = T // GT
NBODY = NG // RING
W = 40
NQ = 4
QG = NG // NQ
PIECE = 448
NPIECE = 4
CAP = PIECE * NPIECE
BLK = 4
NBLK = -(-N // (BLK * P))
BC = BLK * P
NC = NBLK * BLK
LAST = N - (NBLK - 1) * BC
ACC = N + CAP
NWIN = -(-(N + 1) // W)
EPS = 1e-5
NTAB = GT
TABR = NBLK * BLK * P
PASSES = 5
PRODUCTS_AHEAD = RING
ADDED_AHEAD = 2
ROWS_AHEAD = {1: 1, 2: 2, 3: 2}
AX_X = mybir.AxisListType.X
assert NG % RING == 0 and QG % RING == 0 and LAST < P and ACC >= NWIN * W and ACC >= TABR >= N + P


def gnn_program(nc, src, src_row, dst, type2, type64, weight, x, k0, bias0, bases, rel_weights,
                w_data_ctrl, b_data_ctrl, w_self, b_self, w1, b1, w2, b2, out):
    from contextlib import ExitStack

    ctx = ExitStack()
    with ctx:
        def sb(name, shape, dt=FP):
            return ctx.enter_context(nc.sbuf_tensor(name, shape, dt))

        def sem(name):
            return ctx.enter_context(nc.semaphore(name))

        t1 = nc.dram_tensor("t1", (N, P), FP, kind="Internal").ap()
        t2 = nc.dram_tensor("t2", (2 * N, P), FP, kind="Internal").ap()
        t3 = nc.dram_tensor("t3", (N, P), FP, kind="Internal").ap()
        t4 = nc.dram_tensor("t4", (N, P), FP, kind="Internal").ap()
        tables = [x, t1, t2, t3, t4]
        sums_t = [nc.dram_tensor(f"sums{k}", (TABR, P), FP, kind="Internal").ap() for k in range(NTAB)]

        src_i = sb("src_i", [P, TX], I32)
        src2_i = sb("src2_i", [P, TX], I32)
        wgt = sb("wgt", [P, TX])
        dst_f = sb("dst_f", [P, T])
        rel = sb("rel", [P, TX])
        missed_dst = sb("missed_dst", [P, T])
        alpha = sb("alpha", [P, TX * NB])
        base_bc = sb("base_bc", [P, NG])
        off_bc = sb("off_bc", [P, NG])
        base_i = sb("base_i", [1, NG], I32)
        off_i = sb("off_i", [1, NG], I32)
        missed_any = sb("missed_any", [P, 1])
        flag_i = sb("flag_i", [1, 1], I32)

        xcur = sb("xcur", [P, NC, P])
        acc = sb("acc", [P, ACC])
        dis = sb("dis", [P, NC])
        mv = sb("mv", [P, NC, 2])
        std = sb("std", [P, NC])
        rstd = sb("rstd", [P, NC])
        bst = sb("bst", [P, BLK, 6])
        mvs = sb("mvs", [P, BLK, 2])
        deg_std = sb("deg_std", [P, NC])

        rows = sb("rows", [P, RING, GT, P])
        idx_ring = sb("idx_ring", [P, RING, GT], I32)
        S = sb("S", [P, 2, GT, NB * W])
        S01 = sb("S01", [P, 2, GT, W])
        sel = [[S[:, s, t, 64:64 + P] for t in range(GT)] for s in range(2)]
        masked = [[S[:, s, t, 192:192 + P] for t in range(GT)] for s in range(2)]
        msg = [rows[:, s, :, :] for s in range(2)]
        xwin = [rows[0:W, 2, k, :] for k in range(RING)]
        dup = sb("dup", [P, 2, GT])
        tab_rows = [rows[:, :, :, :].rearrange("p k c f -> p (k c f)"),
                    S[:, :, :, :].rearrange("p s t w -> p (s t w)")[:, 0:NTAB * BC]]

        arena = sb("arena", [P, NB * CAP])
        G = arena[:, :].rearrange("p (b c) -> p b c", b=NB)
        TW = BODY * P
        type_rows = arena[0:R, 0:TW].bitcast(I32)
        type_hot = arena[0:R, TW:2 * TW]
        dst_i = arena[:, 2 * TW:2 * TW + T].bitcast(I32)
        type2_i = arena[:, 2 * TW + TX:2 * TW + 2 * TX].bitcast(I32)
        ok = arena[:, 2 * TW + 2 * TX:2 * TW + 2 * TX + T]
        ok2 = arena[:, 2 * TW + 3 * TX:2 * TW + 3 * TX + T]
        off_ok = arena[:, 2 * TW + 4 * TX:2 * TW + 4 * TX + NG]
        off_ok2 = arena[:, 2 * TW + 5 * TX:2 * TW + 5 * TX + NG]
        src_f = arena[:, 2 * TW + 6 * TX:2 * TW + 6 * TX + T]
        to_spare = arena[:, 2 * TW + 7 * TX:2 * TW + 7 * TX + T]
        HW = TW // 2
        h0 = 2 * TW + 8 * TX
        src_rows = [arena[:, h0 + s * HW:h0 + (s + 1) * HW].bitcast(I32) for s in range(2)]
        C = [arena[0:W, h0 + 2 * HW + s * BC:h0 + 2 * HW + (s + 1) * BC] for s in range(2)]
        assert h0 + 2 * HW + 2 * BC <= NB * CAP
        cnt = arena[0:1, 0:NBLK * BC]
        a0 = NBLK * BC

        def scratch(n):
            nonlocal a0
            a0 += n
            return arena[:, a0 - n:a0]

        xn = [scratch(BC) for _ in range(2)]
        xT = [scratch(BC) for _ in range(2)]
        hst = [scratch(2 * BC) for _ in range(2)]
        assert a0 <= NB * CAP
        stage = [sb(f"stage{k}", [P, BC]) for k in range(2)]

        k0_sb = sb("k0_sb", [P, P])
        bias0_row = sb("bias0_row", [1, P])
        bases_sb = sb("bases_sb", [P, NB, P])
        relw_sb = sb("relw_sb", [R, NB])
        wdc_sb = sb("wdc_sb", [P, 2 * P])
        bdc_bc = sb("bdc_bc", [P, 2 * P])
        ws_sb = sb("ws_sb", [P, P])
        bs_sb = sb("bs_sb", [P, 1])
        w1_sb = sb("w1_sb", [P, P])
        b1_bc = sb("b1_bc", [P, P])
        w2_sb = sb("w2_sb", [P, P])
        b2_bc = sb("b2_bc", [P, P])
        ident = sb("ident", [P, P])
        first_row = sb("first_row", [P, P])
        ones = sb("ones", [P, P])
        zeros = sb("zeros", [P, PIECE])
        iota_w = sb("iota_w", [P, W])
        iota_p = sb("iota_p", [P, 1])
        spare_row = sb("spare_row", [P, 1])
        earlier = sb("earlier", [P, P])
        slow_out_idx = sb("slow_out_idx", [P, 1], I32)
        slow_w = sb("slow_w", [P, 1])
        slow_dup = sb("slow_dup", [P, 1])
        eps_sb = sb("eps_sb", [P, 1])
        slow_idx = sb("slow_idx", [P, 1], I32)
        slow_rel = sb("slow_rel", [P, 1])
        slow_win = sb("slow_win", [P, 1])
        slow_G = sb("slow_G", [P, NB * W])

        bank = [ctx.enter_context(nc.psum_tensor(f"bank{k}", [P, 512], FP)) for k in range(8)]

        edges_in = sem("edges_in")
        src_in = sem("src_in")
        weights_in = sem("weights_in")
        x_in = sem("x_in")
        consts_set = sem("consts_set")
        const_step = sem("const_step")
        acc_zeroed = sem("acc_zeroed")
        xpad_zeroed = sem("xpad_zeroed")
        prep = sem("prep")
        dst_ready = sem("dst_ready")
        base_summed = sem("base_summed")
        missed_ready = sem("missed_ready")
        missed_summed = sem("missed_summed")
        flag_ready = sem("flag_ready")
        types_in = sem("types_in")
        hot_ready = sem("hot_ready")
        alpha_summed = sem("alpha_summed")
        alpha_ready = sem("alpha_ready")

        idx_ready = [sem(f"idx_ready{p}") for p in range(PASSES)]
        gathered = [sem(f"gathered{k}") for k in range(RING)]
        s01_ready = sem("s01_ready")
        s_ready = [sem(f"s_ready{p}") for p in range(PASSES)]
        products = [sem(f"products{p}") for p in range(PASSES)]
        added = [sem(f"added{p}") for p in range(PASSES)]
        counted = sem("counted")
        src_rows_in = [sem(f"src_rows_in{k}") for k in range(2)]
        xwin_in = [sem(f"xwin_in{k}") for k in range(RING)]
        sel_ready = sem("sel_ready")
        dup_step = sem("dup_step")
        c_summed = sem("c_summed")
        c_kept = sem("c_kept")
        messages = sem("messages")
        msg_kept = sem("msg_kept")
        scattered = [sem(f"scattered{k}") for k in range(NTAB)]
        scatter_through = sem("scatter_through")
        tables_done = sem("tables_done")
        tab_in = [sem(f"tab_in{k}") for k in range(2)]
        tab_turned = sem("tab_turned")
        slow0_ready = sem("slow0_ready")
        slow0_summed = sem("slow0_summed")
        slow0_step = sem("slow0_step")
        slow0_rows = sem("slow0_rows")
        slow0_scattered = sem("slow0_scattered")
        pass_done = sem("pass_done")
        part_summed = sem("part_summed")
        based = sem("based")
        based_added = sem("based_added")
        G_zeroed = sem("G_zeroed")

        slow_idx_ready = sem("slow_idx_ready")
        slow0_gathered = sem("slow0_gathered")
        slow_gathered = sem("slow_gathered")
        slow_step = sem("slow_step")
        slow_s = sem("slow_s")
        slow_products = sem("slow_products")
        slow_moved = sem("slow_moved")
        slow_based = sem("slow_based")

        LAYERS = range(5)
        NORMED = (0, 1, 2, 4)
        NTH = {e: n for n, e in enumerate(NORMED)}

        def sems(name, stages):
            return {e: sem(f"{name}{e}") for e in stages}

        staged = sems("staged", LAYERS)
        turned = sems("turned", LAYERS)
        summed = sems("summed", NORMED)
        stats = sem("stats")
        all_stats = sem("all_stats")
        std_ready = sem("std_ready")
        rstd_ready = sem("rstd_ready")
        normed = sems("normed", LAYERS)
        kept = sems("kept", (1, 2))
        rowsT = sems("rowsT", (1, 2, 3))
        rowsT_kept = sems("rowsT_kept", (1, 2, 3))
        projected = sems("projected", (1, 2, 3))
        selfed = sem("selfed")
        rows_ready = sems("rows_ready", (1, 2, 3))
        stored = [[sem(f"stored{e}_{k}") for k in range(2)] for e in range(4)]
        loop_turned = sems("loop_turned", (2, 3))
        acc_set = sems("acc_set", (1, 2, 3))
        scaled = sem("scaled")
        biased = sem("biased")
        deg_ready = sem("deg_ready")
        deg_turned = sem("deg_turned")
        sqrt_ready = sem("sqrt_ready")
        out_stored = sem("out_stored")
        summed_scale = sem("summed_scale")

        waits_passed = sem("waits_passed")
        block = ctx.enter_context(nc.Block())

        def apart(eng):
            eng.sem_inc(waits_passed, 1)

        PAIRS = (NBLK - 1) // 2
        assert NBLK % 2 == 1

        def over_blocks(eng, step):
            step(0, 0, 0, True)
            step(1, 1, 0, True)
            with eng.Fori(1, PAIRS) as j:
                step(j * 2, 0, j, True)
                step(j * 2 + 1, 1, j, True)
            step(NBLK - 1, 0, PAIRS, False)

        def node_rows(table, b):
            return table[bass.ds(b * BC, BC), :].rearrange("(c p) f -> p c f", p=P)

        t2_pairs = t2.rearrange("(n t) f -> n (t f)", t=2)

        @block.sync
        def _(sp):
            sp.dma_start(src_i[:, :], src).then_inc(src_in, 16)
            sp.dma_start(dst_i, dst).then_inc(edges_in, 16)
            sp.dma_start(wgt[:, :], weight).then_inc(edges_in, 16)
            sp.dma_start(type2_i, type2).then_inc(edges_in, 16)
            sp.dma_start(relw_sb[:, :], rel_weights).then_inc(weights_in, 16)
            sp.dma_start(k0_sb[:, :], k0).then_inc(weights_in, 16)
            sp.dma_start(bases_sb[:, :, :], bases.rearrange("b f o -> f b o")).then_inc(weights_in, 16)
            sp.dma_start(wdc_sb[:, :], w_data_ctrl).then_inc(weights_in, 16)
            sp.dma_start(ws_sb[:, :], w_self).then_inc(weights_in, 16)
            sp.dma_start(w1_sb[:, :], w1).then_inc(weights_in, 16)
            sp.dma_start(w2_sb[:, :], w2).then_inc(weights_in, 16)
            sp.dma_start(bs_sb[:, :], b_self).then_inc(weights_in, 16)
            sp.dma_start(bias0_row[:, :], bias0).then_inc(weights_in, 16)
            sp.dma_start(bdc_bc[:, :], b_data_ctrl.to_broadcast([P, 2 * P])).then_inc(weights_in, 16)
            sp.dma_start(b1_bc[:, :], b1.to_broadcast([P, P])).then_inc(weights_in, 16)
            sp.dma_start(b2_bc[:, :], b2.to_broadcast([P, P])).then_inc(weights_in, 16)
            sp.wait_ge(xpad_zeroed, 1)
            sp.dma_start(xcur[:, 0:NC - BLK, :],
                         x[0:(NBLK - 1) * BC, :].rearrange("(c p) f -> p c f", p=P)).then_inc(x_in, 16)
            sp.dma_start(xcur[0:LAST, NC - BLK, :], x[(NBLK - 1) * BC:N, :]).then_inc(x_in, 16)

            sp.wait_ge(flag_ready, 1)
            with sp.Fori(0, NBODY) as i:
                sp.wait_ge(hot_ready, i + 1)
                sp.dma_start(type_rows, type64[0:1, bass.ds(i * TW, TW)].to_broadcast([R, TW])
                             ).then_inc(types_in, 16)
                for h in range(2):
                    sp.wait_ge(sel_ready, i * RING + 2 * h + 2)
                    sp.dma_start(src_rows[h], src_row[0:1, bass.ds(i * TW + h * HW, HW)].to_broadcast([P, HW])
                                 ).then_inc(src_rows_in[h], 16)
                    for k in (2 * h, 2 * h + 1):
                        base = sp.value_load(base_i[0:1, bass.ds(i * RING + k, 1)], min_val=0, max_val=N)
                        sp.wait_ge(messages, i * RING + k + 1)
                        sp.dma_start(xwin[k], x[bass.ds(base, W), :]).then_inc(xwin_in[k], 16)

            sp.wait_ge(tables_done, 1)
            def load_tables(b, k, j, more):
                sp.wait_ge(tab_turned, b + 1)
                for n in range(NTAB):
                    sp.dma_start(tab_rows[k][:, n * BC:(n + 1) * BC].rearrange("p (c f) -> p c f", c=BLK),
                                 node_rows(sums_t[n], b)).then_inc(tab_in[k], 16)
            over_blocks(sp, load_tables)

            def store_x1(b, k, j, more):
                sp.wait_ge(normed[0], b + 1)
                if more:
                    sp.dma_start(node_rows(t1, b), xcur[:, bass.ds(b * BLK, BLK), :]).then_inc(stored[0][k], 16)
                else:
                    sp.dma_start(t1[b * BC:N, :], xcur[0:LAST, b * BLK, :]).then_inc(stored[0][k], 16)
            over_blocks(sp, store_x1)

            for e, table, width in ((1, t2_pairs, 2 * P), (2, t3, P), (3, t4, P)):
                def store_rows(b, k, j, more):
                    sp.wait_ge(rows_ready[e], b + ROWS_AHEAD[e] + 1)
                    if more:
                        sp.dma_start(node_rows(table, b), hst[k][:, 0:BLK * width].rearrange(
                            "p (c f) -> p c f", c=BLK)).then_inc(stored[e][k], 16)
                    else:
                        sp.dma_start(table[b * BC:N, :], hst[k][0:LAST, 0:width]).then_inc(stored[e][k], 16)
                over_blocks(sp, store_rows)

            def store_out(b, k, j, more):
                sp.wait_ge(normed[4], b + 1)
                if more:
                    sp.dma_start(node_rows(out, b), xcur[:, bass.ds(b * BLK, BLK), :]).then_inc(out_stored, 16)
                else:
                    sp.dma_start(out[b * BC:N, :], xcur[0:LAST, b * BLK, :]).then_inc(out_stored, 16)
            over_blocks(sp, store_out)
            sp.wait_ge(out_stored, 16 * NBLK)

        @block.gpsimd
        def _(pool):
            for e in (1, 2):
                pool.sem_inc(kept[e], 2)
            nc.gpsimd.memset(ones[:, :], 1.0).then_inc(const_step, 1)
            nc.gpsimd.memset(xcur[:, NC - BLK:NC, :], 0.0).then_inc(xpad_zeroed, 1)
            nc.gpsimd.memset(zeros[:, :], 0.0).then_inc(consts_set, 1)
            nc.gpsimd.memset(eps_sb[:, :], EPS).then_inc(consts_set, 1)
            nc.gpsimd.iota(iota_w[:, :], [[1, W]], base=0, channel_multiplier=0,
                           allow_small_or_imprecise_dtypes=True).then_inc(consts_set, 1)
            nc.gpsimd.iota(iota_p[:, :], [[0, 1]], base=0, channel_multiplier=1,
                           allow_small_or_imprecise_dtypes=True).then_inc(consts_set, 1)
            pool.wait_ge(const_step, 1)
            nc.gpsimd.affine_select(out=ident[:, :], in_=ones[:, :], compare_op=ALU.is_equal, fill=0.0,
                                    base=0, pattern=[[-1, P]], channel_multiplier=1).then_inc(consts_set, 1)
            nc.gpsimd.affine_select(out=first_row[:, :], in_=ones[:, :], compare_op=ALU.is_equal, fill=0.0,
                                    base=0, pattern=[[0, P]], channel_multiplier=1).then_inc(consts_set, 1)
            nc.gpsimd.affine_select(out=earlier[:, :], in_=ones[:, :], compare_op=ALU.is_ge, fill=0.0,
                                    base=-1, pattern=[[-1, P]], channel_multiplier=1).then_inc(consts_set, 1)
            nc.gpsimd.iota(spare_row[:, :], [[0, 1]], base=N, channel_multiplier=1,
                           allow_small_or_imprecise_dtypes=True).then_inc(consts_set, 1)

            def gather_pass(p):
                with pool.Fori(0, NBODY) as i:
                    for k in range(RING):
                        g = i * RING + k
                        pool.wait_ge(idx_ready[p], g + 1)
                        pool.wait_ge(products[p], g + 1)
                        apart(pool)
                        for t in range(GT):
                            nc.gpsimd.indirect_dma_start(
                                out=rows[:, k, t, :], out_offset=None, in_=tables[p],
                                in_offset=bass.IndirectOffsetOnAxis(ap=idx_ring[:, k, t:t + 1], axis=0),
                            ).then_inc(gathered[k], 16)

            def gather_general(p, flag):
                with pool.If(flag != 0):
                    with pool.Fori(0, T) as t:
                        pool.wait_ge(slow_idx_ready, t + (p * T + 1))
                        apart(pool)
                        nc.gpsimd.indirect_dma_start(
                            out=rows[:, 0, 0, :], out_offset=None, in_=tables[p],
                            in_offset=bass.IndirectOffsetOnAxis(ap=slow_idx[:, 0:1], axis=0),
                        ).then_inc(slow_gathered, 16)

            pool.sem_inc(scatter_through, 3)
            pool.wait_ge(acc_zeroed, 1)
            for t in range(NTAB):
                pool.dma_start(sums_t[t].rearrange("(p r) f -> p (r f)", p=P), acc[:, 0:TABR]).then_inc(scattered[t], 16)
            with pool.Fori(0, NBODY) as i:
                for k in range(RING):
                    g = i * RING + k
                    pool.wait_ge(idx_ready[0], g + 1)
                    pool.wait_ge(msg_kept, g + 3)
                    for t in range(NTAB):
                        pool.wait_ge(scattered[t], g * 16 + 16)
                        apart(pool)
                        if t == NTAB - 1:
                            pool.sem_inc(scatter_through, 1)
                        nc.gpsimd.indirect_dma_start(
                            out=sums_t[t], out_offset=bass.IndirectOffsetOnAxis(ap=idx_ring[:, k, t:t + 1], axis=0),
                            in_=msg[k % 2][:, t, :], in_offset=None, compute_op=ALU.add).then_inc(scattered[t], 16)
            for t in range(NTAB):
                pool.wait_ge(scattered[t], (NG + 1) * 16)
            flag = pool.value_load(flag_i[0:1, 0:1], min_val=0, max_val=1)
            with pool.If(flag != 0):
                with pool.Fori(0, T) as t:
                    pool.wait_ge(slow_idx_ready, t + 1)
                    apart(pool)
                    nc.gpsimd.indirect_dma_start(
                        out=rows[:, 0, 0, :], out_offset=None, in_=tables[0],
                        in_offset=bass.IndirectOffsetOnAxis(ap=slow_idx[:, 0:1], axis=0),
                    ).then_inc(slow0_gathered, 16)
                    pool.wait_ge(slow0_rows, t + 1)
                    apart(pool)
                    nc.gpsimd.indirect_dma_start(
                        out=sums_t[0], out_offset=bass.IndirectOffsetOnAxis(ap=slow_out_idx[:, 0:1], axis=0),
                        in_=rows[:, 0, 2, :], in_offset=None, compute_op=ALU.add).then_inc(slow0_scattered, 16)
                pool.wait_ge(slow0_scattered, 16 * T)
            pool.sem_inc(tables_done, 1)

            pool.wait_ge(alpha_summed, NBODY + 1)
            nc.gpsimd.memset(arena[:, :], 0.0).then_inc(G_zeroed, 1)

            for p in range(1, PASSES):
                e = p - 1
                if e in (1, 2):
                    def keep(b, k, j, more):
                        pool.wait_ge(normed[e], b + 1)
                        to = xcur[:, bass.ds(b * BLK, BLK), :]
                        rows_in = xn[k].rearrange("p (c f) -> p c f", c=BLK)
                        if e == 1:
                            nc.gpsimd.tensor_copy(to, rows_in).then_inc(kept[e], 1)
                        else:
                            nc.gpsimd.tensor_tensor(to, rows_in, b2_bc[:, :].unsqueeze(1).to_broadcast([P, BLK, P]),
                                                    ALU.add).then_inc(kept[e], 1)
                    over_blocks(pool, keep)
                pool.wait_ge(stored[e][0], 16 * (PAIRS + 1))
                pool.wait_ge(stored[e][1], 16 * PAIRS)
                gather_pass(p)
                gather_general(p, flag)

        @block.scalar
        def _(act):
            act.sem_inc(alpha_ready, 1)
            act.sem_inc(staged[0], 2)
            for e in (1, 2, 3):
                act.sem_inc(rowsT_kept[e], 2)
                act.sem_inc(acc_set[e], 2)

            act.sem_inc(c_kept, 2)
            act.sem_inc(msg_kept, 2)
            def keep_window(i, k):
                act.wait_ge(c_summed, i * RING + (k + 3))
                act.wait_ge(messages, i * RING + (k + 3))
                nc.scalar.activation(C[k % 2], bank[k % 2][0:W, :], ACT.Copy).then_inc(c_kept, 1)

            def keep_rows(i, k):
                act.wait_ge(messages, i * RING + (k + 5))
                act.wait_ge(scatter_through, i * RING + (k + 3))
                nc.scalar.activation(msg[k % 2].rearrange("p t f -> p (t f)"), bank[4 + k % 2][:, :],
                                     ACT.Copy).then_inc(msg_kept, 1)

            with act.Fori(0, NBODY) as i:
                keep_window(i, 0)
                for k in range(RING - 1):
                    keep_window(i, k + 1)
                    keep_rows(i, k)
                keep_rows(i, RING - 1)
                act.wait_ge(alpha_summed, i + 2)
                apart(act)
                nc.scalar.activation(alpha[:, bass.ds(i * BODY * NB, BODY * NB)], bank[2][:, 0:BODY * NB],
                                     ACT.Copy).then_inc(alpha_ready, 1)

            def take_acc(e, func):
                act.wait_ge(pass_done, e)

                def step(b, k, j, more):
                    act.wait_ge(turned[e], b + 1)
                    apart(act)
                    nc.scalar.activation(stage[k][:, :], acc[:, bass.ds(b * BC, BC)], func).then_inc(staged[e], 1)
                over_blocks(act, step)

            def take_std(e):
                act.wait_ge(all_stats, NTH[e] + 1)
                nc.scalar.activation(std[:, :], mv[:, :, 1], ACT.Sqrt, bias=eps_sb[:, 0:1]).then_inc(std_ready, 1)

            act.wait_ge(consts_set, 8)
            act.wait_ge(weights_in, 16 * 12)

            def take_tables(b, k, j, more):
                act.wait_ge(tab_turned, b + 3)
                act.wait_ge(turned[0], b + 1)
                nc.scalar.activation(stage[k][:, :], bank[2 + k][:, :], ACT.Copy).then_inc(staged[0], 1)
            over_blocks(act, take_tables)
            take_std(0)

            with act.Fori(0, NQ) as q:
                for j in range(NPIECE):
                    act.wait_ge(based, q * NPIECE + (j + 1))
                    nc.scalar.activation(G[:, :, j * PIECE:(j + 1) * PIECE],
                                         zeros[:, :].unsqueeze(1).to_broadcast([P, NB, PIECE]),
                                         ACT.Copy).then_inc(G_zeroed, 1)

            take_acc(1, ACT.Copy)
            take_std(1)

            def keep_rowsT(e, b, k):
                act.wait_ge(rowsT[e], b + 3)
                act.wait_ge(projected[e], b + 1)
                nc.scalar.activation(xT[k], bank[2 + k][:, :], ACT.Copy).then_inc(rowsT_kept[e], 1)

            def stage1(b, k, j, more):
                if more:
                    keep_rowsT(1, b + 1, 1 - k)
                act.wait_ge(selfed, b + 1)
                apart(act)
                nc.scalar.activation(acc[:, bass.ds(b * BC, BC)], bank[6 + k][:, :], ACT.Identity,
                                     bias=bs_sb[:, 0:1]).then_inc(acc_set[1], 1)
            keep_rowsT(1, 0, 0)
            over_blocks(act, stage1)

            take_acc(2, ACT.Relu)
            act.wait_ge(deg_turned, 1)
            nc.scalar.activation(deg_std[:, :], bank[7][:, 0:NC], ACT.Sqrt, bias=ones[:, 0:1]).then_inc(sqrt_ready, 1)
            take_std(2)

            def start_acc(e, b, k):
                act.wait_ge(loop_turned[e], b + 3)
                apart(act)
                nc.scalar.activation(acc[:, bass.ds(b * BC, BC)], bank[6 + k][:, :], ACT.Copy).then_inc(acc_set[e], 1)

            def stage2(b, k, j, more):
                if more:
                    keep_rowsT(2, b + 1, 1 - k)
                start_acc(2, b, k)
            keep_rowsT(2, 0, 0)
            over_blocks(act, stage2)

            act.wait_ge(pass_done, 3)

            def stage3(b, k, j, more):
                act.wait_ge(turned[3], b + 1)
                apart(act)
                nc.scalar.activation(stage[k][:, :], acc[:, bass.ds(b * BC, BC)], ACT.Copy).then_inc(staged[3], 1)
                act.wait_ge(biased, b + 1)
                nc.scalar.activation(xn[k], xn[k], ACT.Relu).then_inc(normed[3], 1)
                keep_rowsT(3, b, k)
                start_acc(3, b, k)
            over_blocks(act, stage3)

            take_acc(4, ACT.Copy)
            take_std(4)

        @block.tensor
        def _(pe):
            for p in range(1, PASSES):
                pe.sem_inc(products[p], PRODUCTS_AHEAD)
            pe.sem_inc(alpha_summed, 1)
            pe.sem_inc(c_summed, 2)
            pe.sem_inc(messages, RING)
            pe.sem_inc(tab_turned, 2)
            for e in LAYERS:
                pe.sem_inc(turned[e], 2)
            for e in (1, 2, 3):
                pe.sem_inc(projected[e], 2)
                pe.sem_inc(rowsT[e], 2)
            for e in (2, 3):
                pe.sem_inc(loop_turned[e], 2)
            pe.wait_ge(consts_set, 8)
            pe.wait_ge(dst_ready, 1)
            nc.tensor.matmul(bank[0][:, 0:NG], first_row[:, :], dst_f[:, 0:T:GT], start=True,
                             stop=True).then_inc(base_summed, 1)
            pe.wait_ge(missed_ready, 1)
            nc.tensor.matmul(bank[0][0:1, 0:1], missed_any[:, 0:1], ones[:, 0:1], start=True,
                             stop=True).then_inc(missed_summed, 1)
            pe.wait_ge(weights_in, 16 * 12)

            def group_products(p, i, k):
                g = i * RING + k
                width = NB * W if p == 1 else W
                pe.wait_ge(gathered[k], i * (16 * GT) + ((p - 1) * NBODY + 1) * 16 * GT)
                pe.wait_ge(s_ready[p], g + 1)
                pe.wait_ge(added[p], g + 1)
                if p == 2:
                    for t in range(GT):
                        nc.tensor.matmul(bank[4 + k % 2][0:1, 0:W], ones[:, 0:1], S[:, k % 2, t, 0:W],
                                         start=t == 0, stop=t == GT - 1)
                for t in range(GT):
                    last = nc.tensor.matmul(bank[k % 2][:, 0:width], rows[:, k, t, :], S[:, k % 2, t, 0:width],
                                            start=t == 0, stop=t == GT - 1)
                last.then_inc(products[p], 1)

            def pass_products(p):
                with pe.Fori(0, NBODY) as i:
                    for k in range(RING):
                        group_products(p, i, k)

            def general_products(p, flag):
                width = NB * W if p == 1 else W
                with pe.If(flag != 0):
                    with pe.Fori(0, T) as t:
                        pe.wait_ge(slow_gathered, t * 16 + ((p - 1) * T + 1) * 16)
                        apart(pe)
                        with pe.Fori(0, NWIN) as c:
                            n = t * NWIN + c + (p - 1) * T * NWIN
                            pe.wait_ge(slow_s, n + 1)
                            if p == 2:
                                nc.tensor.matmul(bank[4][0:1, 0:W], ones[:, 0:1], S[:, 0, 0, 0:W], start=True, stop=True)
                            nc.tensor.matmul(bank[0][:, 0:width], rows[:, 0, 0, :], S[:, 0, 0, 0:width], start=True,
                                             stop=True).then_inc(slow_products, 1)
                            if p == 1:
                                pe.wait_ge(slow_moved, n + 1)
                                for b in range(NB):
                                    last = nc.tensor.matmul(bank[1][:, 0:W], bases_sb[:, b, :],
                                                            slow_G[:, b * W:(b + 1) * W], start=b == 0, stop=b == NB - 1)
                                last.then_inc(slow_based, 1)

            def turn(to, rows_in, rhs, more=False):
                for c in range(BLK):
                    last = nc.tensor.matmul(to[:, c * P:(c + 1) * P], rows_in[:, c * P:(c + 1) * P], rhs,
                                            start=True, stop=not more)
                    if more:
                        last = nc.tensor.matmul(to[:, c * P:(c + 1) * P], ones[0:1, :], bias0_row[0:1, :],
                                                start=False, stop=True)
                return last

            def turn_acc(e, rhs):
                def step(b, k, j, more):
                    pe.wait_ge(staged[e], b + 1)
                    pe.wait_ge(summed[e], b + 1)
                    turn(bank[k], stage[k], rhs).then_inc(turned[e], 1)
                over_blocks(pe, step)

            def turn_rows(e, b, k):
                pe.wait_ge(normed[e], b + 1)
                pe.wait_ge(rowsT_kept[e], b + 1)
                turn(bank[2 + k], xn[k], ident[:, :]).then_inc(rowsT[e], 1)

            def window_by_edge(i, k):
                g = i * RING + k
                pe.wait_ge(sel_ready, g + (RING + 1))
                pe.wait_ge(c_kept, g + 1)
                for t in range(GT):
                    last = nc.tensor.matmul(bank[k % 2][0:W, t * P:(t + 1) * P], S[:, k % 2, t, 0:W], sel[k % 2][t],
                                            start=True, stop=True)
                last.then_inc(c_summed, 1)

            def rows_to_add(i, k):
                g = i * RING + k
                pe.wait_ge(c_kept, g + 3)
                pe.wait_ge(xwin_in[k], i * 16 + 16)
                pe.wait_ge(msg_kept, g + 1)
                for t in range(GT):
                    last = nc.tensor.matmul(bank[4 + k % 2][:, t * P:(t + 1) * P], C[k % 2][:, t * P:(t + 1) * P],
                                            xwin[k], start=True, stop=True)
                last.then_inc(messages, 1)

            with pe.Fori(0, NBODY) as i:
                window_by_edge(i, 0)
                for k in range(RING - 1):
                    window_by_edge(i, k + 1)
                    rows_to_add(i, k)
                pe.wait_ge(hot_ready, i + 2)
                pe.wait_ge(alpha_ready, i + 1)
                for t in range(BODY):
                    last = nc.tensor.matmul(bank[2][:, t * NB:(t + 1) * NB], type_hot[:, t * P:(t + 1) * P],
                                            relw_sb[:, :], start=True, stop=True)
                last.then_inc(alpha_summed, 1)
                rows_to_add(i, RING - 1)
            flag = pe.value_load(flag_i[0:1, 0:1], min_val=0, max_val=1)
            with pe.If(flag != 0):
                with pe.Fori(0, T) as t:
                    pe.wait_ge(slow0_ready, t * 2 + 1)
                    nc.tensor.matmul(bank[0][:, 0:P], ones[:, :], masked[0][0], start=True, stop=True).then_inc(slow0_summed, 1)
                    pe.wait_ge(slow0_ready, t * 2 + 2)
                    nc.tensor.matmul(bank[1][:, 0:P], sel[0][0], rows[:, 0, 1, :], start=True, stop=True).then_inc(slow0_summed, 1)

            def turn_tables(b, k, j, more):
                pe.wait_ge(tab_in[k], j * (16 * NTAB) + 16 * NTAB)
                pe.wait_ge(staged[0], b + 1)
                for c in range(BLK):
                    for n in range(NTAB):
                        last = nc.tensor.matmul(bank[2 + k][:, c * P:(c + 1) * P],
                                                tab_rows[k][:, n * BC + c * P:n * BC + (c + 1) * P], ident[:, :],
                                                start=n == 0, stop=n == NTAB - 1)
                last.then_inc(tab_turned, 1)

            def stage0(b, k, j, more):
                turn_tables(b, k, j, more)
                pe.wait_ge(staged[0], b + 3)
                pe.wait_ge(summed[0], b + 1)
                turn(bank[k], stage[k], k0_sb[:, :], True).then_inc(turned[0], 1)
            pe.wait_ge(alpha_ready, NBODY + 1)
            over_blocks(pe, stage0)

            with pe.Fori(0, NQ) as q:
                with pe.Fori(0, QG // RING) as i:
                    for k in range(RING):
                        group_products(1, q * (QG // RING) + i, k)
                pe.wait_ge(part_summed, q + 1)
                for j in range(NPIECE):
                    pe.wait_ge(based_added, q * NPIECE + (j + 1))
                    for b in range(NB):
                        last = nc.tensor.matmul(bank[4 + j % 2][:, 0:PIECE], bases_sb[:, b, :],
                                                G[:, b, j * PIECE:(j + 1) * PIECE], start=b == 0, stop=b == NB - 1)
                    last.then_inc(based, 1)
            general_products(1, flag)
            turn_acc(1, ident[:, :])

            def stage1(b, k, j, more):
                if more:
                    turn_rows(1, b + 1, 1 - k)
                pe.wait_ge(rowsT_kept[1], b + 3)
                pe.wait_ge(rows_ready[1], b + 1)
                for c in range(BLK):
                    last = nc.tensor.matmul(bank[4 + c // 2][:, (c % 2) * 2 * P:(c % 2 + 1) * 2 * P],
                                            xT[k][:, c * P:(c + 1) * P], wdc_sb[:, :], start=True, stop=True)
                last.then_inc(projected[1], 1)
                pe.wait_ge(acc_set[1], b + 1)
                nc.tensor.matmul(bank[6 + k][:, :], ws_sb[:, :], xT[k], start=True, stop=True).then_inc(selfed, 1)
            turn_rows(1, 0, 0)
            over_blocks(pe, stage1)

            pass_products(2)
            general_products(2, flag)
            pe.wait_ge(pass_done, 2)
            for c in range(NC):
                last = nc.tensor.matmul(bank[7][:, c:c + 1], cnt[:, c * P:(c + 1) * P], ones[0:1, 0:1], start=True, stop=True)
            last.then_inc(deg_turned, 1)
            turn_acc(2, ident[:, :])

            def project(e, b, k, w):
                pe.wait_ge(rowsT_kept[e], b + 3)
                pe.wait_ge(rows_ready[e], b + 1)
                turn(bank[4 + k], xT[k], w).then_inc(projected[e], 1)

            def turn_loops(e, b, k):
                pe.wait_ge(rows_ready[e], b + 3)
                pe.wait_ge(acc_set[e], b + 1)
                turn(bank[6 + k], hst[k], ident[:, :]).then_inc(loop_turned[e], 1)

            def stage2(b, k, j, more):
                if more:
                    turn_rows(2, b + 1, 1 - k)
                project(2, b, k, w1_sb[:, :])
                turn_loops(2, b, k)
            pe.wait_ge(sqrt_ready, 1)
            turn_rows(2, 0, 0)
            over_blocks(pe, stage2)

            pass_products(3)
            general_products(3, flag)

            def stage3(b, k, j, more):
                pe.wait_ge(staged[3], b + 1)
                pe.wait_ge(scaled, b + 1)
                turn(bank[k], stage[k], ident[:, :]).then_inc(turned[3], 1)
                turn_rows(3, b, k)
                project(3, b, k, w2_sb[:, :])
                turn_loops(3, b, k)
            over_blocks(pe, stage3)

            pass_products(4)
            general_products(4, flag)
            turn_acc(4, ident[:, :])

        @block.vector
        def _(dve):
            nprep = [0]

            def after(ins):
                nprep[0] += 1
                ins.then_inc(prep, 1)
                dve.wait_ge(prep, nprep[0])

            for p in range(1, PASSES):
                dve.sem_inc(added[p], ADDED_AHEAD)
            dve.sem_inc(based_added, 2)
            dve.sem_inc(sel_ready, RING)
            dve.sem_inc(hot_ready, 1)
            dve.sem_inc(scaled, 2)
            for e in NORMED:
                dve.sem_inc(summed[e], 2)
            for e in (1, 2, 3):
                dve.sem_inc(rows_ready[e], ROWS_AHEAD[e])

            def copy_idx(p, i, k):
                source = src2_i if p == 2 else src_i
                nc.vector.tensor_copy(idx_ring[:, k, :], source[:, bass.ds(i * BODY + k * GT, GT)]).then_inc(idx_ready[p], 1)

            dve.wait_ge(src_in, 16)
            nc.vector.memset(acc[:, :], 0.0).then_inc(acc_zeroed, 1)

            dve.wait_ge(edges_in, 16 * 3)
            nc.vector.tensor_copy(dst_f[:, :], dst_i).then_inc(dst_ready, 1)
            after(nc.vector.tensor_copy(src_f, src_i[:, 0:T]))
            dve.wait_ge(consts_set, 8)
            after(nc.vector.tensor_scalar(to_spare, src_f, -1.0, spare_row[:, 0:1], ALU.mult, ALU.add))
            after(nc.vector.tensor_scalar(src2_i[:, :], type2_i, 0, None, ALU.not_equal))
            after(nc.vector.scalar_tensor_tensor(src2_i[:, :], src_i[:, :], 2, src2_i[:, :], ALU.mult, ALU.add))
            dve.wait_ge(base_summed, 1)
            after(nc.vector.tensor_copy(base_bc[:, :], bank[0][:, 0:NG]))
            after(nc.vector.tensor_copy(base_i[:, :], base_bc[0:1, :]))
            parts = base_bc[:, :].rearrange("p (q g) -> p q g", q=NQ)
            after(nc.vector.tensor_tensor(off_bc[:, :].rearrange("p (q g) -> p q g", q=NQ), parts,
                                          parts[:, :, 0:1].to_broadcast([P, NQ, QG]), ALU.subtract))
            after(nc.vector.tensor_scalar(off_ok, off_bc[:, :], 0.0, None, ALU.is_ge))
            after(nc.vector.scalar_tensor_tensor(off_ok2, off_bc[:, :], float(CAP - W), off_ok, ALU.is_le, ALU.mult))
            after(nc.vector.tensor_scalar(off_bc[:, :], off_bc[:, :], 0.0, float(CAP - W), ALU.max, ALU.min))
            after(nc.vector.tensor_copy(off_i[:, :], off_bc[0:1, :]))

            def by_group(a):
                return a.rearrange("p (g t) -> p g t", t=GT)

            def to_tiles(a):
                return a.unsqueeze(2).to_broadcast([P, NG, GT])

            after(nc.vector.memset(rel[:, T:TX], -1.0))
            after(nc.vector.memset(alpha[:, T * NB:TX * NB], 0.0))
            after(nc.vector.tensor_tensor(by_group(rel[:, 0:T]), by_group(dst_f[:, :]), to_tiles(base_bc[:, :]), ALU.subtract))
            after(nc.vector.scalar_tensor_tensor(by_group(ok), by_group(rel[:, 0:T]), 0.0, to_tiles(off_ok2), ALU.is_ge, ALU.mult))
            after(nc.vector.scalar_tensor_tensor(ok2, rel[:, 0:T], float(W), ok, ALU.is_lt, ALU.mult))
            after(nc.vector.scalar_tensor_tensor(rel[:, 0:T], rel[:, 0:T], 1.0, ok2, ALU.add, ALU.mult))
            after(nc.vector.tensor_scalar(rel[:, 0:T], rel[:, 0:T], -1.0, None, ALU.add))
            after(nc.vector.tensor_scalar(ok, ok2, -1.0, 1.0, ALU.mult, ALU.add))
            nc.vector.reduce_max(missed_any[:, 0:1], ok, AX_X).then_inc(missed_ready, 1)
            after(nc.vector.scalar_tensor_tensor(missed_dst[:, :], dst_f[:, :], 1.0, ok, ALU.add, ALU.mult))
            after(nc.vector.tensor_scalar(missed_dst[:, :], missed_dst[:, :], -1.0, None, ALU.add))
            dve.wait_ge(missed_summed, 1)
            nc.vector.tensor_scalar(flag_i[0:1, 0:1], bank[0][0:1, 0:1], 0.0, None, ALU.is_gt).then_inc(flag_ready, 1)
            dve.wait_ge(flag_ready, 1)
            flag = dve.value_load(flag_i[0:1, 0:1], min_val=0, max_val=1)
            dve.wait_ge(consts_set, 8)
            dve.wait_ge(acc_zeroed, 1)

            def make_S(p, g, k):
                dve.wait_ge(products[p], g + (PRODUCTS_AHEAD - 1))
                if p == 1:
                    nc.vector.tensor_tensor(S01[:, k % 2, :, :], iota_w[:, :].unsqueeze(1).to_broadcast([P, GT, W]),
                                            rel[:, bass.ds(g * GT, GT)].unsqueeze(2).to_broadcast([P, GT, W]),
                                            ALU.is_equal).then_inc(s01_ready, 1)
                    dve.wait_ge(s01_ready, g + 1)
                    nc.vector.tensor_tensor(
                        S[:, k % 2, :, :].rearrange("p t (b w) -> p t b w", w=W),
                        S01[:, k % 2, :, :].unsqueeze(2).to_broadcast([P, GT, NB, W]),
                        alpha[:, bass.ds(g * (GT * NB), GT * NB)].rearrange("p (t b) -> p t b", b=NB)
                        .unsqueeze(3).to_broadcast([P, GT, NB, W]), ALU.mult).then_inc(s_ready[p], 1)
                    return
                for t in range(GT):
                    last = nc.vector.tensor_scalar(S[:, k % 2, t, 0:W], iota_w[:, :], rel[:, bass.ds(g * GT + t, 1)], None,
                                                   ALU.is_equal)
                last.then_inc(s_ready[p], 1)

            def add_sums(p, g, k, at):
                dve.wait_ge(products[p], g + (PRODUCTS_AHEAD + 1))
                dve.wait_ge(added[p], g + ADDED_AHEAD)
                if p == 1:
                    to = G[:, :, bass.ds(at, W)]
                    sums = bank[k % 2][:, 0:NB * W].rearrange("p (b w) -> p b w", w=W)
                else:
                    to, sums = acc[:, bass.ds(at, W)], bank[k % 2][:, 0:W]
                if p == 2:
                    counts = cnt[:, bass.ds(at, W)]
                    nc.vector.tensor_tensor(counts, counts, bank[4 + k % 2][0:1, 0:W], ALU.add).then_inc(counted, 1)
                    dve.wait_ge(counted, g + 1)
                nc.vector.tensor_tensor(to, to, sums, ALU.add).then_inc(added[p], 1)

            def sum_body(p, i):
                places = off_i if p == 1 else base_i
                for k in range(RING):
                    g = i * RING + k
                    make_S(p, g + 1, k + 1)
                    at = dve.value_load(places[0:1, bass.ds(g, 1)], min_val=0, max_val=CAP - W if p == 1 else N)
                    add_sums(p, g, k, at)
                    copy_idx(p, i + 1, k)

            def start_pass(p):
                for k in range(RING):
                    copy_idx(p, 0, k)
                make_S(p, 0, 0)

            def general_sums(p):
                source = src2_i if p == 2 else src_i
                with dve.If(flag != 0):
                    dve.wait_ge(s_ready[p], NG + 1)
                    with dve.Fori(0, T) as t:
                        nc.vector.tensor_copy(slow_idx[:, 0:1], source[:, bass.ds(t, 1)]).then_inc(slow_idx_ready, 1)
                        nc.vector.tensor_copy(slow_rel[:, 0:1], missed_dst[:, bass.ds(t, 1)]).then_inc(slow_step, 1)
                        with dve.Fori(0, NWIN) as c:
                            n = t * NWIN + c
                            steps = n * 2 + t + (p - 1) * (2 * NWIN + 1) * T
                            past = (p - 1) * T * NWIN
                            dve.wait_ge(slow_step, steps + 1)
                            if p == 1:
                                nc.vector.tensor_scalar(S01[:, 0, 0, :], iota_w[:, :], slow_rel[:, 0:1], None,
                                                        ALU.is_equal).then_inc(s01_ready, 1)
                                dve.wait_ge(s01_ready, n + (NG + 2))
                                nc.vector.tensor_tensor(
                                    S[:, 0, 0, :].rearrange("p (b w) -> p b w", w=W),
                                    S01[:, 0, 0, :].unsqueeze(1).to_broadcast([P, NB, W]),
                                    alpha[:, bass.ds(t * NB, NB)].unsqueeze(2).to_broadcast([P, NB, W]),
                                    ALU.mult).then_inc(slow_s, 1)
                            else:
                                nc.vector.tensor_scalar(S[:, 0, 0, 0:W], iota_w[:, :], slow_rel[:, 0:1], None,
                                                        ALU.is_equal).then_inc(slow_s, 1)
                            dve.wait_ge(slow_s, n + (past + 1))
                            nc.vector.tensor_scalar(slow_rel[:, 0:1], slow_rel[:, 0:1], float(-W), None,
                                                    ALU.add).then_inc(slow_step, 1)
                            dve.wait_ge(slow_products, n + (past + 1))
                            to = acc[:, bass.ds(c * W, W)]
                            sums = bank[0][:, 0:W]
                            if p == 1:
                                nc.vector.tensor_copy(slow_G[:, :], bank[0][:, 0:NB * W]).then_inc(slow_moved, 1)
                                dve.wait_ge(slow_based, n + 1)
                                sums = bank[1][:, 0:W]
                            if p == 2:
                                counts = cnt[:, bass.ds(c * W, W)]
                                nc.vector.tensor_tensor(counts, counts, bank[4][0:1, 0:W], ALU.add).then_inc(counted, 1)
                                dve.wait_ge(counted, n + (NG + 1))
                            nc.vector.tensor_tensor(to, to, sums, ALU.add).then_inc(slow_step, 1)
                            dve.wait_ge(slow_step, steps + 3)

            def finish_pass(p):
                dve.wait_ge(added[p], NG + ADDED_AHEAD)
                general_sums(p)
                dve.sem_inc(pass_done, 1)

            def blk(b):
                return bass.ds(b * BLK, BLK)

            def as_chunks(a):
                return a.rearrange("p (c f) -> p c f", c=BLK)

            def to_rows(v):
                return v.unsqueeze(2).to_broadcast([P, BLK, P])

            def residual(e):
                seen = NTH[e] * NBLK * 3

                def step(b, k, j, more):
                    dve.wait_ge(turned[e], b + 3)
                    to = xcur[:, blk(b), :]
                    new = as_chunks(bank[k][:, :])
                    if e == 4:
                        nc.vector.tensor_tensor(as_chunks(xn[k]), new, to_rows(dis[:, blk(b)]),
                                                ALU.mult).then_inc(summed_scale, 1)
                        dve.wait_ge(summed_scale, b + 1)
                        new = as_chunks(xn[k])
                    nc.vector.tensor_tensor(to, new, to, ALU.add).then_inc(summed[e], 1)
                    dve.wait_ge(summed[e], b + 3)
                    apart(dve)
                    for c in range(BLK):
                        last = nc.vector.bn_stats(bst[:, c, :], xcur[:, bass.ds(b * BLK + c, 1), :].rearrange("p c f -> p (c f)"))
                    last.then_inc(stats, 1)
                    dve.wait_ge(stats, b * 3 + (seen + 1))
                    apart(dve)
                    for c in range(BLK):
                        last = nc.vector.bn_aggr(mvs[:, c, :], bst[:, c, :])
                    last.then_inc(stats, 1)
                    dve.wait_ge(stats, b * 3 + (seen + 2))
                    nc.vector.tensor_copy(mv[:, blk(b), :], mvs[:, :, :]).then_inc(stats, 1)
                    dve.wait_ge(stats, b * 3 + (seen + 3))
                over_blocks(dve, step)

            def finish_stats(e):
                dve.sem_inc(all_stats, 1)
                dve.wait_ge(std_ready, NTH[e] + 1)
                nc.vector.reciprocal(rstd[:, :], std[:, :]).then_inc(rstd_ready, 1)
                dve.wait_ge(rstd_ready, NTH[e] + 1)

            def norm(e, b, k, to_xn):
                if to_xn:
                    dve.wait_ge(rowsT[e], b + 1)
                    dve.wait_ge(kept[e], b + 1)
                for c in range(BLK):
                    ch = b * BLK + c
                    row = xcur[:, bass.ds(ch, 1), :].rearrange("p c f -> p (c f)")
                    last = nc.vector.tensor_scalar(xn[k][:, c * P:(c + 1) * P] if to_xn else row, row,
                                                   mv[:, bass.ds(ch, 1), 0:1].rearrange("p c s -> p (c s)"),
                                                   rstd[:, bass.ds(ch, 1)], ALU.subtract, ALU.mult)
                last.then_inc(normed[e], 1)

            def slot_stored(e, k, j):
                if not isinstance(j, int) or j > 0:
                    dve.wait_ge(stored[e][k], j * 16)

            def scale_rows(e, b, k, j):
                dve.wait_ge(projected[e], b + 3)
                dve.wait_ge(loop_turned[e], b + 1)
                slot_stored(e, k, j)
                nc.vector.tensor_tensor(as_chunks(hst[k][:, 0:BC]), as_chunks(bank[4 + k][:, :]),
                                        to_rows(dis[:, blk(b)]), ALU.mult).then_inc(rows_ready[e], 1)

            with dve.Fori(0, NBODY) as i:
                for k in range(RING):
                    g = i * RING + k
                    dve.wait_ge(c_summed, g + 1)
                    if k % 2 == 0:
                        dve.wait_ge(src_rows_in[k // 2], i * 16 + 16)
                    for t in range(GT):
                        nc.vector.tensor_scalar(S[:, k % 2, t, 0:W], iota_w[:, :], rel[:, bass.ds(g * GT + t, 1)],
                                                wgt[:, bass.ds(g * GT + t, 1)], ALU.is_equal, ALU.mult)
                        at = (k % 2 * GT + t) * P
                        last = nc.vector.tensor_scalar(sel[k % 2][t], src_rows[k // 2][:, at:at + P],
                                                       src_f[:, bass.ds(g * GT + t, 1)], None, ALU.is_equal)
                    last.then_inc(sel_ready, 1)
                    dve.wait_ge(sel_ready, g + (RING + 1))
                    for t in range(GT):
                        last = nc.vector.tensor_tensor_reduce(
                            out=masked[k % 2][t], in0=sel[k % 2][t], in1=earlier[:, :], scale=1.0, scalar=0.0,
                            op0=ALU.mult, op1=ALU.add, accum_out=dup[:, k % 2, t:t + 1])
                    last.then_inc(dup_step, 1)
                    dve.wait_ge(dup_step, g * 3 + 1)
                    nc.vector.scalar_tensor_tensor(dup[:, k % 2, :], dup[:, k % 2, :], 1.0, to_spare[:, bass.ds(g * GT, GT)],
                                                   ALU.min, ALU.mult).then_inc(dup_step, 1)
                    dve.wait_ge(dup_step, g * 3 + 2)
                    dve.wait_ge(scatter_through, g + 1)
                    nc.vector.tensor_tensor(idx_ring[:, k, :], dup[:, k % 2, :], src_f[:, bass.ds(g * GT, GT)],
                                            ALU.add).then_inc(idx_ready[0], 1)
                    dve.sem_inc(dup_step, 1)
                    if k == 1:
                        dve.wait_ge(types_in, i * 16 + 16)
                        dve.wait_ge(alpha_summed, i + 1)
                        nc.vector.tensor_scalar(type_hot, type_rows, iota_p[0:R, 0:1], None,
                                                ALU.is_equal).then_inc(hot_ready, 1)
            with dve.If(flag != 0):
                for k in range(NTAB):
                    dve.wait_ge(scattered[k], (NG + 1) * 16)
                with dve.Fori(0, T) as t:
                    nc.vector.tensor_copy(slow_idx[:, 0:1], dst_i[:, bass.ds(t, 1)]).then_inc(slow_idx_ready, 1)
                    source = src_f[:, bass.ds(t, 1)]
                    nc.vector.tensor_scalar(masked[0][0], ident[:, :], source, None, ALU.mult).then_inc(slow0_ready, 1)
                    nc.vector.tensor_scalar(slow_w[:, 0:1], missed_dst[:, bass.ds(t, 1)], 0.0, wgt[:, bass.ds(t, 1)],
                                            ALU.is_ge, ALU.mult).then_inc(slow0_step, 1)
                    dve.wait_ge(slow0_summed, t * 2 + 1)
                    nc.vector.tensor_scalar(sel[0][0], bank[0][:, 0:P], source, None, ALU.is_equal).then_inc(slow0_step, 1)
                    dve.wait_ge(slow0_step, t * 5 + 2)
                    nc.vector.tensor_tensor_reduce(
                        out=masked[0][1], in0=sel[0][0], in1=earlier[:, :], scale=1.0, scalar=0.0,
                        op0=ALU.mult, op1=ALU.add, accum_out=slow_dup[:, 0:1]).then_inc(slow0_step, 1)
                    dve.wait_ge(slow0_step, t * 5 + 3)
                    nc.vector.scalar_tensor_tensor(slow_dup[:, 0:1], slow_dup[:, 0:1], 1.0, to_spare[:, bass.ds(t, 1)],
                                                   ALU.min, ALU.mult).then_inc(slow0_step, 1)
                    dve.wait_ge(slow0_step, t * 5 + 4)
                    nc.vector.tensor_tensor(slow_out_idx[:, 0:1], slow_dup[:, 0:1], source, ALU.add).then_inc(slow0_step, 1)
                    dve.wait_ge(slow0_gathered, t * 16 + 16)
                    nc.vector.tensor_scalar(rows[:, 0, 1, :], rows[:, 0, 0, :], slow_w[:, 0:1], None,
                                            ALU.mult).then_inc(slow0_ready, 1)
                    dve.wait_ge(slow0_summed, t * 2 + 2)
                    dve.wait_ge(slow0_step, t * 5 + 5)
                    nc.vector.tensor_copy(rows[:, 0, 2, :], bank[1][:, 0:P]).then_inc(slow0_rows, 1)
                    dve.wait_ge(slow0_scattered, t * 16 + 16)
            dve.wait_ge(x_in, 16 * 2)
            residual(0)
            finish_stats(0)
            over_blocks(dve, lambda b, k, j, more: norm(0, b, k, False))

            dve.wait_ge(alpha_ready, NBODY + 1)
            start_pass(1)
            with dve.Fori(0, NQ) as q:
                dve.wait_ge(G_zeroed, q * NPIECE + 1)
                apart(dve)
                with dve.Fori(0, QG // RING) as i:
                    sum_body(1, q * (QG // RING) + i)
                dve.wait_ge(added[1], q * QG + (QG + ADDED_AHEAD))
                dve.sem_inc(part_summed, 1)
                first = dve.value_load(base_i[0:1, bass.ds(q * QG, 1)], min_val=0, max_val=N)
                for j in range(NPIECE):
                    n = q * NPIECE + j
                    dve.wait_ge(based, n + 1)
                    dve.wait_ge(based_added, n + 2)
                    to = acc[:, bass.ds(first + j * PIECE, PIECE)]
                    nc.vector.tensor_tensor(to, to, bank[4 + j % 2][:, 0:PIECE], ALU.add).then_inc(based_added, 1)
            dve.wait_ge(based_added, NQ * NPIECE + 2)
            finish_pass(1)
            residual(1)
            finish_stats(1)
            dve.wait_ge(G_zeroed, NQ * NPIECE + 1)

            def stage1(b, k, j, more):
                if more:
                    norm(1, b + 1, 1 - k, True)
                dve.wait_ge(projected[1], b + 3)
                slot_stored(1, k, j)
                for h in range(2):
                    last = nc.vector.tensor_tensor(
                        hst[k][:, h * BC:(h + 1) * BC].rearrange("p (c f) -> p c f", c=2),
                        bank[4 + h][:, :].rearrange("p (c f) -> p c f", c=2),
                        bdc_bc[:, :].unsqueeze(1).to_broadcast([P, 2, 2 * P]), ALU.add)
                last.then_inc(rows_ready[1], 1)
            norm(1, 0, 0, True)
            over_blocks(dve, stage1)

            dve.wait_ge(acc_set[1], NBLK + 2)
            start_pass(2)
            with dve.Fori(0, NBODY) as i:
                sum_body(2, i)
            finish_pass(2)
            dve.wait_ge(kept[1], NBLK + 2)
            residual(2)
            dve.wait_ge(sqrt_ready, 1)
            nc.vector.reciprocal(dis[:, :], deg_std[:, :]).then_inc(deg_ready, 1)
            dve.wait_ge(deg_ready, 1)
            finish_stats(2)

            def stage2(b, k, j, more):
                if more:
                    norm(2, b + 1, 1 - k, True)
                scale_rows(2, b, k, j)
            norm(2, 0, 0, True)
            over_blocks(dve, stage2)

            dve.wait_ge(acc_set[2], NBLK + 2)
            start_pass(3)
            with dve.Fori(0, NBODY) as i:
                sum_body(3, i)
            finish_pass(3)
            dve.wait_ge(kept[2], NBLK + 2)

            def stage3(b, k, j, more):
                dve.wait_ge(turned[3], b + 3)
                dve.wait_ge(rowsT[3], b + 1)
                nc.vector.tensor_tensor(as_chunks(xn[k]), as_chunks(bank[k][:, :]), to_rows(dis[:, blk(b)]),
                                        ALU.mult).then_inc(scaled, 1)
                dve.wait_ge(scaled, b + 3)
                nc.vector.tensor_tensor(as_chunks(xn[k]), as_chunks(xn[k]),
                                        b1_bc[:, :].unsqueeze(1).to_broadcast([P, BLK, P]), ALU.add).then_inc(biased, 1)
                scale_rows(3, b, k, j)
            over_blocks(dve, stage3)

            dve.wait_ge(acc_set[3], NBLK + 2)
            start_pass(4)
            with dve.Fori(0, NBODY) as i:
                sum_body(4, i)
            finish_pass(4)
            residual(4)
            finish_stats(4)
            over_blocks(dve, lambda b, k, j, more: norm(4, b, k, False))


def kernel(x, src, dst, edge_type_2, edge_type_64, edge_weight, L0_gnn_kernel, L0_gnn_bias, L1_gnn_bases,
           L1_gnn_relation_base_weights, L2_gnn_W_data, L2_gnn_b_data, L2_gnn_W_control, L2_gnn_b_control,
           L2_gnn_W_self, L2_gnn_b_self, L3_gnn_W1, L3_gnn_b1, L3_gnn_W2, L3_gnn_b2):
    from concourse import bacc
    from concourse.bass_utils import run_bass_kernel_spmd

    def tiles(a, columns, pad):
        a = np.asarray(a)
        filled = np.concatenate([a, np.full(columns * P - E, pad, a.dtype)])
        return np.ascontiguousarray(filled.reshape(columns, P).T)

    def row(*parts):
        return np.ascontiguousarray(np.concatenate([np.asarray(a) for a in parts])[None, :])

    def turned(*parts):
        return np.ascontiguousarray(np.concatenate([np.asarray(a).T for a in parts], axis=1))

    arrays = {
        "src": tiles(src, TX, 0),
        "src_row": row(src, np.zeros(T * P - E, np.asarray(src).dtype)),
        "dst": tiles(dst, T, N),
        "type2": tiles(edge_type_2, TX, 0),
        "type64": row(edge_type_64, np.zeros(T * P - E, np.asarray(edge_type_64).dtype)),
        "weight": tiles(edge_weight, TX, 0),
        "x": np.concatenate([np.asarray(x), np.zeros((W, P), np.asarray(x).dtype)]),
        "k0": np.ascontiguousarray(L0_gnn_kernel),
        "bias0": row(L0_gnn_bias),
        "bases": np.ascontiguousarray(L1_gnn_bases),
        "rel_weights": np.ascontiguousarray(L1_gnn_relation_base_weights),
        "w_data_ctrl": turned(L2_gnn_W_data, L2_gnn_W_control),
        "b_data_ctrl": row(L2_gnn_b_data, L2_gnn_b_control),
        "w_self": turned(L2_gnn_W_self),
        "b_self": np.ascontiguousarray(np.asarray(L2_gnn_b_self)[:, None]),
        "w1": turned(L3_gnn_W1),
        "b1": row(L3_gnn_b1),
        "w2": turned(L3_gnn_W2),
        "b2": row(L3_gnn_b2),
    }
    nc = bacc.Bacc("TRN2", target_bir_lowering=False, num_devices=1)
    args = {n: nc.dram_tensor(n, a.shape, mybir.dt.from_np(a.dtype), kind="ExternalInput").ap() for n, a in arrays.items()}
    args["out"] = nc.dram_tensor("out", (N, P), FP, kind="ExternalOutput").ap()
    gnn_program(nc, **args)
    r = run_bass_kernel_spmd(nc, [arrays], core_ids=[0])
    return r.results[0]["out"]
```

```python
import numpy as np

import concourse.bass as bass
from concourse import mybir

FP = mybir.dt.float32
I32 = mybir.dt.int32
ALU = mybir.AluOpType
ACT = mybir.ActivationFunctionType

P = 128
N = 6250
E = 106250
NB = 8
R = 64
GT = 2
RING = 8
BODY = GT * RING
FT = 4
FSTEPS = BODY // FT
FHALF = FT // GT
T = -(-E // (P * BODY)) * BODY
TX = T + BODY
NG = T // GT
NBODY = NG // RING
W = 24
PIECE = 272
NPIECE = 2
CAP = PIECE * NPIECE
BLK = 4
NBLK = -(-N // (BLK * P))
BC = BLK * P
NC = NBLK * BLK
BPP = NBODY // NBLK
GPP = NG // NBLK
LAST = N - (NBLK - 1) * BC
ACC = N + CAP
NWIN = -(-(N + 1) // W)
EPS = 1e-5
NTAB = FT
TABR = NBLK * BLK * P
PASSES = 5
PRODUCTS_AHEAD = RING
ADDED_AHEAD = 2
STEPS = BODY * BPP // (2 * GT)
TURN, RESIDUAL, NORM, TURN_ROWS, PROJECT, TABLE, LOOPS = 5, 6, 7, 8, 10, 11, 12
CHUNKS = (BLK, 1)
AX_X = mybir.AxisListType.X
assert NBODY == BPP * NBLK and LAST < P and ACC >= NWIN * W and ACC >= TABR >= N + P


def gnn_program(nc, src, src_row, dst, type2, type64, weight, x, k0, bias0, bases, rel_weights,
                w_data_ctrl, b_data_ctrl, w_self, b_self, w1, b1, w2, b2, out):
    from contextlib import ExitStack

    ctx = ExitStack()
    with ctx:
        def sb(name, shape, dt=FP):
            return ctx.enter_context(nc.sbuf_tensor(name, shape, dt))

        def sem(name):
            return ctx.enter_context(nc.semaphore(name))

        t1 = nc.dram_tensor("t1", (N, P), FP, kind="Internal").ap()
        t2 = nc.dram_tensor("t2", (2 * N, P), FP, kind="Internal").ap()
        t3 = nc.dram_tensor("t3", (N, P), FP, kind="Internal").ap()
        t4 = nc.dram_tensor("t4", (N, P), FP, kind="Internal").ap()
        tables = [x, t1, t2, t3, t4]
        sums_t = [nc.dram_tensor(f"sums{k}", (TABR, P), FP, kind="Internal").ap() for k in range(NTAB)]

        src_i = sb("src_i", [P, TX], I32)
        src2_i = sb("src2_i", [P, TX], I32)
        wgt = sb("wgt", [P, TX])
        dst_f = sb("dst_f", [P, T])
        rel = sb("rel", [P, TX])
        missed_dst = sb("missed_dst", [P, T])
        alpha = sb("alpha", [P, TX * NB])
        base_bc = sb("base_bc", [P, NG])
        off_bc = sb("off_bc", [P, NG])
        base_i = sb("base_i", [1, NG], I32)
        off_i = sb("off_i", [1, NG], I32)
        part_at = sb("part_at", [1, NBLK])
        part_i = sb("part_i", [1, NBLK], I32)
        missed_any = sb("missed_any", [P, 1])
        flag_i = sb("flag_i", [1, 1], I32)

        xcur = sb("xcur", [P, NC, P])
        acc = sb("acc", [P, ACC])
        dis = sb("dis", [P, NC])
        mv = sb("mv", [P, NC, 2])
        std = sb("std", [P, NC])
        rstd = sb("rstd", [P, NC])
        bst = sb("bst", [P, BLK, 6])
        mvs = sb("mvs", [P, BLK, 2])
        moments_of = sb("moments_of", [P, 2, BLK, 2])
        dev_of = sb("dev_of", [P, 2, BLK])
        inv_of = sb("inv_of", [P, 2, BLK])
        deg_dev = sb("deg_dev", [P, 2, BLK])

        rows = sb("rows", [P, RING, GT, P])
        idx_ring = sb("idx_ring", [P, RING, GT], I32)
        S = sb("S", [P, 2, GT, NB * W])
        S01 = sb("S01", [P, 2, GT, W])
        rows4 = rows[:, :, :, :].rearrange("p (s h) t f -> p s (h t) f", h=FHALF)
        first = sb("first", [P, 2, FT, W + 2 * P])
        wS = [[first[:, s, t, 0:W] for t in range(FT)] for s in range(2)]
        sel = [[first[:, s, t, W:W + P] for t in range(FT)] for s in range(2)]
        masked = [[first[:, s, t, W + P:W + 2 * P] for t in range(FT)] for s in range(2)]
        msg = [rows4[:, s, :, :] for s in range(2)]
        xwin = [[rows4[0:W, 2 + h, k, :] for h in range(FHALF)] for k in range(FSTEPS)]
        dup = sb("dup", [P, 2, FT])
        tab_rows = [rows[:, :, :, :].rearrange("p k c f -> p (k c f)"),
                    first[:, :, :, :].rearrange("p s t w -> p (s t w)")[:, 0:NTAB * BC]]
        idx4 = idx_ring[:, :, :].rearrange("p (s h) t -> p s (h t)", h=FHALF)

        TW = BODY * P
        NG_COLS = 2 * NB * CAP
        arena = sb("arena", [P, 2 * TW + 8 * TX + TW + 2 * BC])
        G = arena[:, 0:NG_COLS].rearrange("p (b c) -> p b c", b=NB)
        type_rows = arena[0:R, 0:TW].bitcast(I32)
        type_hot = arena[0:R, TW:2 * TW]
        dst_i = arena[:, 2 * TW:2 * TW + T].bitcast(I32)
        type2_i = arena[:, 2 * TW + TX:2 * TW + 2 * TX].bitcast(I32)
        ok = arena[:, 2 * TW + 2 * TX:2 * TW + 2 * TX + T]
        ok2 = arena[:, 2 * TW + 3 * TX:2 * TW + 3 * TX + T]
        off_ok = arena[:, 2 * TW + 4 * TX:2 * TW + 4 * TX + NG]
        off_ok2 = arena[:, 2 * TW + 5 * TX:2 * TW + 5 * TX + NG]
        src_f = arena[:, 2 * TW + 6 * TX:2 * TW + 6 * TX + T]
        to_spare = arena[:, 2 * TW + 7 * TX:2 * TW + 7 * TX + T]
        HW = TW // 2
        h0 = 2 * TW + 8 * TX
        src_rows = [arena[:, h0 + s * HW:h0 + (s + 1) * HW].bitcast(I32) for s in range(2)]
        C = [arena[0:W, h0 + 2 * HW + s * BC:h0 + 2 * HW + (s + 1) * BC] for s in range(2)]
        assert h0 + 2 * HW + 2 * BC == arena.shape[1]
        cnt = arena[0:1, 0:NBLK * BC]
        a0 = max(NG_COLS, NBLK * BC)

        def scratch(n):
            nonlocal a0
            a0 += n
            return arena[:, a0 - n:a0]

        xn = [scratch(c * P) for c in CHUNKS]
        xT = [scratch(c * P) for c in CHUNKS]
        hst = [scratch(2 * c * P) for c in CHUNKS]
        cnt_blk = [scratch(c * P)[0:1, :] for c in CHUNKS]
        assert a0 <= arena.shape[1]
        stage = [sb(f"stage{k}", [P, BC]) for k in range(2)]

        k0_sb = sb("k0_sb", [P, P])
        bias0_row = sb("bias0_row", [1, P])
        bases_sb = sb("bases_sb", [P, NB, P])
        relw_sb = sb("relw_sb", [R, NB])
        wdc_sb = sb("wdc_sb", [P, 2 * P])
        bdc_bc = sb("bdc_bc", [P, 2 * P])
        ws_sb = sb("ws_sb", [P, P])
        bs_sb = sb("bs_sb", [P, 1])
        w1_sb = sb("w1_sb", [P, P])
        b1_bc = sb("b1_bc", [P, P])
        w2_sb = sb("w2_sb", [P, P])
        b2_bc = sb("b2_bc", [P, P])
        ident = sb("ident", [P, P])
        first_row = sb("first_row", [P, P])
        ones = sb("ones", [P, P])
        zeros = sb("zeros", [P, PIECE])
        iota_w = sb("iota_w", [P, W])
        iota_p = sb("iota_p", [P, 1])
        spare_row = sb("spare_row", [P, 1])
        earlier = sb("earlier", [P, P])
        slow_out_idx = sb("slow_out_idx", [P, 1], I32)
        slow_w = sb("slow_w", [P, 1])
        slow_dup = sb("slow_dup", [P, 1])
        eps_sb = sb("eps_sb", [P, 1])
        slow_idx = sb("slow_idx", [P, 1], I32)
        slow_rel = sb("slow_rel", [P, 1])
        slow_win = sb("slow_win", [P, 1])
        slow_G = sb("slow_G", [P, NB * W])

        bank = [ctx.enter_context(nc.psum_tensor(f"bank{k}", [P, 512], FP)) for k in range(8)]

        edges_in = sem("edges_in")
        src_in = sem("src_in")
        weights_in = sem("weights_in")
        x_in = sem("x_in")
        consts_set = sem("consts_set")
        const_step = sem("const_step")
        acc_zeroed = sem("acc_zeroed")
        xpad_zeroed = sem("xpad_zeroed")
        prep = sem("prep")
        dst_ready = sem("dst_ready")
        base_summed = sem("base_summed")
        missed_ready = sem("missed_ready")
        missed_summed = sem("missed_summed")
        flag_ready = sem("flag_ready")
        types_in = sem("types_in")
        hot_ready = sem("hot_ready")
        alpha_summed = sem("alpha_summed")
        alpha_ready = sem("alpha_ready")

        idx_ready = [sem(f"idx_ready{p}") for p in range(PASSES)]
        gathered = [sem(f"gathered{k}") for k in range(RING)]
        s01_ready = sem("s01_ready")
        s_ready = [sem(f"s_ready{p}") for p in range(PASSES)]
        products = [sem(f"products{p}") for p in range(PASSES)]
        added = [sem(f"added{p}") for p in range(PASSES)]
        counted = sem("counted")
        src_rows_in = [sem(f"src_rows_in{k}") for k in range(2)]
        xwin_in = [sem(f"xwin_in{k}") for k in range(FSTEPS)]
        sel_ready = sem("sel_ready")
        dup_step = sem("dup_step")
        c_summed = sem("c_summed")
        c_kept = sem("c_kept")
        messages = sem("messages")
        msg_kept = sem("msg_kept")
        scattered = [sem(f"scattered{k}") for k in range(NTAB)]
        scatter_through = sem("scatter_through")
        tables_done = sem("tables_done")
        tab_in = [sem(f"tab_in{k}") for k in range(2)]
        tab_turned = sem("tab_turned")
        slow0_ready = sem("slow0_ready")
        slow0_summed = sem("slow0_summed")
        slow0_step = sem("slow0_step")
        slow0_rows = sem("slow0_rows")
        slow0_scattered = sem("slow0_scattered")
        based = sem("based")
        based_added = sem("based_added")
        G_zeroed = sem("G_zeroed")

        slow_idx_ready = sem("slow_idx_ready")
        slow0_gathered = sem("slow0_gathered")
        slow_gathered = sem("slow_gathered")
        slow_step = sem("slow_step")
        slow_s = sem("slow_s")
        slow_s01 = sem("slow_s01")
        slow_counted = sem("slow_counted")
        slow_products = sem("slow_products")
        slow_moved = sem("slow_moved")
        slow_based = sem("slow_based")

        LAYERS = range(5)
        NORMED = (0, 1, 2, 4)
        NTH = {e: n for n, e in enumerate(NORMED)}

        def sems(name, stages):
            return {e: sem(f"{name}{e}") for e in stages}

        staged = sems("staged", LAYERS)
        turned = sems("turned", LAYERS)
        summed = sems("summed", NORMED)
        stats = sem("stats")
        all_stats = sem("all_stats")
        std_ready = sem("std_ready")
        rstd_ready = sem("rstd_ready")
        moments = sem("moments")
        dev_ready = sem("dev_ready")
        inv_ready = sem("inv_ready")
        normed = sems("normed", LAYERS)
        kept = sems("kept", (1, 2))
        rowsT = sems("rowsT", (1, 2, 3))
        rowsT_kept = sems("rowsT_kept", (1, 2, 3))
        projected = sems("projected", (1, 2, 3))
        selfed = sem("selfed")
        rows_ready = sems("rows_ready", (1, 2, 3))
        stored0 = sem("stored0")
        stored = sems("stored", (1, 2, 3))
        loop_turned = sems("loop_turned", (2, 3))
        acc_set = sems("acc_set", (1, 2, 3))
        scaled = sem("scaled")
        biased = sem("biased")
        deg_ready = sem("deg_ready")
        cnt_staged = sem("cnt_staged")
        deg_turned = sem("deg_turned")
        sqrt_ready = sem("sqrt_ready")
        out_stored = sem("out_stored")
        summed_scale = sem("summed_scale")

        waits_passed = sem("waits_passed")
        block = ctx.enter_context(nc.Block())

        def apart(eng):
            eng.sem_inc(waits_passed, 1)

        PAIRS = (NBLK - 1) // 2
        assert NBLK % 2 == 1

        def over_blocks(eng, step):
            step(0, 0, 0, True)
            step(1, 1, 0, True)
            with eng.Fori(1, PAIRS) as j:
                step(j * 2, 0, j, True)
                step(j * 2 + 1, 1, j, True)
            step(NBLK - 1, 0, PAIRS, False)

        def in_steps(eng, stage_step):
            with eng.Fori(0, NBLK - 2) as b:
                for at in range(STEPS):
                    stage_step(b, 0, at)
            for at in range(STEPS):
                stage_step(NBLK - 2, 0, at)
                stage_step(NBLK - 1, 1, at)

        def sums_whole(eng, p, b):
            if p == 1:
                eng.wait_ge(based_added, NPIECE * NBLK + 1 if isinstance(b, int) else b * NPIECE + (2 * NPIECE + 1))
            else:
                eng.wait_ge(added[p], NG + ADDED_AHEAD if isinstance(b, int) else b * GPP + (2 * GPP + ADDED_AHEAD))

        def moment_steps(e):
            return (NTH[e] - 1) * NBLK

        def count_at(k):
            return bank[k % 2][0:1, BC - W:BC]

        def node_rows(table, b):
            return table[bass.ds(b * BC, BC), :].rearrange("(c p) f -> p c f", p=P)

        t2_pairs = t2.rearrange("(n t) f -> n (t f)", t=2)

        @block.sync
        def _(sp):
            for e in (1, 2, 3):
                sp.sem_inc(stored[e], 16)
            sp.dma_start(src_i[:, :], src).then_inc(src_in, 16)
            sp.dma_start(dst_i, dst).then_inc(edges_in, 16)
            sp.dma_start(wgt[:, :], weight).then_inc(edges_in, 16)
            sp.dma_start(type2_i, type2).then_inc(edges_in, 16)
            sp.dma_start(relw_sb[:, :], rel_weights).then_inc(weights_in, 16)
            sp.dma_start(k0_sb[:, :], k0).then_inc(weights_in, 16)
            sp.dma_start(bases_sb[:, :, :], bases.rearrange("b f o -> f b o")).then_inc(weights_in, 16)
            sp.dma_start(wdc_sb[:, :], w_data_ctrl).then_inc(weights_in, 16)
            sp.dma_start(ws_sb[:, :], w_self).then_inc(weights_in, 16)
            sp.dma_start(w1_sb[:, :], w1).then_inc(weights_in, 16)
            sp.dma_start(w2_sb[:, :], w2).then_inc(weights_in, 16)
            sp.dma_start(bs_sb[:, :], b_self).then_inc(weights_in, 16)
            sp.dma_start(bias0_row[:, :], bias0).then_inc(weights_in, 16)
            sp.dma_start(bdc_bc[:, :], b_data_ctrl.to_broadcast([P, 2 * P])).then_inc(weights_in, 16)
            sp.dma_start(b1_bc[:, :], b1.to_broadcast([P, P])).then_inc(weights_in, 16)
            sp.dma_start(b2_bc[:, :], b2.to_broadcast([P, P])).then_inc(weights_in, 16)
            sp.wait_ge(xpad_zeroed, 1)
            sp.dma_start(xcur[:, 0:NC - BLK, :],
                         x[0:(NBLK - 1) * BC, :].rearrange("(c p) f -> p c f", p=P)).then_inc(x_in, 16)
            sp.dma_start(xcur[0:LAST, NC - BLK, :], x[(NBLK - 1) * BC:N, :]).then_inc(x_in, 16)

            sp.wait_ge(flag_ready, 1)
            with sp.Fori(0, NBODY) as i:
                sp.wait_ge(hot_ready, i + 1)
                sp.dma_start(type_rows, type64[0:1, bass.ds(i * TW, TW)].to_broadcast([R, TW])
                             ).then_inc(types_in, 16)
                for h in range(2):
                    sp.wait_ge(sel_ready, i * FSTEPS + 2 * h + 2)
                    sp.dma_start(src_rows[h], src_row[0:1, bass.ds(i * TW + h * HW, HW)].to_broadcast([P, HW])
                                 ).then_inc(src_rows_in[h], 16)
                    for k in (2 * h, 2 * h + 1):
                        for w in range(FHALF):
                            base = sp.value_load(base_i[0:1, bass.ds(i * RING + (k * FHALF + w), 1)], min_val=0, max_val=N)
                            if w == 0:
                                sp.wait_ge(messages, i * FSTEPS + k + 1)
                            sp.dma_start(xwin[k][w], x[bass.ds(base, W), :]).then_inc(xwin_in[k], 16)

            sp.wait_ge(tables_done, 1)
            def load_tables(b, k, j, more):
                sp.wait_ge(tab_turned, b + 1)
                for n in range(NTAB):
                    sp.dma_start(tab_rows[k][:, n * BC:(n + 1) * BC].rearrange("p (c f) -> p c f", c=BLK),
                                 node_rows(sums_t[n], b)).then_inc(tab_in[k], 16)
            over_blocks(sp, load_tables)

            def store_x1(b, k, j, more):
                sp.wait_ge(normed[0], b + 1)
                if more:
                    sp.dma_start(node_rows(t1, b), xcur[:, bass.ds(b * BLK, BLK), :]).then_inc(stored0, 16)
                else:
                    sp.dma_start(t1[b * BC:N, :], xcur[0:LAST, b * BLK, :]).then_inc(stored0, 16)
            over_blocks(sp, store_x1)

            for e, table, width in ((1, t2_pairs, 2 * P), (2, t3, P), (3, t4, P)):
                with sp.Fori(0, NBLK - 1) as b:
                    sp.wait_ge(rows_ready[e], b + 2)
                    sp.dma_start(node_rows(table, b), hst[0][:, 0:BLK * width].rearrange(
                        "p (c f) -> p c f", c=BLK)).then_inc(stored[e], 16)
                sp.wait_ge(rows_ready[e], NBLK + 1)
                sp.dma_start(table[(NBLK - 1) * BC:N, :], hst[1][0:LAST, 0:width]).then_inc(stored[e], 16)

            def store_out(b, k, j, more):
                sp.wait_ge(normed[4], b + 1)
                if more:
                    sp.dma_start(node_rows(out, b), xcur[:, bass.ds(b * BLK, BLK), :]).then_inc(out_stored, 16)
                else:
                    sp.dma_start(out[b * BC:N, :], xcur[0:LAST, b * BLK, :]).then_inc(out_stored, 16)
            over_blocks(sp, store_out)
            sp.wait_ge(out_stored, 16 * NBLK)

        @block.gpsimd
        def _(pool):
            nc.gpsimd.memset(ones[:, :], 1.0).then_inc(const_step, 1)
            nc.gpsimd.memset(xcur[:, NC - BLK:NC, :], 0.0).then_inc(xpad_zeroed, 1)
            nc.gpsimd.memset(zeros[:, :], 0.0).then_inc(consts_set, 1)
            nc.gpsimd.memset(eps_sb[:, :], EPS).then_inc(consts_set, 1)
            nc.gpsimd.iota(iota_w[:, :], [[1, W]], base=0, channel_multiplier=0,
                           allow_small_or_imprecise_dtypes=True).then_inc(consts_set, 1)
            nc.gpsimd.iota(iota_p[:, :], [[0, 1]], base=0, channel_multiplier=1,
                           allow_small_or_imprecise_dtypes=True).then_inc(consts_set, 1)
            pool.wait_ge(const_step, 1)
            nc.gpsimd.affine_select(out=ident[:, :], in_=ones[:, :], compare_op=ALU.is_equal, fill=0.0,
                                    base=0, pattern=[[-1, P]], channel_multiplier=1).then_inc(consts_set, 1)
            nc.gpsimd.affine_select(out=first_row[:, :], in_=ones[:, :], compare_op=ALU.is_equal, fill=0.0,
                                    base=0, pattern=[[0, P]], channel_multiplier=1).then_inc(consts_set, 1)
            nc.gpsimd.affine_select(out=earlier[:, :], in_=ones[:, :], compare_op=ALU.is_ge, fill=0.0,
                                    base=-1, pattern=[[-1, P]], channel_multiplier=1).then_inc(consts_set, 1)
            nc.gpsimd.iota(spare_row[:, :], [[0, 1]], base=N, channel_multiplier=1,
                           allow_small_or_imprecise_dtypes=True).then_inc(consts_set, 1)

            def gather_pass(p):
                with pool.Fori(0, NBODY) as i:
                    for k in range(RING):
                        g = i * RING + k
                        pool.wait_ge(idx_ready[p], g + 1)
                        pool.wait_ge(products[p], g + 1)
                        apart(pool)
                        for t in range(GT):
                            nc.gpsimd.indirect_dma_start(
                                out=rows[:, k, t, :], out_offset=None, in_=tables[p],
                                in_offset=bass.IndirectOffsetOnAxis(ap=idx_ring[:, k, t:t + 1], axis=0),
                            ).then_inc(gathered[k], 16)

            def gather_general(p, flag):
                with pool.If(flag != 0):
                    with pool.Fori(0, T) as t:
                        pool.wait_ge(slow_idx_ready, t + (p * T + 1))
                        apart(pool)
                        nc.gpsimd.indirect_dma_start(
                            out=rows[:, 0, 0, :], out_offset=None, in_=tables[p],
                            in_offset=bass.IndirectOffsetOnAxis(ap=slow_idx[:, 0:1], axis=0),
                        ).then_inc(slow_gathered, 16)

            pool.sem_inc(scatter_through, 3)
            pool.wait_ge(acc_zeroed, 1)
            for t in range(NTAB):
                pool.dma_start(sums_t[t].rearrange("(p r) f -> p (r f)", p=P), acc[:, 0:TABR]).then_inc(scattered[t], 16)
            with pool.Fori(0, NBODY) as i:
                for k in range(FSTEPS):
                    g = i * FSTEPS + k
                    pool.wait_ge(idx_ready[0], g + 1)
                    pool.wait_ge(msg_kept, g + 3)
                    for t in range(NTAB):
                        pool.wait_ge(scattered[t], g * 16 + 16)
                        apart(pool)
                        if t == NTAB - 1:
                            pool.sem_inc(scatter_through, 1)
                        nc.gpsimd.indirect_dma_start(
                            out=sums_t[t], out_offset=bass.IndirectOffsetOnAxis(ap=idx4[:, k, t:t + 1], axis=0),
                            in_=msg[k % 2][:, t, :], in_offset=None, compute_op=ALU.add).then_inc(scattered[t], 16)
            for t in range(NTAB):
                pool.wait_ge(scattered[t], (T // FT + 1) * 16)
            flag = pool.value_load(flag_i[0:1, 0:1], min_val=0, max_val=1)
            with pool.If(flag != 0):
                with pool.Fori(0, T) as t:
                    pool.wait_ge(slow_idx_ready, t + 1)
                    apart(pool)
                    nc.gpsimd.indirect_dma_start(
                        out=rows[:, 0, 0, :], out_offset=None, in_=tables[0],
                        in_offset=bass.IndirectOffsetOnAxis(ap=slow_idx[:, 0:1], axis=0),
                    ).then_inc(slow0_gathered, 16)
                    pool.wait_ge(slow0_rows, t + 1)
                    apart(pool)
                    nc.gpsimd.indirect_dma_start(
                        out=sums_t[0], out_offset=bass.IndirectOffsetOnAxis(ap=slow_out_idx[:, 0:1], axis=0),
                        in_=rows4[:, 0, 2, :], in_offset=None, compute_op=ALU.add).then_inc(slow0_scattered, 16)
                pool.wait_ge(slow0_scattered, 16 * T)
            pool.sem_inc(tables_done, 1)

            pool.wait_ge(alpha_summed, NBODY + 1)
            nc.gpsimd.memset(arena[:, 0:NG_COLS], 0.0).then_inc(G_zeroed, 1)

            for p in range(1, PASSES):
                if p == 1:
                    pool.wait_ge(stored0, 16 * NBLK)
                else:
                    pool.wait_ge(stored[p - 1], 16 * (NBLK + 1))
                gather_general(p, flag)
                gather_pass(p)

        @block.scalar
        def _(act):
            act.sem_inc(alpha_ready, 1)
            act.sem_inc(staged[0], 2)
            act.sem_inc(sqrt_ready, 1)
            for e in (1, 2, 3):
                act.sem_inc(rowsT_kept[e], 1)
                act.sem_inc(acc_set[e], 1)

            act.sem_inc(c_kept, 2)
            act.sem_inc(msg_kept, 2)
            def keep_window(i, k):
                act.wait_ge(c_summed, i * FSTEPS + (k + 3))
                act.wait_ge(messages, i * FSTEPS + (k + 3))
                nc.scalar.activation(C[k % 2], bank[k % 2][0:W, :], ACT.Copy).then_inc(c_kept, 1)

            def keep_rows(i, k):
                act.wait_ge(messages, i * FSTEPS + (k + 5))
                act.wait_ge(scatter_through, i * FSTEPS + (k + 3))
                nc.scalar.activation(msg[k % 2].rearrange("p t f -> p (t f)"), bank[4 + k % 2][:, :],
                                     ACT.Copy).then_inc(msg_kept, 1)

            with act.Fori(0, NBODY) as i:
                keep_window(i, 0)
                for k in range(FSTEPS - 1):
                    keep_window(i, k + 1)
                    keep_rows(i, k)
                keep_rows(i, FSTEPS - 1)
                act.wait_ge(alpha_summed, i + 2)
                apart(act)
                nc.scalar.activation(alpha[:, bass.ds(i * BODY * NB, BODY * NB)], bank[2][:, 0:BODY * NB],
                                     ACT.Copy).then_inc(alpha_ready, 1)

            act.wait_ge(consts_set, 8)
            act.wait_ge(weights_in, 16 * 12)

            def take_tables(b, k, j, more):
                act.wait_ge(tab_turned, b + 3)
                act.wait_ge(turned[0], b + 1)
                nc.scalar.activation(stage[k][:, :], bank[2 + k][:, :], ACT.Copy).then_inc(staged[0], 1)
            over_blocks(act, take_tables)
            act.wait_ge(all_stats, 1)
            nc.scalar.activation(std[:, :], mv[:, :, 1], ACT.Sqrt, bias=eps_sb[:, 0:1]).then_inc(std_ready, 1)

            def zero_part(q):
                for j in range(NPIECE):
                    at = act.value_load(part_i[0:1, bass.ds(q, 1)], min_val=0, max_val=CAP)
                    act.wait_ge(based, q * NPIECE + (j + 1))
                    apart(act)
                    nc.scalar.activation(G[:, :, bass.ds(at + j * PIECE, PIECE)],
                                         zeros[:, :].unsqueeze(1).to_broadcast([P, NB, PIECE]),
                                         ACT.Copy).then_inc(G_zeroed, 1)

            def to_acc(b, k, rows_in, func, **more):
                return nc.scalar.activation(acc[:, bass.ds(b * BC, CHUNKS[k] * P)], rows_in[:, 0:CHUNKS[k] * P], func, **more)

            def stage_step(e, b, k, at):
                n = CHUNKS[k]
                if at == TURN:
                    sums_whole(act, e, b)
                    act.wait_ge(turned[e], b + 1)
                    apart(act)
                    nc.scalar.activation(stage[0][:, 0:n * P], acc[:, bass.ds(b * BC, n * P)],
                                         ACT.Relu if e == 2 else ACT.Copy).then_inc(staged[e], 1)
                    if e == 2:
                        nc.scalar.activation(cnt_blk[k], cnt[:, bass.ds(b * BC, n * P)], ACT.Copy).then_inc(cnt_staged, 1)
                elif at == RESIDUAL and e == 2:
                    act.wait_ge(deg_turned, b + 1)
                    apart(act)
                    nc.scalar.activation(deg_dev[:, k, 0:n], bank[5][:, 0:n], ACT.Sqrt, bias=ones[:, 0:1]).then_inc(sqrt_ready, 1)
                elif at == NORM and e == 3:
                    act.wait_ge(biased, b + 1)
                    nc.scalar.activation(xn[k], xn[k], ACT.Relu).then_inc(normed[3], 1)
                elif at == NORM:
                    act.wait_ge(moments, b * 2 + (2 * moment_steps(e) + 2))
                    apart(act)
                    nc.scalar.activation(dev_of[:, k, 0:n], moments_of[:, k, 0:n, 1], ACT.Sqrt,
                                         bias=eps_sb[:, 0:1]).then_inc(dev_ready, 1)
                elif at == TURN_ROWS and e != 4:
                    act.wait_ge(rowsT[e], b + 2)
                    act.wait_ge(projected[e], b + 1)
                    nc.scalar.activation(xT[k], bank[3][:, 0:n * P], ACT.Copy).then_inc(rowsT_kept[e], 1)
                    if e == 1:
                        act.wait_ge(normed[1], b + 1)
                        apart(act)
                        nc.scalar.activation(xcur[:, bass.ds(b * BLK, n), :], xn[k].rearrange("p (c f) -> p c f", c=n),
                                             ACT.Copy).then_inc(kept[1], 1)
                elif at == PROJECT and e == 1:
                    act.wait_ge(selfed, b + 1)
                    apart(act)
                    to_acc(b, k, bank[6], ACT.Identity, bias=bs_sb[:, 0:1]).then_inc(acc_set[1], 1)
                elif at == LOOPS and e in (2, 3):
                    act.wait_ge(loop_turned[e], b + 2)
                    apart(act)
                    to_acc(b, k, bank[6], ACT.Copy).then_inc(acc_set[e], 1)

            def stage1(b, k, at):
                if at == 0 and not isinstance(b, int):
                    zero_part(b + 1)
                elif at == 0 and k == 0:
                    zero_part(NBLK - 1)
                stage_step(1, b, k, at)
            zero_part(0)
            in_steps(act, stage1)
            in_steps(act, lambda b, k, at: stage_step(2, b, k, at))
            in_steps(act, lambda b, k, at: stage_step(3, b, k, at))
            in_steps(act, lambda b, k, at: stage_step(4, b, k, at))

        @block.tensor
        def _(pe):
            for p in range(1, PASSES):
                pe.sem_inc(products[p], PRODUCTS_AHEAD)
            pe.sem_inc(alpha_summed, 1)
            pe.sem_inc(c_summed, 2)
            pe.sem_inc(messages, FSTEPS)
            pe.sem_inc(tab_turned, 2)
            for e in LAYERS:
                pe.sem_inc(turned[e], 1 if e else 2)
            for e in (1, 2, 3):
                pe.sem_inc(projected[e], 1)
                pe.sem_inc(rowsT[e], 1)
            for e in (2, 3):
                pe.sem_inc(loop_turned[e], 1)
            pe.wait_ge(consts_set, 8)
            pe.wait_ge(dst_ready, 1)
            nc.tensor.matmul(bank[0][:, 0:NG], first_row[:, :], dst_f[:, 0:T:GT], start=True,
                             stop=True).then_inc(base_summed, 1)
            pe.wait_ge(missed_ready, 1)
            nc.tensor.matmul(bank[0][0:1, 0:1], missed_any[:, 0:1], ones[:, 0:1], start=True,
                             stop=True).then_inc(missed_summed, 1)
            pe.wait_ge(weights_in, 16 * 12)

            def group_products(p, i, k):
                g = i * RING + k
                width = NB * W if p == 1 else W
                pe.wait_ge(gathered[k], i * (16 * GT) + ((p - 1) * NBODY + 1) * 16 * GT)
                pe.wait_ge(s_ready[p], g + 1)
                pe.wait_ge(added[p], g + 1)
                if p == 2:
                    for t in range(GT):
                        nc.tensor.matmul(count_at(k), ones[:, 0:1], S[:, k % 2, t, 0:W],
                                         start=t == 0, stop=t == GT - 1)
                for t in range(GT):
                    last = nc.tensor.matmul(bank[k % 2][:, 0:width], rows[:, k, t, :], S[:, k % 2, t, 0:width],
                                            start=t == 0, stop=t == GT - 1)
                last.then_inc(products[p], 1)

            def general_products(p, flag):
                width = NB * W if p == 1 else W
                with pe.If(flag != 0):
                    with pe.Fori(0, T) as t:
                        pe.wait_ge(slow_gathered, t * 16 + ((p - 1) * T + 1) * 16)
                        apart(pe)
                        with pe.Fori(0, NWIN) as c:
                            n = t * NWIN + c + (p - 1) * T * NWIN
                            pe.wait_ge(slow_s, n + 1)
                            if p == 2:
                                nc.tensor.matmul(count_at(0), ones[:, 0:1], S[:, 0, 0, 0:W], start=True, stop=True)
                            nc.tensor.matmul(bank[0][:, 0:width], rows[:, 0, 0, :], S[:, 0, 0, 0:width], start=True,
                                             stop=True).then_inc(slow_products, 1)
                            if p == 1:
                                pe.wait_ge(slow_moved, n + 1)
                                for b in range(NB):
                                    last = nc.tensor.matmul(bank[1][:, 0:W], bases_sb[:, b, :],
                                                            slow_G[:, b * W:(b + 1) * W], start=b == 0, stop=b == NB - 1)
                                last.then_inc(slow_based, 1)

            def turn(to, rows_in, rhs, more=False, n=BLK):
                for c in range(n):
                    last = nc.tensor.matmul(to[:, c * P:(c + 1) * P], rows_in[:, c * P:(c + 1) * P], rhs,
                                            start=True, stop=not more)
                    if more:
                        last = nc.tensor.matmul(to[:, c * P:(c + 1) * P], ones[0:1, :], bias0_row[0:1, :],
                                                start=False, stop=True)
                return last

            def stage_step(e, b, k, at):
                n = CHUNKS[k]
                if at == TURN:
                    pe.wait_ge(staged[e], b + 1)
                    pe.wait_ge(scaled if e == 3 else summed[e], b + 1)
                    turn(bank[2], stage[0], ident[:, :], n=n).then_inc(turned[e], 1)
                    if e == 2:
                        pe.wait_ge(cnt_staged, b + 1)
                        pe.wait_ge(sqrt_ready, b + 1)
                        for c in range(n):
                            last = nc.tensor.matmul(bank[5][:, c:c + 1], cnt_blk[k][:, c * P:(c + 1) * P], ones[0:1, 0:1],
                                                    start=True, stop=True)
                        last.then_inc(deg_turned, 1)
                elif at == TURN_ROWS and e != 4:
                    pe.wait_ge(normed[e], b + 1)
                    pe.wait_ge(rowsT_kept[e], b + 1)
                    turn(bank[3], xn[k], ident[:, :], n=n).then_inc(rowsT[e], 1)
                elif at == PROJECT and e != 4:
                    pe.wait_ge(rowsT_kept[e], b + 2)
                    pe.wait_ge(rows_ready[e], b + 1)
                    if e == 1:
                        for c in range(n):
                            last = nc.tensor.matmul(bank[4 + c // 2][:, (c % 2) * 2 * P:(c % 2 + 1) * 2 * P],
                                                    xT[k][:, c * P:(c + 1) * P], wdc_sb[:, :], start=True, stop=True)
                        last.then_inc(projected[1], 1)
                        pe.wait_ge(acc_set[1], b + 1)
                        nc.tensor.matmul(bank[6][:, 0:n * P], ws_sb[:, :], xT[k], start=True, stop=True).then_inc(selfed, 1)
                    else:
                        turn(bank[4], xT[k], (w1_sb if e == 2 else w2_sb)[:, :], n=n).then_inc(projected[e], 1)
                elif at == LOOPS and e in (2, 3):
                    pe.wait_ge(rows_ready[e], b + 2)
                    pe.wait_ge(acc_set[e], b + 1)
                    turn(bank[6], hst[k], ident[:, :], n=n).then_inc(loop_turned[e], 1)

            def base_piece(q, j):
                at = pe.value_load(part_i[0:1, bass.ds(q, 1)], min_val=0, max_val=CAP)
                pe.wait_ge(added[1], q * GPP + (GPP + ADDED_AHEAD))
                pe.wait_ge(based_added, q * NPIECE + (j + 1))
                for b in range(NB):
                    last = nc.tensor.matmul(bank[7][:, 0:PIECE], bases_sb[:, b, :], G[:, b, bass.ds(at + j * PIECE, PIECE)],
                                            start=b == 0, stop=b == NB - 1)
                last.then_inc(based, 1)

            def part_products(p, m, whole):
                for j in range(BPP):
                    for k in range(RING):
                        group_products(p, m * BPP + j, k)
                        at = (j * RING + k) // 2
                        if k % 2 == 1:
                            if p == 1 and at in (0, 2):
                                base_piece(m - 1, at // 2)
                            if whole:
                                stage_step(p, m - 2, 0, at)

            def pass_products(p):
                with pe.Fori(0, BPP if p == 1 else 2 * BPP) as i:
                    for k in range(RING):
                        group_products(p, i, k)
                if p == 1:
                    part_products(1, 1, False)
                with pe.Fori(2, NBLK) as m:
                    part_products(p, m, True)
                if p == 1:
                    for j in range(NPIECE):
                        base_piece(NBLK - 1, j)
                for at in range(STEPS):
                    stage_step(p, NBLK - 2, 0, at)
                    stage_step(p, NBLK - 1, 1, at)

            def window_by_edge(i, k):
                g = i * FSTEPS + k
                pe.wait_ge(sel_ready, g + (FSTEPS + 1))
                pe.wait_ge(c_kept, g + 1)
                for t in range(FT):
                    last = nc.tensor.matmul(bank[k % 2][0:W, t * P:(t + 1) * P], wS[k % 2][t], sel[k % 2][t],
                                            start=True, stop=True)
                last.then_inc(c_summed, 1)

            def rows_to_add(i, k):
                g = i * FSTEPS + k
                pe.wait_ge(c_kept, g + 3)
                pe.wait_ge(xwin_in[k], i * (16 * FHALF) + 16 * FHALF)
                pe.wait_ge(msg_kept, g + 1)
                for t in range(FT):
                    last = nc.tensor.matmul(bank[4 + k % 2][:, t * P:(t + 1) * P], C[k % 2][:, t * P:(t + 1) * P],
                                            xwin[k][t // GT], start=True, stop=True)
                last.then_inc(messages, 1)

            with pe.Fori(0, NBODY) as i:
                window_by_edge(i, 0)
                for k in range(FSTEPS - 1):
                    window_by_edge(i, k + 1)
                    rows_to_add(i, k)
                pe.wait_ge(hot_ready, i + 2)
                pe.wait_ge(alpha_ready, i + 1)
                for t in range(BODY):
                    last = nc.tensor.matmul(bank[2][:, t * NB:(t + 1) * NB], type_hot[:, t * P:(t + 1) * P],
                                            relw_sb[:, :], start=True, stop=True)
                last.then_inc(alpha_summed, 1)
                rows_to_add(i, FSTEPS - 1)
            flag = pe.value_load(flag_i[0:1, 0:1], min_val=0, max_val=1)
            with pe.If(flag != 0):
                with pe.Fori(0, T) as t:
                    pe.wait_ge(slow0_ready, t * 2 + 1)
                    nc.tensor.matmul(bank[0][:, 0:P], ones[:, :], masked[0][0], start=True, stop=True).then_inc(slow0_summed, 1)
                    pe.wait_ge(slow0_ready, t * 2 + 2)
                    nc.tensor.matmul(bank[1][:, 0:P], sel[0][0], rows4[:, 0, 1, :], start=True, stop=True).then_inc(slow0_summed, 1)

            def turn_tables(b, k, j, more):
                pe.wait_ge(tab_in[k], j * (16 * NTAB) + 16 * NTAB)
                pe.wait_ge(staged[0], b + 1)
                for c in range(BLK):
                    for n in range(NTAB):
                        last = nc.tensor.matmul(bank[2 + k][:, c * P:(c + 1) * P],
                                                tab_rows[k][:, n * BC + c * P:n * BC + (c + 1) * P], ident[:, :],
                                                start=n == 0, stop=n == NTAB - 1)
                last.then_inc(tab_turned, 1)

            def stage0(b, k, j, more):
                turn_tables(b, k, j, more)
                pe.wait_ge(staged[0], b + 3)
                pe.wait_ge(summed[0], b + 1)
                turn(bank[k], stage[k], k0_sb[:, :], True).then_inc(turned[0], 1)
            pe.wait_ge(alpha_ready, NBODY + 1)
            over_blocks(pe, stage0)

            for p in range(1, PASSES):
                general_products(p, flag)
                pass_products(p)

        @block.vector
        def _(dve):
            nprep = [0]

            def after(ins):
                nprep[0] += 1
                ins.then_inc(prep, 1)
                dve.wait_ge(prep, nprep[0])

            for p in range(1, PASSES):
                dve.sem_inc(added[p], ADDED_AHEAD)
            dve.sem_inc(based_added, 1)
            dve.sem_inc(sel_ready, FSTEPS)
            dve.sem_inc(hot_ready, 1)
            dve.sem_inc(scaled, 1)
            for e in NORMED:
                dve.sem_inc(summed[e], 1 if e else 2)
            for e in (1, 2, 3):
                dve.sem_inc(rows_ready[e], 1)

            def copy_idx(p, i, k):
                source = src2_i if p == 2 else src_i
                nc.vector.tensor_copy(idx_ring[:, k, :], source[:, bass.ds(i * BODY + k * GT, GT)]).then_inc(idx_ready[p], 1)

            dve.wait_ge(src_in, 16)
            nc.vector.memset(acc[:, :], 0.0).then_inc(acc_zeroed, 1)

            dve.wait_ge(edges_in, 16 * 3)
            nc.vector.tensor_copy(dst_f[:, :], dst_i).then_inc(dst_ready, 1)
            after(nc.vector.tensor_copy(src_f, src_i[:, 0:T]))
            dve.wait_ge(consts_set, 8)
            after(nc.vector.tensor_scalar(to_spare, src_f, -1.0, spare_row[:, 0:1], ALU.mult, ALU.add))
            after(nc.vector.tensor_scalar(src2_i[:, :], type2_i, 0, None, ALU.not_equal))
            after(nc.vector.scalar_tensor_tensor(src2_i[:, :], src_i[:, :], 2, src2_i[:, :], ALU.mult, ALU.add))
            dve.wait_ge(base_summed, 1)
            after(nc.vector.tensor_copy(base_bc[:, :], bank[0][:, 0:NG]))
            for m in range(2, NBLK):
                part = base_bc[:, m * GPP:(m + 1) * GPP]
                after(nc.vector.tensor_scalar(part, part, float((m - 1) * BC), None, ALU.max))
            after(nc.vector.tensor_copy(base_i[:, :], base_bc[0:1, :]))
            parts = base_bc[:, :].rearrange("p (q g) -> p q g", q=NBLK)
            after(nc.vector.tensor_tensor(off_bc[:, :].rearrange("p (q g) -> p q g", q=NBLK), parts,
                                          parts[:, :, 0:1].to_broadcast([P, NBLK, GPP]), ALU.subtract))
            after(nc.vector.tensor_scalar(off_ok, off_bc[:, :], 0.0, None, ALU.is_ge))
            after(nc.vector.scalar_tensor_tensor(off_ok2, off_bc[:, :], float(CAP - W), off_ok, ALU.is_le, ALU.mult))
            after(nc.vector.tensor_scalar(off_bc[:, :], off_bc[:, :], 0.0, float(CAP - W), ALU.max, ALU.min))
            after(nc.vector.memset(part_at[:, :], 0.0))
            for m in range(1, NBLK, 2):
                part = off_bc[:, m * GPP:(m + 1) * GPP]
                after(nc.vector.tensor_scalar(part, part, float(CAP), None, ALU.add))
                after(nc.vector.memset(part_at[:, m:m + 1], float(CAP)))
            after(nc.vector.tensor_copy(part_i[:, :], part_at[:, :]))
            after(nc.vector.tensor_copy(off_i[:, :], off_bc[0:1, :]))

            def by_group(a):
                return a.rearrange("p (g t) -> p g t", t=GT)

            def to_tiles(a):
                return a.unsqueeze(2).to_broadcast([P, NG, GT])

            after(nc.vector.memset(rel[:, T:TX], -1.0))
            after(nc.vector.memset(alpha[:, T * NB:TX * NB], 0.0))
            after(nc.vector.tensor_tensor(by_group(rel[:, 0:T]), by_group(dst_f[:, :]), to_tiles(base_bc[:, :]), ALU.subtract))
            after(nc.vector.scalar_tensor_tensor(by_group(ok), by_group(rel[:, 0:T]), 0.0, to_tiles(off_ok2), ALU.is_ge, ALU.mult))
            after(nc.vector.scalar_tensor_tensor(ok2, rel[:, 0:T], float(W), ok, ALU.is_lt, ALU.mult))
            after(nc.vector.scalar_tensor_tensor(rel[:, 0:T], rel[:, 0:T], 1.0, ok2, ALU.add, ALU.mult))
            after(nc.vector.tensor_scalar(rel[:, 0:T], rel[:, 0:T], -1.0, None, ALU.add))
            after(nc.vector.tensor_scalar(ok, ok2, -1.0, 1.0, ALU.mult, ALU.add))
            nc.vector.reduce_max(missed_any[:, 0:1], ok, AX_X).then_inc(missed_ready, 1)
            after(nc.vector.scalar_tensor_tensor(missed_dst[:, :], dst_f[:, :], 1.0, ok, ALU.add, ALU.mult))
            after(nc.vector.tensor_scalar(missed_dst[:, :], missed_dst[:, :], -1.0, None, ALU.add))
            dve.wait_ge(missed_summed, 1)
            nc.vector.tensor_scalar(flag_i[0:1, 0:1], bank[0][0:1, 0:1], 0.0, None, ALU.is_gt).then_inc(flag_ready, 1)
            dve.wait_ge(flag_ready, 1)
            flag = dve.value_load(flag_i[0:1, 0:1], min_val=0, max_val=1)
            dve.wait_ge(consts_set, 8)
            dve.wait_ge(acc_zeroed, 1)

            def make_S(p, g, k):
                dve.wait_ge(products[p], g + (PRODUCTS_AHEAD - 1))
                if p == 1:
                    nc.vector.tensor_tensor(S01[:, k % 2, :, :], iota_w[:, :].unsqueeze(1).to_broadcast([P, GT, W]),
                                            rel[:, bass.ds(g * GT, GT)].unsqueeze(2).to_broadcast([P, GT, W]),
                                            ALU.is_equal).then_inc(s01_ready, 1)
                    dve.wait_ge(s01_ready, g + 1)
                    nc.vector.tensor_tensor(
                        S[:, k % 2, :, :].rearrange("p t (b w) -> p t b w", w=W),
                        S01[:, k % 2, :, :].unsqueeze(2).to_broadcast([P, GT, NB, W]),
                        alpha[:, bass.ds(g * (GT * NB), GT * NB)].rearrange("p (t b) -> p t b", b=NB)
                        .unsqueeze(3).to_broadcast([P, GT, NB, W]), ALU.mult).then_inc(s_ready[p], 1)
                    return
                for t in range(GT):
                    last = nc.vector.tensor_scalar(S[:, k % 2, t, 0:W], iota_w[:, :], rel[:, bass.ds(g * GT + t, 1)], None,
                                                   ALU.is_equal)
                last.then_inc(s_ready[p], 1)

            def add_sums(p, g, k, at):
                dve.wait_ge(products[p], g + (PRODUCTS_AHEAD + 1))
                dve.wait_ge(added[p], g + ADDED_AHEAD)
                if p == 1:
                    to = G[:, :, bass.ds(at, W)]
                    sums = bank[k % 2][:, 0:NB * W].rearrange("p (b w) -> p b w", w=W)
                else:
                    to, sums = acc[:, bass.ds(at, W)], bank[k % 2][:, 0:W]
                if p == 2:
                    counts = cnt[:, bass.ds(at, W)]
                    nc.vector.tensor_tensor(counts, counts, count_at(k), ALU.add).then_inc(counted, 1)
                    dve.wait_ge(counted, g + 1)
                nc.vector.tensor_tensor(to, to, sums, ALU.add).then_inc(added[p], 1)

            def group_sums(p, i, k):
                places = off_i if p == 1 else base_i
                g = i * RING + k
                make_S(p, g + 1, k + 1)
                at = dve.value_load(places[0:1, bass.ds(g, 1)], min_val=0, max_val=2 * CAP - W if p == 1 else N)
                add_sums(p, g, k, at)
                copy_idx(p, i + 1, k)

            def start_pass(p):
                for k in range(RING):
                    copy_idx(p, 0, k)
                make_S(p, 0, 0)

            def general_sums(p):
                source = src2_i if p == 2 else src_i
                with dve.If(flag != 0):
                    with dve.Fori(0, T) as t:
                        nc.vector.tensor_copy(slow_idx[:, 0:1], source[:, bass.ds(t, 1)]).then_inc(slow_idx_ready, 1)
                        nc.vector.tensor_copy(slow_rel[:, 0:1], missed_dst[:, bass.ds(t, 1)]).then_inc(slow_step, 1)
                        with dve.Fori(0, NWIN) as c:
                            n = t * NWIN + c
                            steps = n * 2 + t + (p - 1) * (2 * NWIN + 1) * T
                            past = (p - 1) * T * NWIN
                            dve.wait_ge(slow_step, steps + 1)
                            if p == 1:
                                nc.vector.tensor_scalar(S01[:, 0, 0, :], iota_w[:, :], slow_rel[:, 0:1], None,
                                                        ALU.is_equal).then_inc(slow_s01, 1)
                                dve.wait_ge(slow_s01, n + 1)
                                nc.vector.tensor_tensor(
                                    S[:, 0, 0, :].rearrange("p (b w) -> p b w", w=W),
                                    S01[:, 0, 0, :].unsqueeze(1).to_broadcast([P, NB, W]),
                                    alpha[:, bass.ds(t * NB, NB)].unsqueeze(2).to_broadcast([P, NB, W]),
                                    ALU.mult).then_inc(slow_s, 1)
                            else:
                                nc.vector.tensor_scalar(S[:, 0, 0, 0:W], iota_w[:, :], slow_rel[:, 0:1], None,
                                                        ALU.is_equal).then_inc(slow_s, 1)
                            dve.wait_ge(slow_s, n + (past + 1))
                            nc.vector.tensor_scalar(slow_rel[:, 0:1], slow_rel[:, 0:1], float(-W), None,
                                                    ALU.add).then_inc(slow_step, 1)
                            dve.wait_ge(slow_products, n + (past + 1))
                            to = acc[:, bass.ds(c * W, W)]
                            sums = bank[0][:, 0:W]
                            if p == 1:
                                nc.vector.tensor_copy(slow_G[:, :], bank[0][:, 0:NB * W]).then_inc(slow_moved, 1)
                                dve.wait_ge(slow_based, n + 1)
                                sums = bank[1][:, 0:W]
                            if p == 2:
                                counts = cnt[:, bass.ds(c * W, W)]
                                nc.vector.tensor_tensor(counts, counts, count_at(0), ALU.add).then_inc(slow_counted, 1)
                                dve.wait_ge(slow_counted, n + 1)
                            nc.vector.tensor_tensor(to, to, sums, ALU.add).then_inc(slow_step, 1)
                            dve.wait_ge(slow_step, steps + 3)

            def blk(b, n=BLK):
                return bass.ds(b * BLK, n)

            def as_chunks(a, n=BLK):
                return a.rearrange("p (c f) -> p c f", c=n)

            def to_rows(v, n=BLK):
                return v.unsqueeze(2).to_broadcast([P, n, P])

            def to_chunks(v, n=BLK):
                return v.unsqueeze(1).to_broadcast([P, n, P])

            def chunk(b, c):
                return xcur[:, bass.ds(b * BLK + c, 1), :].rearrange("p c f -> p (c f)")

            def residual0(b, k, j, more):
                dve.wait_ge(turned[0], b + 3)
                to = xcur[:, blk(b), :]
                nc.vector.tensor_tensor(to, as_chunks(bank[k][:, :]), to, ALU.add).then_inc(summed[0], 1)
                dve.wait_ge(summed[0], b + 3)
                apart(dve)
                for c in range(BLK):
                    last = nc.vector.bn_stats(bst[:, c, :], chunk(b, c))
                last.then_inc(stats, 1)
                dve.wait_ge(stats, b * 3 + 1)
                apart(dve)
                for c in range(BLK):
                    last = nc.vector.bn_aggr(mvs[:, c, :], bst[:, c, :])
                last.then_inc(stats, 1)
                dve.wait_ge(stats, b * 3 + 2)
                nc.vector.tensor_copy(mv[:, blk(b), :], mvs[:, :, :]).then_inc(stats, 1)
                dve.wait_ge(stats, b * 3 + 3)

            def norm0(b, k, j, more):
                for c in range(BLK):
                    ch = b * BLK + c
                    last = nc.vector.tensor_scalar(chunk(b, c), chunk(b, c),
                                                   mv[:, bass.ds(ch, 1), 0:1].rearrange("p c s -> p (c s)"),
                                                   rstd[:, bass.ds(ch, 1)], ALU.subtract, ALU.mult)
                last.then_inc(normed[0], 1)

            def residual(e, b, k):
                n = CHUNKS[k]
                seen = 2 * moment_steps(e)
                dve.wait_ge(turned[e], b + 2)
                if e != 1:
                    dve.wait_ge(kept[e // 2], NBLK)
                to = xcur[:, blk(b, n), :]
                new = as_chunks(bank[2][:, 0:n * P], n)
                if e == 4:
                    nc.vector.tensor_tensor(as_chunks(xn[k], n), new, to_rows(dis[:, blk(b, n)], n),
                                            ALU.mult).then_inc(summed_scale, 1)
                    dve.wait_ge(summed_scale, b + 1)
                    new = as_chunks(xn[k], n)
                nc.vector.tensor_tensor(to, new, to, ALU.add).then_inc(summed[e], 1)
                dve.wait_ge(summed[e], b + 2)
                apart(dve)
                for c in range(n):
                    last = nc.vector.bn_stats(bst[:, c, :], chunk(b, c))
                last.then_inc(moments, 1)
                dve.wait_ge(moments, b * 2 + (seen + 1))
                apart(dve)
                for c in range(n):
                    last = nc.vector.bn_aggr(moments_of[:, k, c, :], bst[:, c, :])
                last.then_inc(moments, 1)
                if e == 2:
                    dve.wait_ge(sqrt_ready, b + 2)
                    nc.vector.reciprocal(dis[:, blk(b, n)], deg_dev[:, k, 0:n]).then_inc(deg_ready, 1)

            def norm(e, b, k):
                n = CHUNKS[k]
                dve.wait_ge(dev_ready, b + (moment_steps(e) + 1))
                nc.vector.reciprocal(inv_of[:, k, 0:n], dev_of[:, k, 0:n]).then_inc(inv_ready, 1)
                dve.wait_ge(inv_ready, b + (moment_steps(e) + 1))
                if e != 4:
                    dve.wait_ge(rowsT[e], b + 1)
                for c in range(n):
                    to = chunk(b, c) if e == 4 else xn[k][:, c * P:(c + 1) * P]
                    last = nc.vector.tensor_scalar(to, chunk(b, c), moments_of[:, k, c, 0:1], inv_of[:, k, c:c + 1],
                                                   ALU.subtract, ALU.mult)
                last.then_inc(normed[e], 1)

            def scale_and_bias(b, k):
                n = CHUNKS[k]
                dve.wait_ge(turned[3], b + 2)
                dve.wait_ge(rowsT[3], b + 1)
                nc.vector.tensor_tensor(as_chunks(xn[k], n), as_chunks(bank[2][:, 0:n * P], n), to_rows(dis[:, blk(b, n)], n),
                                        ALU.mult).then_inc(scaled, 1)
                dve.wait_ge(scaled, b + 2)
                nc.vector.tensor_tensor(as_chunks(xn[k], n), as_chunks(xn[k], n), to_chunks(b1_bc[:, :], n),
                                        ALU.add).then_inc(biased, 1)

            def table_rows(e, b, k):
                n = CHUNKS[k]
                dve.wait_ge(projected[e], b + 2)
                if k == 0:
                    dve.wait_ge(stored[e], b * 16 + 16)
                if e == 1:
                    for h in range(-(-n // 2)):
                        c = min(n, 2)
                        last = nc.vector.tensor_tensor(
                            hst[k][:, h * BC:h * BC + c * 2 * P].rearrange("p (c f) -> p c f", c=c),
                            bank[4 + h][:, 0:c * 2 * P].rearrange("p (c f) -> p c f", c=c),
                            bdc_bc[:, :].unsqueeze(1).to_broadcast([P, c, 2 * P]), ALU.add)
                    last.then_inc(rows_ready[1], 1)
                    return
                dve.wait_ge(loop_turned[e], b + 1)
                if e == 2:
                    dve.wait_ge(deg_ready, b + 1)
                nc.vector.tensor_tensor(as_chunks(hst[k][:, 0:n * P], n), as_chunks(bank[4][:, 0:n * P], n),
                                        to_rows(dis[:, blk(b, n)], n), ALU.mult).then_inc(rows_ready[e], 1)
                if e == 2:
                    dve.wait_ge(normed[2], b + 1)
                    nc.vector.tensor_tensor(xcur[:, blk(b, n), :], as_chunks(xn[k], n), to_chunks(b2_bc[:, :], n),
                                            ALU.add).then_inc(kept[2], 1)

            def stage_step(e, b, k, at):
                if at == RESIDUAL:
                    if e == 3:
                        scale_and_bias(b, k)
                    else:
                        residual(e, b, k)
                elif at == NORM and e != 3:
                    norm(e, b, k)
                elif at == TABLE and e != 4:
                    table_rows(e, b, k)

            def add_piece(q, j):
                start = dve.value_load(base_i[0:1, bass.ds(q * GPP, 1)], min_val=0, max_val=N)
                dve.wait_ge(based, q * NPIECE + (j + 1))
                dve.wait_ge(based_added, q * NPIECE + (j + 1))
                to = acc[:, bass.ds(start + j * PIECE, PIECE)]
                nc.vector.tensor_tensor(to, to, bank[7][:, 0:PIECE], ALU.add).then_inc(based_added, 1)

            def part_sums(p, m, whole):
                if p == 1 and whole:
                    dve.wait_ge(G_zeroed, m * NPIECE - (NPIECE - 1))
                for j in range(BPP):
                    for k in range(RING):
                        group_sums(p, m * BPP + j, k)
                        at = (j * RING + k) // 2
                        if k % 2 == 1:
                            if p == 1 and at in (1, 3):
                                add_piece(m - 1, at // 2)
                            if whole:
                                stage_step(p, m - 2, 0, at)

            def pass_sums(p):
                start_pass(p)
                with dve.Fori(0, BPP if p == 1 else 2 * BPP) as i:
                    for k in range(RING):
                        group_sums(p, i, k)
                if p == 1:
                    part_sums(1, 1, False)
                with dve.Fori(2, NBLK) as m:
                    part_sums(p, m, True)
                if p == 1:
                    for j in range(NPIECE):
                        add_piece(NBLK - 1, j)
                for at in range(STEPS):
                    stage_step(p, NBLK - 2, 0, at)
                    stage_step(p, NBLK - 1, 1, at)

            with dve.Fori(0, NBODY) as i:
                for k in range(FSTEPS):
                    g = i * FSTEPS + k
                    dve.wait_ge(c_summed, g + 1)
                    if k % 2 == 0:
                        dve.wait_ge(src_rows_in[k // 2], i * 16 + 16)
                    for t in range(FT):
                        nc.vector.tensor_scalar(wS[k % 2][t], iota_w[:, :], rel[:, bass.ds(g * FT + t, 1)],
                                                wgt[:, bass.ds(g * FT + t, 1)], ALU.is_equal, ALU.mult)
                        at = (k % 2 * FT + t) * P
                        last = nc.vector.tensor_scalar(sel[k % 2][t], src_rows[k // 2][:, at:at + P],
                                                       src_f[:, bass.ds(g * FT + t, 1)], None, ALU.is_equal)
                    last.then_inc(sel_ready, 1)
                    dve.wait_ge(sel_ready, g + (FSTEPS + 1))
                    for t in range(FT):
                        last = nc.vector.tensor_tensor_reduce(
                            out=masked[k % 2][t], in0=sel[k % 2][t], in1=earlier[:, :], scale=1.0, scalar=0.0,
                            op0=ALU.mult, op1=ALU.add, accum_out=dup[:, k % 2, t:t + 1])
                    last.then_inc(dup_step, 1)
                    dve.wait_ge(dup_step, g * 3 + 1)
                    nc.vector.scalar_tensor_tensor(dup[:, k % 2, :], dup[:, k % 2, :], 1.0, to_spare[:, bass.ds(g * FT, FT)],
                                                   ALU.min, ALU.mult).then_inc(dup_step, 1)
                    dve.wait_ge(dup_step, g * 3 + 2)
                    dve.wait_ge(scatter_through, g + 1)
                    nc.vector.tensor_tensor(idx4[:, k, :], dup[:, k % 2, :], src_f[:, bass.ds(g * FT, FT)],
                                            ALU.add).then_inc(idx_ready[0], 1)
                    dve.sem_inc(dup_step, 1)
                    if k == 1:
                        dve.wait_ge(types_in, i * 16 + 16)
                        dve.wait_ge(alpha_summed, i + 1)
                        nc.vector.tensor_scalar(type_hot, type_rows, iota_p[0:R, 0:1], None,
                                                ALU.is_equal).then_inc(hot_ready, 1)
            with dve.If(flag != 0):
                for k in range(NTAB):
                    dve.wait_ge(scattered[k], (T // FT + 1) * 16)
                with dve.Fori(0, T) as t:
                    nc.vector.tensor_copy(slow_idx[:, 0:1], dst_i[:, bass.ds(t, 1)]).then_inc(slow_idx_ready, 1)
                    source = src_f[:, bass.ds(t, 1)]
                    nc.vector.tensor_scalar(masked[0][0], ident[:, :], source, None, ALU.mult).then_inc(slow0_ready, 1)
                    nc.vector.tensor_scalar(slow_w[:, 0:1], missed_dst[:, bass.ds(t, 1)], 0.0, wgt[:, bass.ds(t, 1)],
                                            ALU.is_ge, ALU.mult).then_inc(slow0_step, 1)
                    dve.wait_ge(slow0_summed, t * 2 + 1)
                    nc.vector.tensor_scalar(sel[0][0], bank[0][:, 0:P], source, None, ALU.is_equal).then_inc(slow0_step, 1)
                    dve.wait_ge(slow0_step, t * 5 + 2)
                    nc.vector.tensor_tensor_reduce(
                        out=masked[0][1], in0=sel[0][0], in1=earlier[:, :], scale=1.0, scalar=0.0,
                        op0=ALU.mult, op1=ALU.add, accum_out=slow_dup[:, 0:1]).then_inc(slow0_step, 1)
                    dve.wait_ge(slow0_step, t * 5 + 3)
                    nc.vector.scalar_tensor_tensor(slow_dup[:, 0:1], slow_dup[:, 0:1], 1.0, to_spare[:, bass.ds(t, 1)],
                                                   ALU.min, ALU.mult).then_inc(slow0_step, 1)
                    dve.wait_ge(slow0_step, t * 5 + 4)
                    nc.vector.tensor_tensor(slow_out_idx[:, 0:1], slow_dup[:, 0:1], source, ALU.add).then_inc(slow0_step, 1)
                    dve.wait_ge(slow0_gathered, t * 16 + 16)
                    nc.vector.tensor_scalar(rows4[:, 0, 1, :], rows[:, 0, 0, :], slow_w[:, 0:1], None,
                                            ALU.mult).then_inc(slow0_ready, 1)
                    dve.wait_ge(slow0_summed, t * 2 + 2)
                    dve.wait_ge(slow0_step, t * 5 + 5)
                    nc.vector.tensor_copy(rows4[:, 0, 2, :], bank[1][:, 0:P]).then_inc(slow0_rows, 1)
                    dve.wait_ge(slow0_scattered, t * 16 + 16)
            dve.wait_ge(x_in, 16 * 2)
            over_blocks(dve, residual0)
            dve.sem_inc(all_stats, 1)
            dve.wait_ge(std_ready, 1)
            nc.vector.reciprocal(rstd[:, :], std[:, :]).then_inc(rstd_ready, 1)
            dve.wait_ge(rstd_ready, 1)
            over_blocks(dve, norm0)

            dve.wait_ge(alpha_ready, NBODY + 1)
            dve.wait_ge(G_zeroed, 1)
            for p in range(1, PASSES):
                if p == 2:
                    dve.wait_ge(G_zeroed, NBLK * NPIECE + 1)
                if p > 1:
                    dve.wait_ge(acc_set[p - 1], NBLK + 1)
                general_sums(p)
                pass_sums(p)


def kernel(x, src, dst, edge_type_2, edge_type_64, edge_weight, L0_gnn_kernel, L0_gnn_bias, L1_gnn_bases,
           L1_gnn_relation_base_weights, L2_gnn_W_data, L2_gnn_b_data, L2_gnn_W_control, L2_gnn_b_control,
           L2_gnn_W_self, L2_gnn_b_self, L3_gnn_W1, L3_gnn_b1, L3_gnn_W2, L3_gnn_b2):
    from concourse import bacc
    from concourse.bass_utils import run_bass_kernel_spmd

    def tiles(a, columns, pad):
        a = np.asarray(a)
        filled = np.concatenate([a, np.full(columns * P - E, pad, a.dtype)])
        return np.ascontiguousarray(filled.reshape(columns, P).T)

    def row(*parts):
        return np.ascontiguousarray(np.concatenate([np.asarray(a) for a in parts])[None, :])

    def turned(*parts):
        return np.ascontiguousarray(np.concatenate([np.asarray(a).T for a in parts], axis=1))

    arrays = {
        "src": tiles(src, TX, 0),
        "src_row": row(src, np.zeros(T * P - E, np.asarray(src).dtype)),
        "dst": tiles(dst, T, N),
        "type2": tiles(edge_type_2, TX, 0),
        "type64": row(edge_type_64, np.zeros(T * P - E, np.asarray(edge_type_64).dtype)),
        "weight": tiles(edge_weight, TX, 0),
        "x": np.concatenate([np.asarray(x), np.zeros((W, P), np.asarray(x).dtype)]),
        "k0": np.ascontiguousarray(L0_gnn_kernel),
        "bias0": row(L0_gnn_bias),
        "bases": np.ascontiguousarray(L1_gnn_bases),
        "rel_weights": np.ascontiguousarray(L1_gnn_relation_base_weights),
        "w_data_ctrl": turned(L2_gnn_W_data, L2_gnn_W_control),
        "b_data_ctrl": row(L2_gnn_b_data, L2_gnn_b_control),
        "w_self": turned(L2_gnn_W_self),
        "b_self": np.ascontiguousarray(np.asarray(L2_gnn_b_self)[:, None]),
        "w1": turned(L3_gnn_W1),
        "b1": row(L3_gnn_b1),
        "w2": turned(L3_gnn_W2),
        "b2": row(L3_gnn_b2),
    }
    nc = bacc.Bacc("TRN2", target_bir_lowering=False, num_devices=1)
    args = {n: nc.dram_tensor(n, a.shape, mybir.dt.from_np(a.dtype), kind="ExternalInput").ap() for n, a in arrays.items()}
    args["out"] = nc.dram_tensor("out", (N, P), FP, kind="ExternalOutput").ap()
    gnn_program(nc, **args)
    r = run_bass_kernel_spmd(nc, [arrays], core_ids=[0])
    return r.results[0]["out"]
```

```python
import numpy as np

import concourse.bass as bass
from concourse import mybir

FP = mybir.dt.float32
I32 = mybir.dt.int32
BF16 = mybir.dt.bfloat16
ALU = mybir.AluOpType
ACT = mybir.ActivationFunctionType

P = 128
N = 6250
E = 106250
NB = 8
NPART = 3
R = 64
GT = 2
RING = 8
BODY = GT * RING
FT = 4
FSTEPS = BODY // FT
FHALF = FT // GT
T = -(-E // (P * BODY)) * BODY
PAIR = 2
PT = PAIR * GT
PAIRS = RING // PAIR
TX = T + BODY
NG = T // GT
NBODY = NG // RING
W = 24
PIECE = 272
NPIECE = 2
CAP = PIECE * NPIECE
PAST = 22
BLK = 4
NBLK = -(-N // (BLK * P))
BC = BLK * P
NC = NBLK * BLK
BPP = NBODY // NBLK
GPP = NG // NBLK
LAST = N - (NBLK - 1) * BC
ACC = N + CAP
NWIN = -(-(N + 1) // W)
EPS = 1e-5
NTAB = FT
TABR = NBLK * BLK * P
SLOTS0 = 4
PASSES = 5
PRODUCTS_AHEAD = RING
ADDED_AHEAD = 2
STEPS = BODY * BPP // (2 * GT)
TURN, RESIDUAL, NORM, TURN_ROWS, PROJECT, TABLE, LOOPS = 5, 6, 7, 8, 10, 11, 12
PIECE_STEPS = 2
LAST_PIECE, FIRST_PIECE = 0, 12
CHUNKS = (BLK, 1)
AX_X = mybir.AxisListType.X
assert NBODY == BPP * NBLK and LAST < P and ACC >= NWIN * W and ACC >= TABR >= N + P


def gnn_program(nc, src, src_row, dst, type2, type64, weight, x, xT0, k0, bias0, bases, rel_weights,
                w_data_ctrl, b_data_ctrl, w_self, b_self, w1, b1, w2, b2, out):
    from contextlib import ExitStack

    ctx = ExitStack()
    with ctx:
        def sb(name, shape, dt=FP):
            return ctx.enter_context(nc.sbuf_tensor(name, shape, dt))

        def sem(name):
            return ctx.enter_context(nc.semaphore(name))

        t1 = nc.dram_tensor("t1", (N, P), FP, kind="Internal").ap()
        t2 = nc.dram_tensor("t2", (2 * N, P), FP, kind="Internal").ap()
        t3 = nc.dram_tensor("t3", (N, P), FP, kind="Internal").ap()
        t4 = nc.dram_tensor("t4", (N, P), FP, kind="Internal").ap()
        hx = nc.dram_tensor("hx", (TABR, P), FP, kind="Internal").ap()
        tables = [hx, t1, t2, t3, t4]
        sums_t = [nc.dram_tensor(f"sums{k}", (TABR, P), FP, kind="Internal").ap() for k in range(NTAB)]

        src_i = sb("src_i", [P, TX], I32)
        src2_i = sb("src2_i", [P, TX], I32)
        wgt = sb("wgt", [P, TX])
        dst_f = sb("dst_f", [P, T])
        rel = sb("rel", [P, TX])
        missed_dst = sb("missed_dst", [P, T])
        alpha = sb("alpha", [P, TX * NB])
        base_bc = sb("base_bc", [P, NG])
        piece_floor = sb("piece_floor", [P, NBLK])
        off_bc = sb("off_bc", [P, NG])
        base_i = sb("base_i", [1, NG], I32)
        off_i = sb("off_i", [1, NG], I32)
        part_at = sb("part_at", [1, NBLK])
        part_i = sb("part_i", [1, NBLK], I32)
        missed_any = sb("missed_any", [P, 1])
        flag_i = sb("flag_i", [1, 1], I32)

        xcur = sb("xcur", [P, NC, P])
        acc = sb("acc", [P, ACC])
        dis = sb("dis", [P, NC])
        bst = sb("bst", [P, BLK, 6])
        moments_of = sb("moments_of", [P, SLOTS0, BLK, 2])
        dev_of = sb("dev_of", [P, SLOTS0, BLK])
        inv_of = sb("inv_of", [P, SLOTS0, BLK])
        shift_of = sb("shift_of", [P, SLOTS0, BLK])
        deg_dev = sb("deg_dev", [P, 2, BLK])

        rows = sb("rows", [P, RING, GT, P])
        idx_ring = sb("idx_ring", [P, RING, GT], I32)
        S = sb("S", [P, 2, PT, NB * W])
        S01 = sb("S01", [P, 2, PT, W])
        rows4 = rows[:, :, :, :].rearrange("p (s h) t f -> p s (h t) f", h=FHALF)
        shared = sb("shared", [P, 2, 2, FT, P])
        sel = [shared[:, 0, s, :, :] for s in range(2)]
        masked = [shared[:, 1, s, :, :] for s in range(2)]
        hits = sb("hits", [P, 2, FT, W])
        wS = sb("wS", [P, 2, FT, W])
        msg = [rows4[:, s, :, :] for s in range(2)]
        xwin = [[rows4[0:W, 2 + h, k, :] for h in range(FHALF)] for k in range(FSTEPS)]
        dup = sb("dup", [P, 2, FT])
        idx4 = idx_ring[:, :, :].rearrange("p (s h) t -> p s (h t)", h=FHALF)

        TW = BODY * P
        NG_COLS = 2 * NB * CAP
        arena = sb("arena", [P, 2 * TW + 8 * TX + TW + 2 * BC])
        G = arena[:, 0:NG_COLS].rearrange("p (b c) -> p b c", b=NB)
        type_rows = arena[0:R, 0:TW].bitcast(I32)
        type_hot = arena[0:R, TW:TW + TW // 2].bitcast(BF16)
        dst_i = arena[:, 2 * TW:2 * TW + T].bitcast(I32)
        type2_i = arena[:, 2 * TW + TX:2 * TW + 2 * TX].bitcast(I32)
        ok = arena[:, 2 * TW + 2 * TX:2 * TW + 2 * TX + T]
        ok2 = arena[:, 2 * TW + 3 * TX:2 * TW + 3 * TX + T]
        off_ok = arena[:, 2 * TW + 4 * TX:2 * TW + 4 * TX + NG]
        off_ok2 = arena[:, 2 * TW + 5 * TX:2 * TW + 5 * TX + NG]
        src_f = arena[:, 2 * TW + 6 * TX:2 * TW + 6 * TX + T]
        to_spare = arena[:, 2 * TW + 7 * TX:2 * TW + 7 * TX + T]
        HW = TW // 2
        h0 = 2 * TW + 8 * TX
        src_rows = [arena[:, h0 + s * HW:h0 + (s + 1) * HW].bitcast(I32) for s in range(2)]
        C = [arena[0:W, h0 + 2 * HW + s * BC:h0 + 2 * HW + (s + 1) * BC] for s in range(2)]
        assert h0 + 2 * HW + 2 * BC == arena.shape[1]
        TAB0 = arena.shape[1] - 2 * NTAB * BC
        assert TAB0 >= NG_COLS
        tab_rows = [a.rearrange("p (n c) -> p n c", n=NTAB) for a in (
            rows[:, :, :, :].rearrange("p k c f -> p (k c f)"), shared[:, :, :, :, :].rearrange("p e s t f -> p (e s t f)"),
            arena[:, TAB0:TAB0 + NTAB * BC], arena[:, TAB0 + NTAB * BC:])]
        cnt = arena[0:1, 0:NBLK * BC]
        a0 = max(NG_COLS, NBLK * BC)

        def scratch(n):
            nonlocal a0
            a0 += n
            return arena[:, a0 - n:a0]

        xn = [scratch(c * P) for c in CHUNKS]
        xT = [scratch(c * P) for c in CHUNKS]
        hst = [scratch(2 * c * P) for c in CHUNKS]
        cnt_blk = [scratch(c * P)[0:1, :] for c in CHUNKS]
        assert a0 <= arena.shape[1]
        stage = sb("stage", [P, BC])
        xT_sb = xcur[:, :, :].rearrange("p c f -> p (c f)")
        hx_sb = alpha[:, 0:NBLK * BC].rearrange("p (c f) -> p c f", f=P)
        HXB = (0, 5, 9, NBLK)

        k0_sb = sb("k0_sb", [P, P])
        bias0_bc = sb("bias0_bc", [P, P])
        bias0_blk = sb("bias0_blk", [P, BLK, P])
        bases_sb = sb("bases_sb", [P, NB, P])
        relw_sb = sb("relw_sb", [R, NB])
        relw_rest = sb("relw_rest", [R, NB])
        relw_parts = sb("relw_parts", [R, NB, NPART], BF16)
        wdc_sb = sb("wdc_sb", [P, 2 * P])
        bdc_bc = sb("bdc_bc", [P, 2 * P])
        ws_sb = sb("ws_sb", [P, P])
        bs_sb = sb("bs_sb", [P, 1])
        w1_sb = sb("w1_sb", [P, P])
        b1_bc = sb("b1_bc", [P, P])
        w2_sb = sb("w2_sb", [P, P])
        b2_bc = sb("b2_bc", [P, P])
        ident = sb("ident", [P, P])
        first_row = sb("first_row", [P, P])
        ones = sb("ones", [P, P])
        zeros = sb("zeros", [P, PIECE])
        iota_w = sb("iota_w", [P, W])
        iota_p = sb("iota_p", [P, 1])
        spare_row = sb("spare_row", [P, 1])
        earlier = sb("earlier", [P, P])
        slow_out_idx = sb("slow_out_idx", [P, 1], I32)
        slow_w = sb("slow_w", [P, 1])
        slow_dup = sb("slow_dup", [P, 1])
        eps_sb = sb("eps_sb", [P, 1])
        slow_idx = sb("slow_idx", [P, 1], I32)
        slow_rel = sb("slow_rel", [P, 1])
        slow_G = sb("slow_G", [P, NB * W])

        bank = [ctx.enter_context(nc.psum_tensor(f"bank{k}", [P, 512], FP)) for k in range(8)]

        edges_in = sem("edges_in")
        src_in = sem("src_in")
        weights_in = sem("weights_in")
        k0_in = sem("k0_in")
        xT_in = [sem(f"xT_in{k}") for k in range(len(HXB) - 1)]
        supported = sem("supported")
        support_kept = sem("support_kept")
        hx_stored = sem("hx_stored")
        bias_ready = sem("bias_ready")
        consts_set = sem("consts_set")
        const_step = sem("const_step")
        acc_zeroed = sem("acc_zeroed")
        prep = sem("prep")
        dst_ready = sem("dst_ready")
        base_summed = sem("base_summed")
        missed_ready = sem("missed_ready")
        missed_summed = sem("missed_summed")
        flag_ready = sem("flag_ready")
        types_in = sem("types_in")
        relw_ready = sem("relw_ready")
        hits_ready = sem("hits_ready")
        hot_ready = sem("hot_ready")
        alpha_summed = sem("alpha_summed")
        alpha_ready = sem("alpha_ready")

        idx_ready = [sem(f"idx_ready{p}") for p in range(PASSES)]
        gathered = [sem(f"gathered{k}") for k in range(RING)]
        s01_ready = sem("s01_ready")
        s_ready = [sem(f"s_ready{p}") for p in range(PASSES)]
        products = [sem(f"products{p}") for p in range(PASSES)]
        added = [sem(f"added{p}") for p in range(PASSES)]
        counted = sem("counted")
        src_rows_in = [sem(f"src_rows_in{k}") for k in range(2)]
        xwin_in = [sem(f"xwin_in{k}") for k in range(FSTEPS)]
        sel_ready = sem("sel_ready")
        dup_step = sem("dup_step")
        c_summed = sem("c_summed")
        c_kept = sem("c_kept")
        messages = sem("messages")
        msg_kept = sem("msg_kept")
        scattered = [sem(f"scattered{k}") for k in range(NTAB)]
        scatter_through = sem("scatter_through")
        tables_done = sem("tables_done")
        tab_in = [sem(f"tab_in{k}") for k in range(SLOTS0)]
        tab_paired = sem("tab_paired")
        slow0_ready = sem("slow0_ready")
        slow0_summed = sem("slow0_summed")
        slow0_step = sem("slow0_step")
        slow0_rows = sem("slow0_rows")
        slow0_scattered = sem("slow0_scattered")
        based = sem("based")
        based_added = sem("based_added")
        G_zeroed = sem("G_zeroed")

        slow_idx_ready = sem("slow_idx_ready")
        slow0_gathered = sem("slow0_gathered")
        slow_gathered = sem("slow_gathered")
        slow_step = sem("slow_step")
        slow_s = sem("slow_s")
        slow_s01 = sem("slow_s01")
        slow_counted = sem("slow_counted")
        slow_products = sem("slow_products")
        slow_moved = sem("slow_moved")
        slow_based = sem("slow_based")

        LAYERS = range(5)
        NORMED = (0, 1, 2, 4)
        NTH = {e: n for n, e in enumerate(NORMED)}

        def sems(name, stages):
            return {e: sem(f"{name}{e}") for e in stages}

        staged = sems("staged", LAYERS[1:])
        turned = sems("turned", LAYERS[1:])
        summed = sems("summed", NORMED)
        stats = sem("stats")
        dev0_ready = sem("dev0_ready")
        inv0_ready = sem("inv0_ready")
        shift0_ready = sem("shift0_ready")
        moments = sem("moments")
        dev_ready = sem("dev_ready")
        inv_ready = sem("inv_ready")
        normed = sems("normed", LAYERS)
        kept = sems("kept", (1, 2))
        rowsT = sems("rowsT", (1, 2, 3))
        rowsT_kept = sems("rowsT_kept", (1, 2, 3))
        projected = sems("projected", (1, 2, 3))
        selfed = sem("selfed")
        rows_ready = sems("rows_ready", (1, 2, 3))
        stored0 = sem("stored0")
        stored = sems("stored", (1, 2, 3))
        loop_turned = sems("loop_turned", (2, 3))
        acc_set = sems("acc_set", (1, 2, 3))
        scaled = sem("scaled")
        biased = sem("biased")
        deg_ready = sem("deg_ready")
        cnt_staged = sem("cnt_staged")
        deg_turned = sem("deg_turned")
        sqrt_ready = sem("sqrt_ready")
        out_stored = sem("out_stored")
        summed_scale = sem("summed_scale")

        waits_passed = sem("waits_passed")
        block = ctx.enter_context(nc.Block())

        def apart(eng):
            eng.sem_inc(waits_passed, 1)

        assert NBLK % SLOTS0 == 1

        def over_blocks(eng, step):
            with eng.Fori(0, NBLK // SLOTS0) as j:
                for k in range(SLOTS0):
                    step(j * SLOTS0 + k, k, j, True)
            step(NBLK - 1, 0, NBLK // SLOTS0, False)

        def in_steps(eng, stage_step):
            with eng.Fori(0, NBLK - 2) as b:
                for at in range(STEPS):
                    stage_step(b, 0, at)
            for at in range(STEPS):
                stage_step(NBLK - 2, 0, at)
                stage_step(NBLK - 1, 1, at)

        def sums_whole(eng, p, b):
            if p == 1:
                eng.wait_ge(based_added, NPIECE * NBLK + 1 if isinstance(b, int) else b * NPIECE + (2 * NPIECE + 1))
            else:
                eng.wait_ge(added[p], NG + ADDED_AHEAD if isinstance(b, int) else b * GPP + (2 * GPP + ADDED_AHEAD))

        def moment_steps(e):
            return (NTH[e] - 1) * NBLK

        def count_at(k):
            return bank[k % 2][0:1, BC - W:BC]

        def node_rows(table, b):
            return table[bass.ds(b * BC, BC), :].rearrange("(c p) f -> p c f", p=P)

        t2_pairs = t2.rearrange("(n t) f -> n (t f)", t=2)

        @block.sync
        def _(sp):
            for e in (1, 2, 3):
                sp.sem_inc(stored[e], 16)
            sp.dma_start(k0_sb[:, :], k0).then_inc(k0_in, 16)
            sp.dma_start(bias0_bc[:, :], bias0.to_broadcast([P, P])).then_inc(k0_in, 16)
            sp.dma_start(src_i[:, :], src).then_inc(src_in, 16)
            sp.dma_start(dst_i, dst).then_inc(edges_in, 16)
            sp.dma_start(wgt[:, :], weight).then_inc(edges_in, 16)
            sp.dma_start(type2_i, type2).then_inc(edges_in, 16)

            for n, (a, b) in enumerate(zip(HXB, HXB[1:])):
                sp.dma_start(xT_sb[:, a * BC:b * BC], xT0[:, a * BC:b * BC]).then_inc(xT_in[n], 16)
            sp.dma_start(relw_sb[:, :], rel_weights).then_inc(weights_in, 16)
            sp.dma_start(bases_sb[:, :, :], bases.rearrange("b f o -> f b o")).then_inc(weights_in, 16)
            sp.dma_start(wdc_sb[:, :], w_data_ctrl).then_inc(weights_in, 16)
            sp.dma_start(ws_sb[:, :], w_self).then_inc(weights_in, 16)
            sp.dma_start(w1_sb[:, :], w1).then_inc(weights_in, 16)
            sp.dma_start(w2_sb[:, :], w2).then_inc(weights_in, 16)
            sp.dma_start(bs_sb[:, :], b_self).then_inc(weights_in, 16)
            sp.dma_start(bdc_bc[:, :], b_data_ctrl.to_broadcast([P, 2 * P])).then_inc(weights_in, 16)
            sp.dma_start(b1_bc[:, :], b1.to_broadcast([P, P])).then_inc(weights_in, 16)
            sp.dma_start(b2_bc[:, :], b2.to_broadcast([P, P])).then_inc(weights_in, 16)

            for a, b in zip(HXB, HXB[1:]):
                sp.wait_ge(support_kept, b + 2)
                sp.dma_start(hx[a * BC:b * BC, :].rearrange("(c p) f -> p c f", p=P),
                             hx_sb[:, a * BLK:b * BLK, :]).then_inc(hx_stored, 16)
            sp.wait_ge(flag_ready, 1)
            sp.wait_ge(hx_stored, 16 * (len(HXB) - 1))
            with sp.Fori(0, NBODY) as i:
                sp.wait_ge(hot_ready, i + 1)
                sp.dma_start(type_rows, type64[0:1, bass.ds(i * TW, TW)].to_broadcast([R, TW])
                             ).then_inc(types_in, 16)
                for h in range(2):
                    sp.wait_ge(sel_ready, i * FSTEPS + 2 * h + 2)
                    sp.dma_start(src_rows[h], src_row[0:1, bass.ds(i * TW + h * HW, HW)].to_broadcast([P, HW])
                                 ).then_inc(src_rows_in[h], 16)
                    for k in (2 * h, 2 * h + 1):
                        for w in range(FHALF):
                            base = sp.value_load(base_i[0:1, bass.ds(i * RING + (k * FHALF + w), 1)], min_val=0, max_val=N + PIECE)
                            if w == 0:
                                sp.wait_ge(messages, i * FSTEPS + k + 1)
                            sp.dma_start(xwin[k][w], hx[bass.ds(base, W), :]).then_inc(xwin_in[k], 16)

            sp.wait_ge(tables_done, 1)
            def load_tables(b, k, j, more):
                sp.wait_ge(summed[0], b + 1)
                for n in range(NTAB):
                    sp.dma_start(tab_rows[k][:, n, :].rearrange("p (c f) -> p c f", c=BLK),
                                 node_rows(sums_t[n], b)).then_inc(tab_in[k], 16)
            over_blocks(sp, load_tables)

            def store_x1(b, k, j, more):
                sp.wait_ge(normed[0], b + (SLOTS0 + 1))
                if more:
                    sp.dma_start(node_rows(t1, b), xcur[:, bass.ds(b * BLK, BLK), :]).then_inc(stored0, 16)
                else:
                    sp.dma_start(t1[b * BC:N, :], xcur[0:LAST, b * BLK, :]).then_inc(stored0, 16)
            over_blocks(sp, store_x1)

            for e, table, width in ((1, t2_pairs, 2 * P), (2, t3, P), (3, t4, P)):
                with sp.Fori(0, NBLK - 1) as b:
                    sp.wait_ge(rows_ready[e], b + 2)
                    sp.dma_start(node_rows(table, b), hst[0][:, 0:BLK * width].rearrange(
                        "p (c f) -> p c f", c=BLK)).then_inc(stored[e], 16)
                sp.wait_ge(rows_ready[e], NBLK + 1)
                sp.dma_start(table[(NBLK - 1) * BC:N, :], hst[1][0:LAST, 0:width]).then_inc(stored[e], 16)

            def store_out(b, k, j, more):
                sp.wait_ge(normed[4], b + 1)
                if more:
                    sp.dma_start(node_rows(out, b), xcur[:, bass.ds(b * BLK, BLK), :]).then_inc(out_stored, 16)
                else:
                    sp.dma_start(out[b * BC:N, :], xcur[0:LAST, b * BLK, :]).then_inc(out_stored, 16)
            over_blocks(sp, store_out)
            sp.wait_ge(out_stored, 16 * NBLK)

        @block.gpsimd
        def _(pool):
            nc.gpsimd.memset(ones[:, :], 1.0).then_inc(const_step, 1)
            nc.gpsimd.memset(zeros[:, :], 0.0).then_inc(consts_set, 1)
            nc.gpsimd.memset(eps_sb[:, :], EPS).then_inc(consts_set, 1)
            nc.gpsimd.iota(iota_w[:, :], [[1, W]], base=0, channel_multiplier=0,
                           allow_small_or_imprecise_dtypes=True).then_inc(consts_set, 1)
            nc.gpsimd.iota(iota_p[:, :], [[0, 1]], base=0, channel_multiplier=1,
                           allow_small_or_imprecise_dtypes=True).then_inc(consts_set, 1)
            pool.wait_ge(const_step, 1)
            nc.gpsimd.affine_select(out=ident[:, :], in_=ones[:, :], compare_op=ALU.is_equal, fill=0.0,
                                    base=0, pattern=[[-1, P]], channel_multiplier=1).then_inc(consts_set, 1)
            nc.gpsimd.affine_select(out=first_row[:, :], in_=ones[:, :], compare_op=ALU.is_equal, fill=0.0,
                                    base=0, pattern=[[0, P]], channel_multiplier=1).then_inc(consts_set, 1)
            nc.gpsimd.affine_select(out=earlier[:, :], in_=ones[:, :], compare_op=ALU.is_ge, fill=0.0,
                                    base=-1, pattern=[[-1, P]], channel_multiplier=1).then_inc(consts_set, 1)
            nc.gpsimd.iota(spare_row[:, :], [[0, 1]], base=N, channel_multiplier=1,
                           allow_small_or_imprecise_dtypes=True).then_inc(consts_set, 1)

            def gather_pass(p):
                with pool.Fori(0, NBODY) as i:
                    for k in range(RING):
                        g = i * RING + k
                        if k % PAIR == 0:
                            pool.wait_ge(idx_ready[p], i * PAIRS + (k // PAIR + 1))
                        pool.wait_ge(products[p], g + 1)
                        apart(pool)
                        for t in range(GT):
                            nc.gpsimd.indirect_dma_start(
                                out=rows[:, k, t, :], out_offset=None, in_=tables[p],
                                in_offset=bass.IndirectOffsetOnAxis(ap=idx_ring[:, k, t:t + 1], axis=0),
                            ).then_inc(gathered[k], 16)

            def gather_general(p, flag):
                with pool.If(flag != 0):
                    with pool.Fori(0, T) as t:
                        pool.wait_ge(slow_idx_ready, t + (p * T + 1))
                        apart(pool)
                        nc.gpsimd.indirect_dma_start(
                            out=rows[:, 0, 0, :], out_offset=None, in_=tables[p],
                            in_offset=bass.IndirectOffsetOnAxis(ap=slow_idx[:, 0:1], axis=0),
                        ).then_inc(slow_gathered, 16)

            pool.sem_inc(scatter_through, 3)
            pool.wait_ge(acc_zeroed, 1)
            pool.wait_ge(bias_ready, 1)
            pool.wait_ge(xT_in[len(HXB) - 2], 16)
            pool.dma_start(sums_t[0], x).then_inc(scattered[0], 16)
            pool.dma_start(sums_t[1].rearrange("(p b r) f -> p b (r f)", p=P, r=BLK),
                           bias0_blk[:, :, :].rearrange("p r f -> p (r f)").unsqueeze(1).to_broadcast([P, NBLK, BC])
                           ).then_inc(scattered[1], 16)
            for t in range(2, NTAB):
                if t == 2:
                    pool.wait_ge(hx_stored, 16 * (len(HXB) - 1))
                else:
                    pool.wait_ge(xwin_in[0], 16 * FHALF)
                pool.dma_start(sums_t[t].rearrange("(p r) f -> p (r f)", p=P), acc[:, 0:TABR]).then_inc(scattered[t], 16)
            with pool.Fori(0, NBODY) as i:
                for k in range(FSTEPS):
                    g = i * FSTEPS + k
                    pool.wait_ge(idx_ready[0], g + 1)
                    pool.wait_ge(msg_kept, g + 3)
                    for t in range(NTAB):
                        pool.wait_ge(scattered[t], g * 16 + 16)
                        apart(pool)
                        if t == NTAB - 1:
                            pool.sem_inc(scatter_through, 1)
                        nc.gpsimd.indirect_dma_start(
                            out=sums_t[t], out_offset=bass.IndirectOffsetOnAxis(ap=idx4[:, k, t:t + 1], axis=0),
                            in_=msg[k % 2][:, t, :], in_offset=None, compute_op=ALU.add).then_inc(scattered[t], 16)
            for t in range(NTAB):
                pool.wait_ge(scattered[t], (T // FT + 1) * 16)
            flag = pool.value_load(flag_i[0:1, 0:1], min_val=0, max_val=1)
            with pool.If(flag != 0):
                with pool.Fori(0, T) as t:
                    pool.wait_ge(slow_idx_ready, t + 1)
                    apart(pool)
                    nc.gpsimd.indirect_dma_start(
                        out=rows[:, 0, 0, :], out_offset=None, in_=tables[0],
                        in_offset=bass.IndirectOffsetOnAxis(ap=slow_idx[:, 0:1], axis=0),
                    ).then_inc(slow0_gathered, 16)
                    pool.wait_ge(slow0_rows, t + 1)
                    apart(pool)
                    nc.gpsimd.indirect_dma_start(
                        out=sums_t[0], out_offset=bass.IndirectOffsetOnAxis(ap=slow_out_idx[:, 0:1], axis=0),
                        in_=rows4[:, 0, 2, :], in_offset=None, compute_op=ALU.add).then_inc(slow0_scattered, 16)
                pool.wait_ge(slow0_scattered, 16 * T)
            pool.sem_inc(tables_done, 1)

            def pair_tables(b, k, j, more):
                pool.wait_ge(tab_in[k], j * (16 * NTAB) + 16 * NTAB)
                half = tab_rows[k][:, 0:NTAB // 2, :]
                nc.gpsimd.tensor_tensor(half, half, tab_rows[k][:, NTAB // 2:NTAB, :], ALU.add).then_inc(tab_paired, 1)
            over_blocks(pool, pair_tables)

            pool.wait_ge(alpha_summed, NBODY + 1)
            nc.gpsimd.memset(arena[:, 0:NG_COLS], 0.0).then_inc(G_zeroed, 1)

            for p in range(1, PASSES):
                if p == 1:
                    pool.wait_ge(stored0, 16 * NBLK)
                else:
                    pool.wait_ge(stored[p - 1], 16 * (NBLK + 1))
                gather_general(p, flag)
                gather_pass(p)

        @block.scalar
        def _(act):
            act.sem_inc(support_kept, 2)
            act.sem_inc(normed[0], SLOTS0)
            act.wait_ge(k0_in, 16 * 2)
            nc.scalar.activation(bias0_blk[:, :, :], bias0_bc[:, :].unsqueeze(1).to_broadcast([P, BLK, P]),
                                 ACT.Copy).then_inc(bias_ready, 1)

            for b in range(NBLK):
                act.wait_ge(supported, b + 1)
                nc.scalar.activation(hx_sb[:, b * BLK:(b + 1) * BLK, :].rearrange("p c f -> p (c f)"), bank[2 + b % 2][:, :],
                                     ACT.Copy).then_inc(support_kept, 1)
            act.sem_inc(sqrt_ready, 1)
            for e in (1, 2, 3):
                act.sem_inc(rowsT_kept[e], 1)
                act.sem_inc(acc_set[e], 1)

            act.sem_inc(c_kept, 2)
            act.sem_inc(msg_kept, 2)
            def keep_window(i, k):
                act.wait_ge(c_summed, i * FSTEPS + (k + 3))
                act.wait_ge(messages, i * FSTEPS + (k + 3))
                nc.scalar.activation(C[k % 2], bank[k % 2][0:W, :], ACT.Copy).then_inc(c_kept, 1)

            def keep_rows(i, k):
                act.wait_ge(messages, i * FSTEPS + (k + 5))
                act.wait_ge(scatter_through, i * FSTEPS + (k + 3))
                nc.scalar.activation(msg[k % 2].rearrange("p t f -> p (t f)"), bank[4 + k % 2][:, :],
                                     ACT.Copy).then_inc(msg_kept, 1)

            with act.Fori(0, NBODY) as i:
                keep_window(i, 0)
                for k in range(FSTEPS - 1):
                    keep_window(i, k + 1)
                    keep_rows(i, k)
                keep_rows(i, FSTEPS - 1)

            act.wait_ge(consts_set, 8)
            act.wait_ge(weights_in, 16 * 10)

            def deviations(b, k):
                act.wait_ge(stats, b * 2 + 2)
                apart(act)
                nc.scalar.activation(dev_of[:, k, :], moments_of[:, k, :, 1], ACT.Sqrt,
                                     bias=eps_sb[:, 0:1]).then_inc(dev0_ready, 1)

            def norm0(b, k, j, more):
                if more:
                    deviations(b + 1, (k + 1) % SLOTS0)
                act.wait_ge(shift0_ready, b + 1)
                apart(act)
                for c in range(BLK):
                    row = xcur[:, bass.ds(b * BLK + c, 1), :].rearrange("p c f -> p (c f)")
                    last = nc.scalar.activation(row, row, ACT.Identity, bias=shift_of[:, k, c:c + 1],
                                                scale=inv_of[:, k, c:c + 1])
                last.then_inc(normed[0], 1)
            deviations(0, 0)
            over_blocks(act, norm0)

            def zero_piece(q, j):
                at = act.value_load(part_i[0:1, bass.ds(q, 1)], min_val=0, max_val=CAP)
                act.wait_ge(based, q * NPIECE + (j + 1))
                apart(act)
                nc.scalar.activation(G[:, :, bass.ds(at + j * PIECE, PIECE)],
                                     zeros[:, :].unsqueeze(1).to_broadcast([P, NB, PIECE]), ACT.Copy).then_inc(G_zeroed, 1)

            def to_acc(b, k, rows_in, func, **more):
                return nc.scalar.activation(acc[:, bass.ds(b * BC, CHUNKS[k] * P)], rows_in[:, 0:CHUNKS[k] * P], func, **more)

            def stage_step(e, b, k, at):
                n = CHUNKS[k]
                if at == TURN:
                    sums_whole(act, e, b)
                    act.wait_ge(turned[e], b + 1)
                    apart(act)
                    nc.scalar.activation(stage[:, 0:n * P], acc[:, bass.ds(b * BC, n * P)],
                                         ACT.Relu if e == 2 else ACT.Copy).then_inc(staged[e], 1)
                    if e == 2:
                        nc.scalar.activation(cnt_blk[k], cnt[:, bass.ds(b * BC, n * P)], ACT.Copy).then_inc(cnt_staged, 1)
                elif at == RESIDUAL and e == 2:
                    act.wait_ge(deg_turned, b + 1)
                    apart(act)
                    nc.scalar.activation(deg_dev[:, k, 0:n], bank[5][:, 0:n], ACT.Sqrt, bias=ones[:, 0:1]).then_inc(sqrt_ready, 1)
                elif at == NORM and e == 3:
                    act.wait_ge(biased, b + 1)
                    nc.scalar.activation(xn[k], xn[k], ACT.Relu).then_inc(normed[3], 1)
                elif at == NORM:
                    act.wait_ge(moments, b * 2 + (2 * moment_steps(e) + 2))
                    apart(act)
                    nc.scalar.activation(dev_of[:, k, 0:n], moments_of[:, k, 0:n, 1], ACT.Sqrt,
                                         bias=eps_sb[:, 0:1]).then_inc(dev_ready, 1)
                elif at == TURN_ROWS and e != 4:
                    act.wait_ge(rowsT[e], b + 2)
                    act.wait_ge(projected[e], b + 1)
                    nc.scalar.activation(xT[k], bank[3][:, 0:n * P], ACT.Copy).then_inc(rowsT_kept[e], 1)
                    if e == 1:
                        act.wait_ge(normed[1], b + 1)
                        apart(act)
                        nc.scalar.activation(xcur[:, bass.ds(b * BLK, n), :], xn[k].rearrange("p (c f) -> p c f", c=n),
                                             ACT.Copy).then_inc(kept[1], 1)
                elif at == PROJECT and e == 1:
                    act.wait_ge(selfed, b + 1)
                    apart(act)
                    to_acc(b, k, bank[6], ACT.Identity, bias=bs_sb[:, 0:1]).then_inc(acc_set[1], 1)
                elif at == LOOPS and e in (2, 3):
                    act.wait_ge(loop_turned[e], b + 2)
                    apart(act)
                    to_acc(b, k, bank[6], ACT.Copy).then_inc(acc_set[e], 1)

            def stage1(b, k, at):
                in_loop = not isinstance(b, int)
                if at == LAST_PIECE and in_loop:
                    zero_piece(b + 1, 1)
                stage_step(1, b, k, at)
                if at == STEPS - 1 and in_loop:
                    zero_piece(b + 2, 0)
            zero_piece(0, 0)
            zero_piece(0, 1)
            zero_piece(1, 0)
            in_steps(act, stage1)
            zero_piece(NBLK - 1, 1)
            in_steps(act, lambda b, k, at: stage_step(2, b, k, at))
            in_steps(act, lambda b, k, at: stage_step(3, b, k, at))
            in_steps(act, lambda b, k, at: stage_step(4, b, k, at))

        @block.tensor
        def _(pe):
            for p in range(1, PASSES):
                pe.sem_inc(products[p], PRODUCTS_AHEAD)
            pe.sem_inc(alpha_summed, 1)
            pe.sem_inc(c_summed, 2)
            pe.sem_inc(messages, FSTEPS)
            for e in LAYERS[1:]:
                pe.sem_inc(turned[e], 1)
            for e in (1, 2, 3):
                pe.sem_inc(projected[e], 1)
                pe.sem_inc(rowsT[e], 1)
            for e in (2, 3):
                pe.sem_inc(loop_turned[e], 1)

            def turn(to, rows_in, rhs=None, n=BLK):
                for c in range(n):
                    at = slice(c * P, (c + 1) * P)
                    if rhs is None:
                        last = nc.tensor.transpose(to[:, at], rows_in[:, at], ident[:, :])
                    else:
                        last = nc.tensor.matmul(to[:, at], rows_in[:, at], rhs, start=True, stop=True)
                return last

            pe.wait_ge(consts_set, 8)
            pe.wait_ge(dst_ready, 1)
            nc.tensor.matmul(bank[0][:, 0:NG], first_row[:, :], dst_f[:, 0:T:GT], start=True,
                             stop=True).then_inc(base_summed, 1)
            pe.wait_ge(k0_in, 16 * 2)

            for n, (a, b) in enumerate(zip(HXB, HXB[1:])):
                pe.wait_ge(xT_in[n], 16)
                for blk in range(a, b):
                    pe.wait_ge(support_kept, blk + 1)
                    turn(bank[2 + blk % 2], xT_sb[:, blk * BC:(blk + 1) * BC], k0_sb[:, :]).then_inc(supported, 1)
            pe.wait_ge(missed_ready, 1)
            nc.tensor.matmul(bank[0][0:1, 0:1], missed_any[:, 0:1], ones[:, 0:1], start=True,
                             stop=True).then_inc(missed_summed, 1)
            pe.wait_ge(weights_in, 16 * 10)

            def group_products(p, i, k):
                g = i * RING + k
                width = NB * W if p == 1 else W
                pe.wait_ge(gathered[k], i * (16 * GT) + ((p - 1) * NBODY + 1) * 16 * GT)
                if k % PAIR == 0:
                    pe.wait_ge(s_ready[p], i * PAIRS + (k // PAIR + 1))
                of_group = S[:, k // PAIR % 2, k % PAIR * GT:(k % PAIR + 1) * GT, :]
                pe.wait_ge(added[p], g + 1)
                if p == 2:
                    for t in range(GT):
                        nc.tensor.matmul(count_at(k), ones[:, 0:1], of_group[:, t, 0:W],
                                         start=t == 0, stop=t == GT - 1)
                for t in range(GT):
                    last = nc.tensor.matmul(bank[k % 2][:, 0:width], rows[:, k, t, :], of_group[:, t, 0:width],
                                            start=t == 0, stop=t == GT - 1)
                last.then_inc(products[p], 1)

            def general_products(p, flag):
                width = NB * W if p == 1 else W
                with pe.If(flag != 0):
                    with pe.Fori(0, T) as t:
                        pe.wait_ge(slow_gathered, t * 16 + ((p - 1) * T + 1) * 16)
                        apart(pe)
                        with pe.Fori(0, NWIN) as c:
                            n = t * NWIN + c + (p - 1) * T * NWIN
                            pe.wait_ge(slow_s, n + 1)
                            if p == 2:
                                nc.tensor.matmul(count_at(0), ones[:, 0:1], S[:, 0, 0, 0:W], start=True, stop=True)
                            nc.tensor.matmul(bank[0][:, 0:width], rows[:, 0, 0, :], S[:, 0, 0, 0:width], start=True,
                                             stop=True).then_inc(slow_products, 1)
                            if p == 1:
                                pe.wait_ge(slow_moved, n + 1)
                                for b in range(NB):
                                    last = nc.tensor.matmul(bank[1][:, 0:W], bases_sb[:, b, :],
                                                            slow_G[:, b * W:(b + 1) * W], start=b == 0, stop=b == NB - 1)
                                last.then_inc(slow_based, 1)

            def stage_step(e, b, k, at):
                n = CHUNKS[k]
                if at == TURN:
                    pe.wait_ge(staged[e], b + 1)
                    pe.wait_ge(scaled if e == 3 else summed[e], b + 1)
                    turn(bank[2], stage, n=n).then_inc(turned[e], 1)
                    if e == 2:
                        pe.wait_ge(cnt_staged, b + 1)
                        pe.wait_ge(sqrt_ready, b + 1)
                        for c in range(n):
                            last = nc.tensor.matmul(bank[5][:, c:c + 1], cnt_blk[k][:, c * P:(c + 1) * P], ones[0:1, 0:1],
                                                    start=True, stop=True)
                        last.then_inc(deg_turned, 1)
                elif at == TURN_ROWS and e != 4:
                    pe.wait_ge(normed[e], b + 1)
                    pe.wait_ge(rowsT_kept[e], b + 1)
                    turn(bank[3], xn[k], n=n).then_inc(rowsT[e], 1)
                elif at == PROJECT and e != 4:
                    pe.wait_ge(rowsT_kept[e], b + 2)
                    pe.wait_ge(rows_ready[e], b + 1)
                    if e == 1:
                        for c in range(n):
                            last = nc.tensor.matmul(bank[4 + c // 2][:, (c % 2) * 2 * P:(c % 2 + 1) * 2 * P],
                                                    xT[k][:, c * P:(c + 1) * P], wdc_sb[:, :], start=True, stop=True)
                        last.then_inc(projected[1], 1)
                        pe.wait_ge(acc_set[1], b + 1)
                        nc.tensor.matmul(bank[6][:, 0:n * P], ws_sb[:, :], xT[k], start=True, stop=True).then_inc(selfed, 1)
                    else:
                        turn(bank[4], xT[k], (w1_sb if e == 2 else w2_sb)[:, :], n=n).then_inc(projected[e], 1)
                elif at == LOOPS and e in (2, 3):
                    pe.wait_ge(rows_ready[e], b + 2)
                    pe.wait_ge(acc_set[e], b + 1)
                    turn(bank[6], hst[k], n=n).then_inc(loop_turned[e], 1)

            def base_piece(q, j):
                at = pe.value_load(part_i[0:1, bass.ds(q, 1)], min_val=0, max_val=CAP)
                pe.wait_ge(added[1], q * GPP + ((GPP if j else PAST) + ADDED_AHEAD))
                pe.wait_ge(based_added, q * NPIECE + (j + 1))
                for b in range(NB):
                    last = nc.tensor.matmul(bank[7][:, 0:PIECE], bases_sb[:, b, :], G[:, b, bass.ds(at + j * PIECE, PIECE)],
                                            start=b == 0, stop=b == NB - 1)
                last.then_inc(based, 1)

            def part_products(p, m, whole, first=False):
                for j in range(BPP):
                    for k in range(RING):
                        group_products(p, m * BPP + j, k)
                        at = (j * RING + k) // 2
                        if k % 2 == 1:
                            if p == 1 and at == LAST_PIECE and not first:
                                base_piece(m - 1, 1)
                            if p == 1 and at == FIRST_PIECE:
                                base_piece(m, 0)
                            if whole:
                                stage_step(p, m - 2, 0, at)

            def pass_products(p):
                if p == 1:
                    part_products(1, 0, False, True)
                    part_products(1, 1, False)
                else:
                    with pe.Fori(0, 2 * BPP) as i:
                        for k in range(RING):
                            group_products(p, i, k)
                with pe.Fori(2, NBLK) as m:
                    part_products(p, m, True)
                if p == 1:
                    base_piece(NBLK - 1, 1)
                for at in range(STEPS):
                    stage_step(p, NBLK - 2, 0, at)
                    stage_step(p, NBLK - 1, 1, at)

            def window_by_edge(i, k):
                g = i * FSTEPS + k
                pe.wait_ge(sel_ready, g + (FSTEPS + 1))
                pe.wait_ge(c_kept, g + 1)
                for t in range(FT):
                    last = nc.tensor.matmul(bank[k % 2][0:W, t * P:(t + 1) * P], wS[:, k % 2, t, :], sel[k % 2][:, t, :],
                                            start=True, stop=True)
                last.then_inc(c_summed, 1)

            def rows_to_add(i, k):
                g = i * FSTEPS + k
                pe.wait_ge(c_kept, g + 3)
                pe.wait_ge(xwin_in[k], i * (16 * FHALF) + 16 * FHALF)
                pe.wait_ge(msg_kept, g + 1)
                for t in range(FT):
                    last = nc.tensor.matmul(bank[4 + k % 2][:, t * P:(t + 1) * P], C[k % 2][:, t * P:(t + 1) * P],
                                            xwin[k][t // GT], start=True, stop=True)
                last.then_inc(messages, 1)

            def body_weights(i):
                pe.wait_ge(hot_ready, i + 2)
                pe.wait_ge(alpha_ready, i + 1)
                for t in range(BODY):
                    last = nc.tensor.matmul(bank[2][:, t * NB * NPART:(t + 1) * NB * NPART], type_hot[:, t * P:(t + 1) * P],
                                            relw_parts[:, :, :].rearrange("r b n -> r (b n)"), start=True, stop=True)
                last.then_inc(alpha_summed, 1)

            pe.wait_ge(relw_ready, 1)
            with pe.Fori(0, NBODY) as i:
                window_by_edge(i, 0)
                for k in range(FSTEPS - 1):
                    window_by_edge(i, k + 1)
                    if k == 1:
                        body_weights(i)
                    rows_to_add(i, k)
                rows_to_add(i, FSTEPS - 1)
            flag = pe.value_load(flag_i[0:1, 0:1], min_val=0, max_val=1)
            with pe.If(flag != 0):
                with pe.Fori(0, T) as t:
                    pe.wait_ge(slow0_ready, t * 2 + 1)
                    nc.tensor.matmul(bank[0][:, 0:P], ones[:, :], masked[0][:, 0, :], start=True, stop=True).then_inc(slow0_summed, 1)
                    pe.wait_ge(slow0_ready, t * 2 + 2)
                    nc.tensor.matmul(bank[1][:, 0:P], sel[0][:, 0, :], rows4[:, 0, 1, :], start=True, stop=True).then_inc(slow0_summed, 1)

            for p in range(1, PASSES):
                general_products(p, flag)
                pass_products(p)

        @block.vector
        def _(dve):
            nprep = [0]

            def after(ins):
                nprep[0] += 1
                ins.then_inc(prep, 1)
                dve.wait_ge(prep, nprep[0])

            for p in range(1, PASSES):
                dve.sem_inc(added[p], ADDED_AHEAD)
            dve.sem_inc(based_added, 1)
            dve.sem_inc(alpha_ready, 1)
            dve.sem_inc(sel_ready, FSTEPS)
            dve.sem_inc(hot_ready, 1)
            dve.sem_inc(scaled, 1)
            for e in NORMED:
                dve.sem_inc(summed[e], 1 if e else SLOTS0)
            for e in (1, 2, 3):
                dve.sem_inc(rows_ready[e], 1)

            def copy_idx(p, i, h):
                source = src2_i if p == 2 else src_i
                nc.vector.tensor_copy(idx_ring[:, h * PAIR:(h + 1) * PAIR, :].rearrange("p k t -> p (k t)"),
                                      source[:, bass.ds(i * BODY + h * PT, PT)]).then_inc(idx_ready[p], 1)

            dve.wait_ge(src_in, 16)
            nc.vector.memset(acc[:, :], 0.0).then_inc(acc_zeroed, 1)

            dve.wait_ge(edges_in, 16 * 3)
            nc.vector.tensor_copy(dst_f[:, :], dst_i).then_inc(dst_ready, 1)
            after(nc.vector.tensor_copy(src_f, src_i[:, 0:T]))
            dve.wait_ge(consts_set, 8)
            after(nc.vector.tensor_scalar(to_spare, src_f, -1.0, spare_row[:, 0:1], ALU.mult, ALU.add))
            after(nc.vector.tensor_scalar(src2_i[:, :], type2_i, 0, None, ALU.not_equal))
            after(nc.vector.scalar_tensor_tensor(src2_i[:, :], src_i[:, :], 2, src2_i[:, :], ALU.mult, ALU.add))
            dve.wait_ge(base_summed, 1)
            after(nc.vector.tensor_copy(base_bc[:, :], bank[0][:, 0:NG]))
            for m in range(2, NBLK):
                part = base_bc[:, m * GPP:(m + 1) * GPP]
                after(nc.vector.tensor_scalar(part, part, float((m - 1) * BC), None, ALU.max))
            parts = base_bc[:, :].rearrange("p (q g) -> p q g", q=NBLK)
            after(nc.vector.tensor_scalar(piece_floor[:, :], parts[:, :, 0], float(PIECE), None, ALU.add))
            after(nc.vector.tensor_tensor(parts[:, :, PAST:], parts[:, :, PAST:],
                                          piece_floor[:, :].unsqueeze(2).to_broadcast([P, NBLK, GPP - PAST]), ALU.max))
            after(nc.vector.tensor_copy(base_i[:, :], base_bc[0:1, :]))
            after(nc.vector.tensor_tensor(off_bc[:, :].rearrange("p (q g) -> p q g", q=NBLK), parts,
                                          parts[:, :, 0:1].to_broadcast([P, NBLK, GPP]), ALU.subtract))
            after(nc.vector.tensor_scalar(off_ok, off_bc[:, :], 0.0, None, ALU.is_ge))
            after(nc.vector.scalar_tensor_tensor(off_ok2, off_bc[:, :], float(CAP - W), off_ok, ALU.is_le, ALU.mult))
            after(nc.vector.tensor_scalar(off_bc[:, :], off_bc[:, :], 0.0, float(CAP - W), ALU.max, ALU.min))
            after(nc.vector.memset(part_at[:, :], 0.0))
            for m in range(1, NBLK, 2):
                part = off_bc[:, m * GPP:(m + 1) * GPP]
                after(nc.vector.tensor_scalar(part, part, float(CAP), None, ALU.add))
                after(nc.vector.memset(part_at[:, m:m + 1], float(CAP)))
            after(nc.vector.tensor_copy(part_i[:, :], part_at[:, :]))
            after(nc.vector.tensor_copy(off_i[:, :], off_bc[0:1, :]))

            def by_group(a):
                return a.rearrange("p (g t) -> p g t", t=GT)

            def to_tiles(a):
                return a.unsqueeze(2).to_broadcast([P, NG, GT])

            after(nc.vector.memset(rel[:, T:TX], -1.0))
            after(nc.vector.memset(alpha[:, T * NB:TX * NB], 0.0))
            after(nc.vector.tensor_tensor(by_group(rel[:, 0:T]), by_group(dst_f[:, :]), to_tiles(base_bc[:, :]), ALU.subtract))
            after(nc.vector.scalar_tensor_tensor(by_group(ok), by_group(rel[:, 0:T]), 0.0, to_tiles(off_ok2), ALU.is_ge, ALU.mult))
            after(nc.vector.scalar_tensor_tensor(ok2, rel[:, 0:T], float(W), ok, ALU.is_lt, ALU.mult))
            after(nc.vector.scalar_tensor_tensor(rel[:, 0:T], rel[:, 0:T], 1.0, ok2, ALU.add, ALU.mult))
            after(nc.vector.tensor_scalar(rel[:, 0:T], rel[:, 0:T], -1.0, None, ALU.add))
            after(nc.vector.tensor_scalar(ok, ok2, -1.0, 1.0, ALU.mult, ALU.add))
            nc.vector.reduce_max(missed_any[:, 0:1], ok, AX_X).then_inc(missed_ready, 1)
            after(nc.vector.scalar_tensor_tensor(missed_dst[:, :], dst_f[:, :], 1.0, ok, ALU.add, ALU.mult))
            after(nc.vector.tensor_scalar(missed_dst[:, :], missed_dst[:, :], -1.0, None, ALU.add))
            dve.wait_ge(missed_summed, 1)
            nc.vector.tensor_scalar(flag_i[0:1, 0:1], bank[0][0:1, 0:1], 0.0, None, ALU.is_gt).then_inc(flag_ready, 1)
            dve.wait_ge(flag_ready, 1)
            flag = dve.value_load(flag_i[0:1, 0:1], min_val=0, max_val=1)
            dve.wait_ge(acc_zeroed, 1)

            dve.wait_ge(weights_in, 16 * 10)
            after(nc.vector.tensor_copy(relw_rest[:, :], relw_sb[:, :]))
            for n in range(NPART):
                after(nc.vector.tensor_copy(relw_parts[:, :, n], relw_rest[:, :]))
                if n < NPART - 1:
                    after(nc.vector.tensor_tensor(relw_rest[:, :], relw_rest[:, :], relw_parts[:, :, n], ALU.subtract))
            dve.sem_inc(relw_ready, 1)

            def make_S(p, n, k):
                dve.wait_ge(products[p], n * PAIR + (PRODUCTS_AHEAD - PAIR))
                S01_of = S01[:, k, :, :] if p == 1 else S[:, k, :, 0:W]
                nc.vector.tensor_tensor(S01_of, iota_w[:, :].unsqueeze(1).to_broadcast([P, PT, W]),
                                        rel[:, bass.ds(n * PT, PT)].unsqueeze(2).to_broadcast([P, PT, W]),
                                        ALU.is_equal).then_inc(s01_ready if p == 1 else s_ready[p], 1)
                if p == 1:
                    dve.wait_ge(s01_ready, n + 1)
                    nc.vector.tensor_tensor(
                        S[:, k, :, :].rearrange("p t (b w) -> p t b w", w=W),
                        S01[:, k, :, :].unsqueeze(2).to_broadcast([P, PT, NB, W]),
                        alpha[:, bass.ds(n * (PT * NB), PT * NB)].rearrange("p (t b) -> p t b", b=NB)
                        .unsqueeze(3).to_broadcast([P, PT, NB, W]), ALU.mult).then_inc(s_ready[p], 1)

            def add_sums(p, g, k, at):
                dve.wait_ge(products[p], g + (PRODUCTS_AHEAD + 1))
                dve.wait_ge(added[p], g + ADDED_AHEAD)
                if p == 1:
                    to = G[:, :, bass.ds(at, W)]
                    sums = bank[k % 2][:, 0:NB * W].rearrange("p (b w) -> p b w", w=W)
                else:
                    to, sums = acc[:, bass.ds(at, W)], bank[k % 2][:, 0:W]
                if p == 2:
                    counts = cnt[:, bass.ds(at, W)]
                    nc.vector.tensor_tensor(counts, counts, count_at(k), ALU.add).then_inc(counted, 1)
                    dve.wait_ge(counted, g + 1)
                nc.vector.tensor_tensor(to, to, sums, ALU.add).then_inc(added[p], 1)

            def body_sums(p, i, between=None):
                places = off_i if p == 1 else base_i
                for h in range(PAIRS):
                    make_S(p, i * PAIRS + (h + 1), (h + 1) % 2)
                    ats = [dve.value_load(places[0:1, bass.ds(i * RING + h * PAIR + n, 1)], min_val=0,
                                          max_val=2 * CAP - W if p == 1 else N + PIECE) for n in range(PAIR)]
                    for n in range(PAIR):
                        add_sums(p, i * RING + (h * PAIR + n), n, ats[n])
                    copy_idx(p, i + 1, h)
                    if between:
                        between(h)

            def start_pass(p):
                for h in range(PAIRS):
                    copy_idx(p, 0, h)
                make_S(p, 0, 0)

            def general_sums(p):
                source = src2_i if p == 2 else src_i
                with dve.If(flag != 0):
                    with dve.Fori(0, T) as t:
                        nc.vector.tensor_copy(slow_idx[:, 0:1], source[:, bass.ds(t, 1)]).then_inc(slow_idx_ready, 1)
                        nc.vector.tensor_copy(slow_rel[:, 0:1], missed_dst[:, bass.ds(t, 1)]).then_inc(slow_step, 1)
                        with dve.Fori(0, NWIN) as c:
                            n = t * NWIN + c
                            steps = n * 2 + t + (p - 1) * (2 * NWIN + 1) * T
                            past = (p - 1) * T * NWIN
                            dve.wait_ge(slow_step, steps + 1)
                            if p == 1:
                                nc.vector.tensor_scalar(S01[:, 0, 0, :], iota_w[:, :], slow_rel[:, 0:1], None,
                                                        ALU.is_equal).then_inc(slow_s01, 1)
                                dve.wait_ge(slow_s01, n + 1)
                                nc.vector.tensor_tensor(
                                    S[:, 0, 0, :].rearrange("p (b w) -> p b w", w=W),
                                    S01[:, 0, 0, :].unsqueeze(1).to_broadcast([P, NB, W]),
                                    alpha[:, bass.ds(t * NB, NB)].unsqueeze(2).to_broadcast([P, NB, W]),
                                    ALU.mult).then_inc(slow_s, 1)
                            else:
                                nc.vector.tensor_scalar(S[:, 0, 0, 0:W], iota_w[:, :], slow_rel[:, 0:1], None,
                                                        ALU.is_equal).then_inc(slow_s, 1)
                            dve.wait_ge(slow_s, n + (past + 1))
                            nc.vector.tensor_scalar(slow_rel[:, 0:1], slow_rel[:, 0:1], float(-W), None,
                                                    ALU.add).then_inc(slow_step, 1)
                            dve.wait_ge(slow_products, n + (past + 1))
                            to = acc[:, bass.ds(c * W, W)]
                            sums = bank[0][:, 0:W]
                            if p == 1:
                                nc.vector.tensor_copy(slow_G[:, :], bank[0][:, 0:NB * W]).then_inc(slow_moved, 1)
                                dve.wait_ge(slow_based, n + 1)
                                sums = bank[1][:, 0:W]
                            if p == 2:
                                counts = cnt[:, bass.ds(c * W, W)]
                                nc.vector.tensor_tensor(counts, counts, count_at(0), ALU.add).then_inc(slow_counted, 1)
                                dve.wait_ge(slow_counted, n + 1)
                            nc.vector.tensor_tensor(to, to, sums, ALU.add).then_inc(slow_step, 1)
                            dve.wait_ge(slow_step, steps + 3)

            def blk(b, n=BLK):
                return bass.ds(b * BLK, n)

            def as_chunks(a, n=BLK):
                return a.rearrange("p (c f) -> p c f", c=n)

            def to_rows(v, n=BLK):
                return v.unsqueeze(2).to_broadcast([P, n, P])

            def to_chunks(v, n=BLK):
                return v.unsqueeze(1).to_broadcast([P, n, P])

            def chunk(b, c):
                return xcur[:, bass.ds(b * BLK + c, 1), :].rearrange("p c f -> p (c f)")

            def residual0(b, k):
                dve.wait_ge(tab_paired, b + 1)
                dve.wait_ge(normed[0], b + 1)
                nc.vector.tensor_tensor(xcur[:, blk(b), :], as_chunks(tab_rows[k][:, 0, :]), as_chunks(tab_rows[k][:, 1, :]),
                                        ALU.add).then_inc(summed[0], 1)
                dve.wait_ge(summed[0], b + (SLOTS0 + 1))
                apart(dve)
                for c in range(BLK):
                    last = nc.vector.bn_stats(bst[:, c, :], chunk(b, c))
                last.then_inc(stats, 1)
                dve.wait_ge(stats, b * 2 + 1)
                apart(dve)
                for c in range(BLK):
                    last = nc.vector.bn_aggr(moments_of[:, k, c, :], bst[:, c, :])
                last.then_inc(stats, 1)

            def scales0(b, k, j, more):
                if more:
                    residual0(b + 1, (k + 1) % SLOTS0)
                dve.wait_ge(dev0_ready, b + 1)
                apart(dve)
                nc.vector.reciprocal(inv_of[:, k, :], dev_of[:, k, :]).then_inc(inv0_ready, 1)
                dve.wait_ge(inv0_ready, b + 1)
                nc.vector.scalar_tensor_tensor(shift_of[:, k, :], moments_of[:, k, :, 0], -1.0, inv_of[:, k, :],
                                               ALU.mult, ALU.mult).then_inc(shift0_ready, 1)

            def residual(e, b, k):
                n = CHUNKS[k]
                seen = 2 * moment_steps(e)
                dve.wait_ge(turned[e], b + 2)
                if e != 1:
                    dve.wait_ge(kept[e // 2], NBLK)
                to = xcur[:, blk(b, n), :]
                new = as_chunks(bank[2][:, 0:n * P], n)
                if e == 4:
                    nc.vector.tensor_tensor(as_chunks(xn[k], n), new, to_rows(dis[:, blk(b, n)], n),
                                            ALU.mult).then_inc(summed_scale, 1)
                    dve.wait_ge(summed_scale, b + 1)
                    new = as_chunks(xn[k], n)
                nc.vector.tensor_tensor(to, new, to, ALU.add).then_inc(summed[e], 1)
                dve.wait_ge(summed[e], b + 2)
                apart(dve)
                for c in range(n):
                    last = nc.vector.bn_stats(bst[:, c, :], chunk(b, c))
                last.then_inc(moments, 1)
                dve.wait_ge(moments, b * 2 + (seen + 1))
                apart(dve)
                for c in range(n):
                    last = nc.vector.bn_aggr(moments_of[:, k, c, :], bst[:, c, :])
                last.then_inc(moments, 1)
                if e == 2:
                    dve.wait_ge(sqrt_ready, b + 2)
                    nc.vector.reciprocal(dis[:, blk(b, n)], deg_dev[:, k, 0:n]).then_inc(deg_ready, 1)

            def norm(e, b, k):
                n = CHUNKS[k]
                dve.wait_ge(dev_ready, b + (moment_steps(e) + 1))
                nc.vector.reciprocal(inv_of[:, k, 0:n], dev_of[:, k, 0:n]).then_inc(inv_ready, 1)
                dve.wait_ge(inv_ready, b + (moment_steps(e) + 1))
                if e != 4:
                    dve.wait_ge(rowsT[e], b + 1)
                for c in range(n):
                    to = chunk(b, c) if e == 4 else xn[k][:, c * P:(c + 1) * P]
                    last = nc.vector.tensor_scalar(to, chunk(b, c), moments_of[:, k, c, 0:1], inv_of[:, k, c:c + 1],
                                                   ALU.subtract, ALU.mult)
                last.then_inc(normed[e], 1)

            def scale_and_bias(b, k):
                n = CHUNKS[k]
                dve.wait_ge(turned[3], b + 2)
                dve.wait_ge(rowsT[3], b + 1)
                nc.vector.tensor_tensor(as_chunks(xn[k], n), as_chunks(bank[2][:, 0:n * P], n), to_rows(dis[:, blk(b, n)], n),
                                        ALU.mult).then_inc(scaled, 1)
                dve.wait_ge(scaled, b + 2)
                nc.vector.tensor_tensor(as_chunks(xn[k], n), as_chunks(xn[k], n), to_chunks(b1_bc[:, :], n),
                                        ALU.add).then_inc(biased, 1)

            def table_rows(e, b, k):
                n = CHUNKS[k]
                dve.wait_ge(projected[e], b + 2)
                if k == 0:
                    dve.wait_ge(stored[e], b * 16 + 16)
                if e == 1:
                    for h in range(-(-n // 2)):
                        c = min(n, 2)
                        last = nc.vector.tensor_tensor(
                            hst[k][:, h * BC:h * BC + c * 2 * P].rearrange("p (c f) -> p c f", c=c),
                            bank[4 + h][:, 0:c * 2 * P].rearrange("p (c f) -> p c f", c=c),
                            bdc_bc[:, :].unsqueeze(1).to_broadcast([P, c, 2 * P]), ALU.add)
                    last.then_inc(rows_ready[1], 1)
                    return
                dve.wait_ge(loop_turned[e], b + 1)
                if e == 2:
                    dve.wait_ge(deg_ready, b + 1)
                nc.vector.tensor_tensor(as_chunks(hst[k][:, 0:n * P], n), as_chunks(bank[4][:, 0:n * P], n),
                                        to_rows(dis[:, blk(b, n)], n), ALU.mult).then_inc(rows_ready[e], 1)
                if e == 2:
                    dve.wait_ge(normed[2], b + 1)
                    nc.vector.tensor_tensor(xcur[:, blk(b, n), :], as_chunks(xn[k], n), to_chunks(b2_bc[:, :], n),
                                            ALU.add).then_inc(kept[2], 1)

            def stage_step(e, b, k, at):
                if at == RESIDUAL:
                    if e == 3:
                        scale_and_bias(b, k)
                    else:
                        residual(e, b, k)
                elif at == NORM and e != 3:
                    norm(e, b, k)
                elif at == TABLE and e != 4:
                    table_rows(e, b, k)

            def add_piece(q, j):
                start = dve.value_load(base_i[0:1, bass.ds(q * GPP, 1)], min_val=0, max_val=N)
                dve.wait_ge(based, q * NPIECE + (j + 1))
                dve.wait_ge(based_added, q * NPIECE + (j + 1))
                to = acc[:, bass.ds(start + j * PIECE, PIECE)]
                nc.vector.tensor_tensor(to, to, bank[7][:, 0:PIECE], ALU.add).then_inc(based_added, 1)

            def part_sums(p, m, whole, first=False):
                if p == 1 and whole:
                    dve.wait_ge(G_zeroed, m * NPIECE - (NPIECE - 1))
                for j in range(BPP):
                    def between(half):
                        at = j * (RING // 2) + half
                        if p == 1 and at == LAST_PIECE + PIECE_STEPS and not first:
                            add_piece(m - 1, 1)
                        if p == 1 and at == FIRST_PIECE + PIECE_STEPS:
                            add_piece(m, 0)
                        if whole:
                            stage_step(p, m - 2, 0, at)
                    body_sums(p, m * BPP + j, between)

            def pass_sums(p):
                start_pass(p)
                if p == 1:
                    part_sums(1, 0, False, True)
                    part_sums(1, 1, False)
                else:
                    with dve.Fori(0, 2 * BPP) as i:
                        body_sums(p, i)
                with dve.Fori(2, NBLK) as m:
                    part_sums(p, m, True)
                if p == 1:
                    add_piece(NBLK - 1, 1)
                for at in range(STEPS):
                    stage_step(p, NBLK - 2, 0, at)
                    stage_step(p, NBLK - 1, 1, at)

            with dve.Fori(0, NBODY) as i:
                for k in range(FSTEPS):
                    g = i * FSTEPS + k
                    dve.wait_ge(c_summed, g + 1)
                    if k % 2 == 0:
                        dve.wait_ge(src_rows_in[k // 2], i * 16 + 16)
                    nc.vector.tensor_tensor(hits[:, k % 2, :, :], iota_w[:, :].unsqueeze(1).to_broadcast([P, FT, W]),
                                            rel[:, bass.ds(g * FT, FT)].unsqueeze(2).to_broadcast([P, FT, W]),
                                            ALU.is_equal).then_inc(hits_ready, 1)
                    at = k % 2 * (FT * P)
                    nc.vector.tensor_tensor(sel[k % 2], src_rows[k // 2][:, at:at + FT * P].rearrange("p (t f) -> p t f", t=FT),
                                            src_f[:, bass.ds(g * FT, FT)].unsqueeze(2).to_broadcast([P, FT, P]),
                                            ALU.is_equal)
                    dve.wait_ge(hits_ready, g + 1)
                    nc.vector.tensor_tensor(wS[:, k % 2, :, :], hits[:, k % 2, :, :],
                                            wgt[:, bass.ds(g * FT, FT)].unsqueeze(2).to_broadcast([P, FT, W]),
                                            ALU.mult).then_inc(sel_ready, 1)
                    dve.wait_ge(sel_ready, g + (FSTEPS + 1))
                    for t in range(FT):
                        last = nc.vector.tensor_tensor_reduce(
                            out=masked[k % 2][:, t, :], in0=sel[k % 2][:, t, :], in1=earlier[:, :], scale=1.0, scalar=0.0,
                            op0=ALU.mult, op1=ALU.add, accum_out=dup[:, k % 2, t:t + 1])
                    last.then_inc(dup_step, 1)
                    dve.wait_ge(dup_step, g * 3 + 1)
                    nc.vector.scalar_tensor_tensor(dup[:, k % 2, :], dup[:, k % 2, :], 1.0, to_spare[:, bass.ds(g * FT, FT)],
                                                   ALU.min, ALU.mult).then_inc(dup_step, 1)
                    dve.wait_ge(dup_step, g * 3 + 2)
                    dve.wait_ge(scatter_through, g + 1)
                    nc.vector.tensor_tensor(idx4[:, k, :], dup[:, k % 2, :], src_f[:, bass.ds(g * FT, FT)],
                                            ALU.add).then_inc(idx_ready[0], 1)
                    dve.sem_inc(dup_step, 1)
                    if k == 0:
                        dve.wait_ge(types_in, i * 16 + 16)
                        dve.wait_ge(alpha_summed, i + 1)
                        nc.vector.tensor_scalar(type_hot, type_rows, iota_p[0:R, 0:1], None,
                                                ALU.is_equal).then_inc(hot_ready, 1)
                dve.wait_ge(alpha_summed, i + 2)
                apart(dve)
                nc.vector.reduce_sum(alpha[:, bass.ds(i * (BODY * NB), BODY * NB)],
                                     bank[2][:, 0:BODY * NB * NPART].rearrange("p (e n) -> p e n", n=NPART),
                                     AX_X).then_inc(alpha_ready, 1)
            with dve.If(flag != 0):
                for k in range(NTAB):
                    dve.wait_ge(scattered[k], (T // FT + 1) * 16)
                with dve.Fori(0, T) as t:
                    nc.vector.tensor_copy(slow_idx[:, 0:1], dst_i[:, bass.ds(t, 1)]).then_inc(slow_idx_ready, 1)
                    source = src_f[:, bass.ds(t, 1)]
                    nc.vector.tensor_scalar(masked[0][:, 0, :], ident[:, :], source, None, ALU.mult).then_inc(slow0_ready, 1)
                    nc.vector.tensor_scalar(slow_w[:, 0:1], missed_dst[:, bass.ds(t, 1)], 0.0, wgt[:, bass.ds(t, 1)],
                                            ALU.is_ge, ALU.mult).then_inc(slow0_step, 1)
                    dve.wait_ge(slow0_summed, t * 2 + 1)
                    nc.vector.tensor_scalar(sel[0][:, 0, :], bank[0][:, 0:P], source, None, ALU.is_equal).then_inc(slow0_step, 1)
                    dve.wait_ge(slow0_step, t * 5 + 2)
                    nc.vector.tensor_tensor_reduce(
                        out=masked[0][:, 1, :], in0=sel[0][:, 0, :], in1=earlier[:, :], scale=1.0, scalar=0.0,
                        op0=ALU.mult, op1=ALU.add, accum_out=slow_dup[:, 0:1]).then_inc(slow0_step, 1)
                    dve.wait_ge(slow0_step, t * 5 + 3)
                    nc.vector.scalar_tensor_tensor(slow_dup[:, 0:1], slow_dup[:, 0:1], 1.0, to_spare[:, bass.ds(t, 1)],
                                                   ALU.min, ALU.mult).then_inc(slow0_step, 1)
                    dve.wait_ge(slow0_step, t * 5 + 4)
                    nc.vector.tensor_tensor(slow_out_idx[:, 0:1], slow_dup[:, 0:1], source, ALU.add).then_inc(slow0_step, 1)
                    dve.wait_ge(slow0_gathered, t * 16 + 16)
                    nc.vector.tensor_scalar(rows4[:, 0, 1, :], rows[:, 0, 0, :], slow_w[:, 0:1], None,
                                            ALU.mult).then_inc(slow0_ready, 1)
                    dve.wait_ge(slow0_summed, t * 2 + 2)
                    dve.wait_ge(slow0_step, t * 5 + 5)
                    nc.vector.tensor_copy(rows4[:, 0, 2, :], bank[1][:, 0:P]).then_inc(slow0_rows, 1)
                    dve.wait_ge(slow0_scattered, t * 16 + 16)
            residual0(0, 0)
            over_blocks(dve, scales0)

            dve.wait_ge(alpha_ready, NBODY + 1)
            dve.wait_ge(G_zeroed, 1)
            for p in range(1, PASSES):
                if p == 2:
                    dve.wait_ge(G_zeroed, NBLK * NPIECE + 1)
                if p > 1:
                    dve.wait_ge(acc_set[p - 1], NBLK + 1)
                general_sums(p)
                pass_sums(p)


def kernel(x, src, dst, edge_type_2, edge_type_64, edge_weight, L0_gnn_kernel, L0_gnn_bias, L1_gnn_bases,
           L1_gnn_relation_base_weights, L2_gnn_W_data, L2_gnn_b_data, L2_gnn_W_control, L2_gnn_b_control,
           L2_gnn_W_self, L2_gnn_b_self, L3_gnn_W1, L3_gnn_b1, L3_gnn_W2, L3_gnn_b2):
    from concourse import bacc
    from concourse.bass_utils import run_bass_kernel_spmd

    def tiles(a, columns, pad):
        a = np.asarray(a)
        filled = np.concatenate([a, np.full(columns * P - E, pad, a.dtype)])
        return np.ascontiguousarray(filled.reshape(columns, P).T)

    def row(*parts):
        return np.ascontiguousarray(np.concatenate([np.asarray(a) for a in parts])[None, :])

    def turned(*parts):
        return np.ascontiguousarray(np.concatenate([np.asarray(a).T for a in parts], axis=1))

    rows = np.concatenate([np.asarray(x), np.zeros((TABR - N, P), np.asarray(x).dtype)])
    arrays = {
        "src": tiles(src, TX, 0),
        "src_row": row(src, np.zeros(T * P - E, np.asarray(src).dtype)),
        "dst": tiles(dst, T, N),
        "type2": tiles(edge_type_2, TX, 0),
        "type64": row(edge_type_64, np.zeros(T * P - E, np.asarray(edge_type_64).dtype)),
        "weight": tiles(edge_weight, TX, 0),
        "x": rows,
        "xT0": np.ascontiguousarray(rows.T),
        "k0": np.ascontiguousarray(L0_gnn_kernel),
        "bias0": row(L0_gnn_bias),
        "bases": np.ascontiguousarray(L1_gnn_bases),
        "rel_weights": np.ascontiguousarray(L1_gnn_relation_base_weights),
        "w_data_ctrl": turned(L2_gnn_W_data, L2_gnn_W_control),
        "b_data_ctrl": row(L2_gnn_b_data, L2_gnn_b_control),
        "w_self": turned(L2_gnn_W_self),
        "b_self": np.ascontiguousarray(np.asarray(L2_gnn_b_self)[:, None]),
        "w1": turned(L3_gnn_W1),
        "b1": row(L3_gnn_b1),
        "w2": turned(L3_gnn_W2),
        "b2": row(L3_gnn_b2),
    }
    nc = bacc.Bacc("TRN2", target_bir_lowering=False, num_devices=1)
    args = {n: nc.dram_tensor(n, a.shape, mybir.dt.from_np(a.dtype), kind="ExternalInput").ap() for n, a in arrays.items()}
    args["out"] = nc.dram_tensor("out", (N, P), FP, kind="ExternalOutput").ap()
    gnn_program(nc, **args)
    r = run_bass_kernel_spmd(nc, [arrays], core_ids=[0])
    return r.results[0]["out"]
```
